# Optimizing a Trainium2 kernel written in Bass

```python
import numpy as np
import jax
import jax.numpy as jnp

def _softmax(x, axis=-1):
    return jax.nn.softmax(x, axis=axis)

def _gelu(x):
    return jax.nn.gelu(x, approximate=True)

def _silu(x):
    return jax.nn.silu(x)

def _sigmoid(x):
    return jax.nn.sigmoid(x)

def _layernorm(x, axis=-1, eps=1e-05):
    m = jnp.mean(x, axis=axis, keepdims=True)
    v = jnp.var(x, axis=axis, keepdims=True)
    return (x - m) / jnp.sqrt(v + eps)

def _scatter_add(tgt, idx, src, axis=0):
    return tgt.at[idx].add(src)

def _segment_sum(src, seg, n):
    return jax.ops.segment_sum(src, seg, n)
kernel_name = 'mk_adj_preln_d4_adj_r2_6e7de7'

def setup_inputs(seed: int=0):
    np.random.seed(seed)
    _w = jnp.asarray

    def _rec_inputs():
        import jax
        import jax.numpy as jnp
        _gk = jax.random.key(seed)
        x = -8.776e-05 + 1 * jax.random.normal(jax.random.fold_in(_gk, 1), (1354, 256), jnp.float32)
        _a = jax.random.bernoulli(jax.random.fold_in(_gk, 2), 0.00295421, (1354, 1354))
        _a = jnp.logical_or(_a, jnp.eye(1354, dtype=bool))
        _af = _a.astype(jnp.float32)
        _af = _af * jax.random.uniform(jax.random.fold_in(_gk, 3), (1354, 1354), jnp.float32, 0.05, 1)
        adj = _af
        return (x, adj)
    x, adj = _rec_inputs()

    def _L0_gnn_setup():
        import jax, jax.numpy as jnp
        import numpy as np
        N = 5000
        IN_F = 256
        OUT_F = 256
        key = jax.random.key(seed)
        k1, k2, k3 = jax.random.split(key, 3)
        x = jax.random.normal(k1, (N, IN_F), dtype=jnp.float32)
        adj = jax.random.uniform(k2, (N, N), dtype=jnp.float32)
        stdv = 1.0 / np.sqrt(OUT_F)
        weight = jax.random.uniform(k3, (IN_F, OUT_F), dtype=jnp.float32, minval=-stdv, maxval=stdv)
        t = jnp.ones((1,), dtype=jnp.float32)
        return {'x': x, 'adj': adj, 't': t, 'weight': weight}
    _L0_gnn_all = _L0_gnn_setup()
    _L0_gnn_in = {k: v for k, v in _L0_gnn_all.items() if k in ('t', 'weight')}
    del _L0_gnn_all

    def _L1_gnn_setup():
        import jax, jax.numpy as jnp
        import numpy as np
        N, D_IN, D_ATTN, STEPS, P_NUC, TAU = (2048, 256, 64, 2, 0.9, 1.0)
        LN_EPS = 1e-05

        def _xavier(key, shape):
            fan_in, fan_out = (shape[-2], shape[-1])
            lim = np.sqrt(6.0 / (fan_in + fan_out))
            return jax.random.uniform(key, shape, jnp.float32, -lim, lim)

        def _adj_from_feats(Xa, W1, W2, W3):
            Q = Xa @ W1
            K = Xa @ W3
            logits = Q @ W2 @ K.T / TAU
            idx = jnp.argsort(-logits, axis=1)
            vals = jnp.take_along_axis(logits, idx, axis=1)
            csum = jnp.cumsum(jax.nn.softmax(vals, axis=1), axis=1)
            k_i = jnp.sum(csum < P_NUC, axis=1) + 1
            ranks = jnp.arange(logits.shape[1])[None, :]
            keep_sorted = ranks < k_i[:, None]
            inv = jnp.argsort(idx, axis=1)
            keep = jnp.take_along_axis(keep_sorted, inv, axis=1)
            masked = jnp.where(keep, logits, -jnp.inf)
            return jax.nn.softmax(masked, axis=1)
        key = jax.random.key(seed)
        ks = jax.random.split(key, 9)
        return {'X': jax.random.normal(ks[0], (N, D_IN), jnp.float32), 'S': jax.random.uniform(ks[1], (N, N), jnp.float32), 'W1': _xavier(ks[2], (D_IN, D_ATTN)), 'W2': _xavier(ks[3], (D_ATTN, D_ATTN)), 'W3': _xavier(ks[4], (D_IN, D_ATTN)), 'U1': _xavier(ks[5], (STEPS, D_IN, D_IN)), 'U2': _xavier(ks[6], (STEPS, D_IN, D_IN)), 'U3': _xavier(ks[7], (STEPS, D_IN, D_IN)), 'gamma': jnp.ones((D_IN,), jnp.float32), 'beta': jnp.zeros((D_IN,), jnp.float32)}
    _L1_gnn_all = _L1_gnn_setup()
    _L1_gnn_in = {k: v for k, v in _L1_gnn_all.items() if k in ('W1', 'W2', 'W3', 'U1', 'U2', 'U3', 'gamma', 'beta')}
    del _L1_gnn_all

    def _L2_gnn_setup():
        import jax, jax.numpy as jnp
        import numpy as np
        N = 1024
        HID = 256
        H = 8
        key = jax.random.key(seed)
        ks = jax.random.split(key, 8)
        x = jax.random.normal(ks[0], (N, HID), dtype=jnp.float32)
        sp = jax.random.normal(ks[1], (N, N), dtype=jnp.float32)
        zero_mask = jax.random.uniform(ks[2], (N, N)) < 0.2
        spatial_encoding = jnp.where(zero_mask, 0.0, sp)
        edge_encoding = jax.random.normal(ks[3], (N, N), dtype=jnp.float32)
        s = 1.0 / np.sqrt(HID)
        Wq = jax.random.normal(ks[4], (HID, HID * H), dtype=jnp.float32) * s
        Wk = jax.random.normal(ks[5], (HID, HID * H), dtype=jnp.float32) * s
        Wv = jax.random.normal(ks[6], (HID, HID * H), dtype=jnp.float32) * s
        Wout = jax.random.normal(ks[7], (HID * H, HID), dtype=jnp.float32) * (1.0 / np.sqrt(HID * H))
        return {'x': x, 'spatial_encoding': spatial_encoding, 'edge_encoding': edge_encoding, 'Wq': Wq, 'Wk': Wk, 'Wv': Wv, 'Wout': Wout}
    _L2_gnn_all = _L2_gnn_setup()
    _L2_gnn_in = {k: v for k, v in _L2_gnn_all.items() if k in ('Wq', 'Wk', 'Wv', 'Wout')}
    del _L2_gnn_all

    def _L3_gnn_setup():
        import jax, jax.numpy as jnp
        import numpy as np
        N = 3072
        D_IN = 256
        D_OUT = 256
        DENSITY = 0.005
        key = jax.random.key(seed)
        ks = jax.random.split(key, 12)
        x = jax.random.normal(ks[0], (N, D_IN), dtype=jnp.float32)
        adj_a = (jax.random.uniform(ks[1], (N, N)) < DENSITY).astype(jnp.float32)
        adj_b = (jax.random.uniform(ks[2], (N, N)) < DENSITY).astype(jnp.float32)
        W_sa = jax.random.normal(ks[3], (D_IN, D_OUT), dtype=jnp.float32) * (1.414 / np.sqrt(D_IN + D_OUT))
        a_sa = jax.random.normal(ks[4], (1, 2 * D_OUT), dtype=jnp.float32) * (1.414 / np.sqrt(1 + 2 * D_OUT))
        stdv = 1.0 / np.sqrt(D_OUT)
        W_gcnb = jax.random.uniform(ks[5], (D_IN, D_OUT), minval=-stdv, maxval=stdv, dtype=jnp.float32)
        b_gcnb = jax.random.uniform(ks[6], (D_OUT,), minval=-stdv, maxval=stdv, dtype=jnp.float32)
        s = 1.0 / np.sqrt(2 * D_IN)
        Wa = jax.random.uniform(ks[7], (1, 2 * D_IN), minval=-s, maxval=s, dtype=jnp.float32)
        ba = jax.random.uniform(ks[8], (1,), minval=-s, maxval=s, dtype=jnp.float32)
        Wb = jax.random.uniform(ks[9], (1, 2 * D_IN), minval=-s, maxval=s, dtype=jnp.float32)
        bb = jax.random.uniform(ks[10], (1,), minval=-s, maxval=s, dtype=jnp.float32)
        return {'x': x, 'adj_a': adj_a, 'adj_b': adj_b, 'W_sa': W_sa, 'a_sa': a_sa, 'W_gcnb': W_gcnb, 'b_gcnb': b_gcnb, 'Wa': Wa, 'ba': ba, 'Wb': Wb, 'bb': bb}
    _L3_gnn_all = _L3_gnn_setup()
    _L3_gnn_in = {k: v for k, v in _L3_gnn_all.items() if k in ('W_sa', 'a_sa', 'W_gcnb', 'b_gcnb', 'Wa', 'ba', 'Wb', 'bb')}
    del _L3_gnn_all
    return {'x': x, 'adj': adj, 'L0_gnn_t': _L0_gnn_in['t'], 'L0_gnn_weight': _L0_gnn_in['weight'], 'L1_gnn_W1': _L1_gnn_in['W1'], 'L1_gnn_W2': _L1_gnn_in['W2'], 'L1_gnn_W3': _L1_gnn_in['W3'], 'L1_gnn_U1': _L1_gnn_in['U1'], 'L1_gnn_U2': _L1_gnn_in['U2'], 'L1_gnn_U3': _L1_gnn_in['U3'], 'L1_gnn_gamma': _L1_gnn_in['gamma'], 'L1_gnn_beta': _L1_gnn_in['beta'], 'L2_gnn_Wq': _L2_gnn_in['Wq'], 'L2_gnn_Wk': _L2_gnn_in['Wk'], 'L2_gnn_Wv': _L2_gnn_in['Wv'], 'L2_gnn_Wout': _L2_gnn_in['Wout'], 'L3_gnn_W_sa': _L3_gnn_in['W_sa'], 'L3_gnn_a_sa': _L3_gnn_in['a_sa'], 'L3_gnn_W_gcnb': _L3_gnn_in['W_gcnb'], 'L3_gnn_b_gcnb': _L3_gnn_in['b_gcnb'], 'L3_gnn_Wa': _L3_gnn_in['Wa'], 'L3_gnn_ba': _L3_gnn_in['ba'], 'L3_gnn_Wb': _L3_gnn_in['Wb'], 'L3_gnn_bb': _L3_gnn_in['bb']}

def reference(x, adj, L0_gnn_t, L0_gnn_weight, L1_gnn_W1, L1_gnn_W2, L1_gnn_W3, L1_gnn_U1, L1_gnn_U2, L1_gnn_U3, L1_gnn_gamma, L1_gnn_beta, L2_gnn_Wq, L2_gnn_Wk, L2_gnn_Wv, L2_gnn_Wout, L3_gnn_W_sa, L3_gnn_a_sa, L3_gnn_W_gcnb, L3_gnn_b_gcnb, L3_gnn_Wa, L3_gnn_ba, L3_gnn_Wb, L3_gnn_bb):
    import jax
    import jax.numpy as jnp

    def _L0_gnn_ref(x, adj, t, weight):
        import jax, jax.numpy as jnp
        import numpy as np
        N = 5000
        IN_F = 256
        OUT_F = 256
        ts = t[0]
        support = x @ weight
        return (1.0 - ts) * support + ts * (adj @ support)

    def _L1_gnn_ref(X, S, W1, W2, W3, U1, U2, U3, gamma, beta):
        import jax, jax.numpy as jnp
        import numpy as np
        N, D_IN, D_ATTN, STEPS, P_NUC, TAU = (2048, 256, 64, 2, 0.9, 1.0)
        LN_EPS = 1e-05

        def _xavier(key, shape):
            fan_in, fan_out = (shape[-2], shape[-1])
            lim = np.sqrt(6.0 / (fan_in + fan_out))
            return jax.random.uniform(key, shape, jnp.float32, -lim, lim)

        def _adj_from_feats(Xa, W1, W2, W3):
            Q = Xa @ W1
            K = Xa @ W3
            logits = Q @ W2 @ K.T / TAU
            idx = jnp.argsort(-logits, axis=1)
            vals = jnp.take_along_axis(logits, idx, axis=1)
            csum = jnp.cumsum(jax.nn.softmax(vals, axis=1), axis=1)
            k_i = jnp.sum(csum < P_NUC, axis=1) + 1
            ranks = jnp.arange(logits.shape[1])[None, :]
            keep_sorted = ranks < k_i[:, None]
            inv = jnp.argsort(idx, axis=1)
            keep = jnp.take_along_axis(keep_sorted, inv, axis=1)
            masked = jnp.where(keep, logits, -jnp.inf)
            return jax.nn.softmax(masked, axis=1)
        n = X.shape[0]
        S = S + jnp.eye(n, dtype=X.dtype)
        Rf = S / jnp.clip(S.sum(axis=1, keepdims=True), 1e-12)
        Rb = S / jnp.clip(S.sum(axis=0), 1e-12)[:, None]
        Xf, Xb, Xa = (X, X, X)
        Z = jnp.zeros_like(X)
        for s in range(STEPS):
            A = _adj_from_feats(Xa, W1, W2, W3)
            Xf = Rf @ Xf
            Xb = Rb @ Xb
            Xa = A @ Xa
            Z = Z + (Xf @ U1[s] + Xb @ U2[s] + Xa @ U3[s])
        Y = X + Z
        mu = Y.mean(axis=-1, keepdims=True)
        var = Y.var(axis=-1, keepdims=True)
        return (Y - mu) / jnp.sqrt(var + LN_EPS) * gamma + beta

    def _L2_gnn_ref(x, spatial_encoding, edge_encoding, Wq, Wk, Wv, Wout):
        import jax, jax.numpy as jnp
        import numpy as np
        N = 1024
        HID = 256
        H = 8
        n, d = x.shape
        h = Wq.shape[1] // d
        scale = d ** (-0.5)
        q = (x @ Wq).reshape(h, n, d)
        k = (x @ Wk).reshape(h, n, d)
        v = (x @ Wv).reshape(h, n, d)
        a = jnp.einsum('hnd,hmd->hnm', q, k) * scale
        a = a + spatial_encoding + edge_encoding
        mask = spatial_encoding == 0.0
        a = jnp.where(mask, -1000000.0, a)
        a = jax.nn.softmax(a, axis=-1)
        a = jnp.where(mask, 0.0, a)
        out = jnp.einsum('hnm,hmd->hnd', a, v)
        out = out.transpose(1, 0, 2).reshape(n, h * d)
        return out @ Wout

    def _L3_gnn_ref(x, adj_a, adj_b, W_sa, a_sa, W_gcnb, b_gcnb, Wa, ba, Wb, bb):
        import jax, jax.numpy as jnp
        import numpy as np
        N = 3072
        D_IN = 256
        D_OUT = 256
        DENSITY = 0.005
        type_sum_a = adj_a @ x
        type_sum_b = adj_b @ x
        attn_a = jax.nn.sigmoid(jnp.concatenate([type_sum_a, x], axis=1) @ Wa.T + ba)
        attn_b = jax.nn.sigmoid(jnp.concatenate([type_sum_b, x], axis=1) @ Wb.T + bb)
        h = x @ W_sa
        Hd = h.shape[1]
        s_left = h @ a_sa[0, :Hd]
        s_right = h @ a_sa[0, Hd:]
        scores = s_left[:, None] + s_right[None, :]
        e = jnp.where(adj_a != 0, jnp.exp(-jax.nn.leaky_relu(scores, 0.01)), 0.0)
        attn = e / (jnp.sum(e, axis=1, keepdims=True) + 1e-05)
        x_a = attn @ h
        x_b = adj_b @ (x @ W_gcnb) + b_gcnb
        return jax.nn.sigmoid(attn_a * x_a + attn_b * x_b)
    h = jnp.maximum(_layernorm(x, axis=-1), 0.0)
    x = x + _L0_gnn_ref(h, adj, L0_gnn_t, L0_gnn_weight)
    h = jnp.maximum(_layernorm(x, axis=-1), 0.0)
    x = x + _L1_gnn_ref(h, adj, L1_gnn_W1, L1_gnn_W2, L1_gnn_W3, L1_gnn_U1, L1_gnn_U2, L1_gnn_U3, L1_gnn_gamma, L1_gnn_beta)
    h = jnp.maximum(_layernorm(x, axis=-1), 0.0)
    x = x + _L2_gnn_ref(h, adj, adj, L2_gnn_Wq, L2_gnn_Wk, L2_gnn_Wv, L2_gnn_Wout)
    h = jnp.maximum(_layernorm(x, axis=-1), 0.0)
    x = x + _L3_gnn_ref(h, adj, adj, L3_gnn_W_sa, L3_gnn_a_sa, L3_gnn_W_gcnb, L3_gnn_b_gcnb, L3_gnn_Wa, L3_gnn_ba, L3_gnn_Wb, L3_gnn_bb)
    return x

_drawn_inputs = setup_inputs


def setup_inputs(seed=0):
    import zlib

    import numpy as np

    out = dict(_drawn_inputs(seed))
    spreads = {'L1_gnn_gamma': (1.0, 0.2), 'L1_gnn_beta': (0.0, 0.1)}
    factors = {'L3_gnn_a_sa': 187.448,
     'L3_gnn_b_gcnb': 34.656,
     'L3_gnn_Wa': 36.775,
     'L3_gnn_Wb': 2.692,
     'L3_gnn_W_sa': 4.482}
    for name, (base, spread) in spreads.items():
        noise = np.random.default_rng([zlib.crc32(name.encode()), seed]).standard_normal(out[name].shape)
        drawn = base * np.exp(spread * noise) if base else spread * noise
        out[name] = jnp.asarray(drawn.astype(out[name].dtype))
    for name, factor in factors.items():
        out[name] = (out[name] * factor).astype(out[name].dtype)
    return out
```

```python
import numpy as np
import concourse.bass as bass
from concourse import mybir
from contextlib import ExitStack

N, D, HEADS, D_ATTN, STEPS = 1354, 256, 8, 64, 2
P = 128
T = -(-N // P)
KD = D // P
ROWS = [min(P, N - t * P) for t in range(T)]
BANK = 512
CHUNKS = [(c * BANK, min(BANK, N - c * BANK)) for c in range(-(-N // BANK))]
QUADS = [range(4 * b, min(4 * b + 4, T)) for b in range(len(CHUNKS))]
LN_EPS = 1e-5
P_NUC = 0.9
MASKED = -1e6
SPAN = float(np.log(N / (1 - P_NUC)) + 0.05)
SEARCH = 24
FAST = (9, 11)
HN = (N + HEADS - 2 + HEADS - 1) // HEADS
LEAD = 8
PADDED = LEAD + HN * HEADS + 8
CGROUPS = [range(0, 3), range(3, 6), range(6, 8)]

HI, LO = 0, 1
PASSES = ((HI, HI), (HI, LO), (LO, HI))
W_SCALE = 64.0
LOG_P_SCALE = float(np.log(1024.0))
STAGE = HEADS * D

fp32 = mybir.dt.float32
fp16 = mybir.dt.float16
ALU = mybir.AluOpType
ACT = mybir.ActivationFunctionType
AX_X = mybir.AxisListType.X


def graph_layers(nc, x_in, adj, t_gate, W0, W1, W2, W3, U1, U2, U3, gamma, beta, Wq, Wk, Wv, Wout,
                 W_sa, a_sa, W_g, b_g, Wa, ba, Wb, bb, out):
    ctx = ExitStack()
    with ctx:
        def sb(name, cols):
            return ctx.enter_context(nc.sbuf_tensor(name, [P, cols], fp32))

        def sem(name):
            return ctx.enter_context(nc.semaphore(name))

        slot_a = sb("slot_a", T * N)
        slot_b = sb("slot_b", T * N)
        slot_x = sb("slot_x", T * D)
        slot_h = sb("slot_h", T * 257)
        slot_t = sb("slot_t", KD * N)
        slot_v = sb("slot_v", T * 260)
        slot_k = sb("slot_k", KD * PADDED)
        slot_p = sb("slot_p", 2 * T * P)
        slot_u = sb("slot_u", 12 * D)
        slot_w = sb("slot_w", 1024)
        tmp = sb("tmp", 4 * D)
        ident = sb("ident", P)
        ab = sb("ab", 4 * P)
        small = sb("small", 800)

        adjT = slot_a[:, :].rearrange("p (k n) -> p k n", k=T)
        rows_b = slot_b[:, :].rearrange("p (k n) -> p k n", k=T)
        x = slot_x[:, :].rearrange("p (t d) -> p t d", t=T)
        y = x
        h = slot_h[:, 0:T * D].rearrange("p (t d) -> p t d", t=T)
        hT = slot_t[:, :].rearrange("p (k n) -> p k n", k=KD)
        v = slot_v[:, 0:T * D].rearrange("p (t d) -> p t d", t=T)
        pT = slot_p[:, :].rearrange("p (s k n) -> p s k n", s=2, k=T)
        rings = tmp[:, :].rearrange("p (r d) -> p r d", r=4)
        qwT = slot_k[0:D_ATTN, 0:N]
        kT1 = slot_k[0:D_ATTN, N:2 * N]
        q1T = slot_p[0:D_ATTN, 0:N]
        junk = slot_p[:, 0:N]
        junk_a = slot_p[:, N:2 * N]
        u1 = slot_u[:, 0:4 * D].rearrange("p (k s d) -> p k s d", k=KD, s=STEPS)
        u2 = slot_u[:, 4 * D:8 * D].rearrange("p (k s d) -> p k s d", k=KD, s=STEPS)
        u3 = slot_u[:, 8 * D:12 * D].rearrange("p (k s d) -> p k s d", k=KD, s=STEPS)
        w0 = slot_w[:, 0:2 * D].rearrange("p (k d) -> p k d", k=KD)
        w1 = slot_w[:, 512:640].rearrange("p (k d) -> p k d", k=KD)
        w3 = slot_w[:, 640:768].rearrange("p (k d) -> p k d", k=KD)
        w2 = slot_w[0:D_ATTN, 768:832]
        gamma_b = ab[:, 0:D]
        beta_b = ab[:, D:2 * D]
        def parts(slot, cols, pattern, **sizes):
            return slot[:, 0:cols].bitcast(fp16).rearrange(pattern, s=2, **sizes)

        def weight(m):
            return parts(slot_b[:, 2 * STAGE * m:2 * STAGE * (m + 1)], 2 * STAGE, "p (s k n) -> p s k n", k=KD)

        wv, wk, wq = (weight(m) for m in range(3))
        stage_in = (slot_u[:, 0:STAGE], slot_b[:, 6 * STAGE:7 * STAGE])
        wout_in = slot_w[:, 0:2 * D].rearrange("p (k d) -> p k d", k=KD)
        wout = parts(slot_w[:, 2 * D:4 * D], 2 * D, "p (s k d) -> p s k d", k=KD)
        bias = adjT
        hT2 = parts(slot_t, KD * N, "p (s k n) -> p s k n", k=KD)
        qT = parts(slot_v, KD * PADDED, "p (s k n) -> p s k n", k=KD)
        vT = qT
        kT = parts(slot_k, KD * PADDED, "p (s k n) -> p s k n", k=KD)
        vw = parts(slot_h, T * D, "p (s t d) -> p s t d", t=T)
        pT2 = [parts(slot_p[:, i * T * P:(i + 1) * T * P], T * P, "p (s k n) -> p s k n", k=T) for i in range(2)]
        att = slot_u[:, 0:2 * N].rearrange("p (s n) -> p s n", s=2)
        edge = adjT
        adjT3 = rows_b
        hs = slot_h[:, :].rearrange("p (t d) -> p t d", t=T)
        hg = slot_v[:, :].rearrange("p (t d) -> p t d", t=T)
        w_s = slot_u[:, N:N + 2 * 257].rearrange("p (k d) -> p k d", k=KD)
        w_c = slot_u[:, N + 514:N + 514 + 2 * 260].rearrange("p (k d) -> p k d", k=KD)
        left = slot_u[:, 0:N]
        z = slot_k[:, 0:2 * N].rearrange("p (s n) -> p s n", s=2)
        a_left = slot_w[:, 0:D]
        a_right = slot_w[:, D:2 * D]
        bg_b = slot_w[:, 2 * D:3 * D]
        dot_junk = slot_w[:, 3 * D:4 * D]
        w_rep = ab[:, 0:2 * P].rearrange("p (k d) -> p k d", k=KD)
        conv = slot_p[:, 0:T * D].rearrange("p (t d) -> p t d", t=T)

        at = [0]

        def table(cols):
            at[0] += cols
            return small[:, at[0] - cols:at[0]]

        stats = table(6 * T).rearrange("p (t s) -> p t s", t=T)
        mean_var = table(2 * T).rearrange("p (t s) -> p t s", t=T)
        var_eps, std, rstd, nmean = table(T), table(T), table(T), table(T)
        row_sum, col_sum, row_inv, col_inv = table(T), table(T), table(T), table(T)
        top, neg_top, total, goal, low, cand, mass, good = (table(T) for _ in range(8))
        kept, kept_inv, above, cut, quota, down_to = (table(T) for _ in range(6))
        top8, sum8 = (table(8 * T).rearrange("p (t s) -> p t s", t=T) for _ in range(2))
        ones_row, flags, flags_all = table(1), table(2), table(2)
        flags_int = table(2).bitcast(mybir.dt.int32)
        steps = table(SEARCH)
        step_now = table(1)
        ts, one_minus_ts = table(1), table(1)
        right, gate_a, gate_b, den = table(T), table(T), table(T), table(T)
        ba_b, bb_b, w_left = table(1), table(1), table(KD)

        psum = ctx.enter_context(nc.psum_tensor("psum", [P, 8 * BANK], fp32))

        def bank(b, w=BANK, rows=P):
            return psum[0:rows, b * BANK:b * BANK + w]

        PT_PIECES = ((P, 0, 4), (P, 4, 8), (P, 8, T - 1), (ROWS[-1], T - 1, T))
        UNSCALE = (1 / W_SCALE, 1 / W_SCALE, D ** -0.5 / W_SCALE)

        def pt_bank(k0, k1, rows, r):
            return bank(3 + k0 // 4)[0:rows, (k0 % 4) * P:(k0 % 4 + k1 - k0) * P].rearrange(
                "p (k n) -> p k n", n=P)[:, :, 0:r]

        def own_wait(engine, signal, value, passed):
            engine.wait_ge(signal, value)
            engine.sem_inc(passed, 1)

        def head_bank(half, g, group):
            return psum[:, (3 * half + g) * BANK:(3 * half + g) * BANK + len(group) * HN].rearrange(
                "p (c i) -> p c i", i=HN)

        def head_cols(dst, part, half, b, group):
            start = b * -2 + (LEAD + group[0])
            run = dst[:, part, half, bass.ds(start, HN * HEADS)].rearrange("p (i c) -> p c i", c=HEADS)
            return run[:, 0:len(group), :]

        y_dram = nc.dram_tensor("x_after_layer_0", (N, D), fp32, kind="Internal").ap()

        s_x_pad, s_x_in, s_w_in, s_ident, s_ones = (sem(n) for n in ("x_pad", "x_in", "w_in", "ident", "ones"))
        s_adj_in = [sem(f"adj_in{b}") for b in range(3)]
        s_u_in, s_gb_in, s_x_out, s_x_back, s_adj_again = (
            sem(n) for n in ("u_in", "gamma_beta_in", "x_spilled", "x_back", "adj_again"))
        s_stage = [sem("stage_in0"), sem("stage_in1")]
        s_w_hi, s_w_lo, s_wout_hi, s_wout_lo = (sem(n) for n in ("w_hi", "w_lo", "wout_hi", "wout_lo"))
        s_wout, s_l3_in, s_out = (sem(n) for n in ("wout_in", "layer3_in", "out"))
        s_ln_var, s_ln_std, s_ln_coef, s_h_rows = (sem(n) for n in ("ln_var", "ln_std", "ln_coef", "h_rows"))
        s_tr, s_hT_dve, s_hT_act = (sem(n) for n in ("transposed", "hT_dve", "hT_act"))
        s_adj_tr, s_adjT_dve, s_adjT_act = (sem(n) for n in ("adj_tr", "adjT_dve", "adjT_act"))
        s_sup, s_sup_taken, s_mix0, s_x0 = (sem(n) for n in ("support", "support_taken", "layer0_product", "x0"))
        s_sums, s_inv, s_s_ready = (sem(n) for n in ("sums", "inv", "s_ready"))
        s_proj, s_proj_taken = sem("l1_proj"), sem("l1_proj_taken")
        s_logit, s_top, s_exp = sem("logits"), sem("top"), sem("exp")
        s_a_rows, s_kept_inv = sem("a_rows"), sem("kept_inv")
        s_a_tr, s_pt_act, s_pt_dve = sem("a_transposed"), sem("pT_act"), sem("pT_dve")
        s_step, s_step_taken = sem("l1_step"), sem("l1_step_taken")
        s_part, s_y_add = sem("y_part"), sem("y_added")
        s_bias = sem("bias")
        s_hproj, s_hproj_dve, s_hproj_act = sem("head_proj"), sem("head_proj_lo"), sem("head_proj_hi")
        s_vw, s_vw_act, s_vw_dve = sem("vw"), sem("vw_act"), sem("vw_dve")
        s_qk, s_biased, s_neg, s_hexp, s_masked = (
            sem(n) for n in ("qk", "biased", "neg_max", "head_exp", "masked"))
        s_htr, s_hpt_act, s_hpt_dve = sem("head_tr"), sem("head_pT_act"), sem("head_pT_dve")
        s_hinv, s_pv, s_x_add = sem("head_inv"), sem("pv"), sem("x_added")
        s_unbias, s_l3w, s_l3proj, s_l3proj_taken = sem("unbiased"), sem("l3_w"), sem("l3_proj"), sem("l3_proj_taken")
        s_left, s_left_taken = sem("left"), sem("left_taken")
        s_z, s_e, s_edge = sem("z"), sem("edge_exp"), sem("edge")
        s_conv, s_conv_taken, s_gate = sem("conv"), sem("conv_taken"), sem("gate")
        s_gat, s_mixed, s_sig, s_done = sem("gat"), sem("mixed"), sem("sigmoid"), sem("done")
        s_dve, s_act_passed, s_pool = sem("dve_chain"), sem("act_passed"), sem("pool_chain")
        s_halve, s_cut, s_halve_on, s_cut_on, s_tied = (
            [sem(f"{n}_step{i}") for i in range(STEPS)] for n in ("halve", "cut", "halve_on", "cut_on", "tied"))
        s_flags, s_flags_all = sem("flags"), sem("flags_all")
        s_x_final, s_hg, s_dve_passed = sem("x_final"), sem("hg"), sem("dve_passed")

        block = ctx.enter_context(nc.Block())

        def rows_of(dram, t0, t1):
            return dram[t0 * P:t1 * P, :].rearrange("(t p) d -> p t d", p=P)

        def col_tiles(w):
            return w.rearrange("(k p) d -> p k d", p=P)

        TL, RL = T - 1, ROWS[-1]

        DIFFUSED = 6 + 4 * T
        L3_LOADS = 16 * (2 + 4 * KD + 5)
        KEEP, PART, BOTH = range(3)
        kinds = [KEEP] * 6 + ([BOTH] * T + [PART] * T) * 2 + [KEEP] * T + [BOTH] * T + [PART] * T

        def step_freed(n):
            if kinds[n] == PART:
                return s_part, sum(k != KEEP for k in kinds[:n + 1])
            return s_step_taken, sum(k != PART for k in kinds[:n + 1])


        @block.sync
        def _(sp):
            sp.dma_start(x[:, 0:TL, :], rows_of(x_in, 0, TL)).then_inc(s_x_in, 16)
            sp.wait_ge(s_x_pad, 1)
            sp.dma_start(x[0:RL, TL, :], x_in[TL * P:N, :]).then_inc(s_x_in, 16)
            sp.dma_start(w0, col_tiles(W0)).then_inc(s_w_in, 16)
            for b, quad in enumerate(QUADS):
                full = [t for t in quad if t < TL]
                sp.dma_start(rows_b[:, full[0]:full[-1] + 1, :],
                             rows_of(adj, full[0], full[-1] + 1)).then_inc(s_adj_in[b], 16)
            sp.dma_start(rows_b[0:RL, TL, :], adj[TL * P:N, :]).then_inc(s_adj_in[2], 16)
            sp.dma_start(ts, t_gate.partition_broadcast(P)).then_inc(s_w_in, 16)
            sp.dma_start(w1, col_tiles(W1)).then_inc(s_w_in, 16)
            sp.dma_start(w3, col_tiles(W3)).then_inc(s_w_in, 16)
            sp.dma_start(w2, W2).then_inc(s_w_in, 16)
            for u, src in ((u1, U1), (u2, U2), (u3, U3)):
                for s in range(STEPS):
                    sp.dma_start(u[:, :, s, :], col_tiles(src[s, :, :])).then_inc(s_u_in, 16)
            sp.dma_start(gamma_b, gamma.partition_broadcast(P)).then_inc(s_gb_in, 16)
            sp.dma_start(beta_b, beta.partition_broadcast(P)).then_inc(s_gb_in, 16)
            sp.wait_ge(s_x0, T)
            sp.dma_start(rows_of(y_dram, 0, TL), x[:, 0:TL, :]).then_inc(s_x_out, 16)
            sp.dma_start(y_dram[TL * P:N, :], x[0:RL, TL, :]).then_inc(s_x_out, 16)
            sp.wait_ge(s_step, DIFFUSED)
            sp.dma_start(adjT[:, 0:TL, :], rows_of(adj, 0, TL)).then_inc(s_adj_again, 16)
            sp.dma_start(adjT[0:RL, TL, :], adj[TL * P:N, :]).then_inc(s_adj_again, 16)
            sp.wait_ge(s_x_out, 32)
            sp.wait_ge(s_step, DIFFUSED + T)
            sp.wait_ge(s_y_add, T)
            sp.dma_start(h[:, 0:TL, :], rows_of(y_dram, 0, TL)).then_inc(s_x_back, 16)
            sp.dma_start(h[0:RL, TL, :], y_dram[TL * P:N, :]).then_inc(s_x_back, 16)
            for u in range(6):
                if u == 0:
                    sp.wait_ge(s_step, DIFFUSED)
                elif u == 1:
                    sp.wait_ge(s_a_tr, 2 * 3 * T)
                else:
                    sp.wait_ge(s_w_lo, u - 1)
                w = (Wv, Wk, Wq)[u // KD]
                sp.dma_start(stage_in[u % 2], w[(u % KD) * P:(u % KD + 1) * P, :]).then_inc(s_stage[u % 2], 16)
            with sp.Fori(0, HEADS) as a:
                sp.wait_ge(s_wout_lo, a + 1)
                sp.dma_start(wout_in, Wout[bass.ds(a * D, D), :].rearrange("(k p) d -> p k d", p=P)).then_inc(s_wout, 16)
            sp.wait_ge(s_x_add, 1 + HEADS * T)
            sp.dma_start(w_s[:, :, 0:D], col_tiles(W_sa)).then_inc(s_l3_in, 16)
            sp.dma_start(w_c[:, :, 0:D], col_tiles(W_g)).then_inc(s_l3_in, 16)
            for j, (w, half) in enumerate(((Wa, 0), (Wb, 0), (Wa, 1), (Wb, 1))):
                src = w[0, half * D:(half + 1) * D].rearrange("(k p a) -> p k a", p=P, a=1)
                for kd in range(KD):
                    sp.dma_start(w_c[:, kd, D + j:D + j + 1], src[:, kd, :]).then_inc(s_l3_in, 16)
            sp.dma_start(a_left, a_sa[0, 0:D].partition_broadcast(P)).then_inc(s_l3_in, 16)
            sp.dma_start(a_right, a_sa[0, D:2 * D].partition_broadcast(P)).then_inc(s_l3_in, 16)
            sp.dma_start(bg_b, b_g.partition_broadcast(P)).then_inc(s_l3_in, 16)
            sp.dma_start(ba_b, ba.partition_broadcast(P)).then_inc(s_l3_in, 16)
            sp.dma_start(bb_b, bb.partition_broadcast(P)).then_inc(s_l3_in, 16)
            for t in range(T):
                sp.wait_ge(s_done, t + 1)
                sp.dma_start(out[t * P:t * P + ROWS[t], :], x[0:ROWS[t], t, :]).then_inc(s_out, 16)
            sp.wait_ge(s_out, 16 * T)

        @block.gpsimd
        def _(pool):
            chain = [0]

            def link(ins):
                chain[0] += 1
                ins.then_inc(s_pool, 1)
                pool.wait_ge(s_pool, chain[0])

            nc.gpsimd.memset(x[:, TL, :], 0.0).then_inc(s_x_pad, 1)
            link(nc.gpsimd.memset(ident[:, :], 0.0))
            nc.gpsimd.affine_select(out=ident[:, :], in_=ident[:, :], compare_op=ALU.not_equal, fill=1.0, base=0,
                                    pattern=[[-1, P]], channel_multiplier=1).then_inc(s_ident, 1)
            for table_, value in ((row_sum, 1.0), (col_sum, 1.0), (total, 1.0), (mass, 0.0), (kept, 1.0),
                                  (ones_row, 1.0), (top8, 1.0), (down_to, 1.0)):
                nc.gpsimd.memset(table_, value)
            for i in range(SEARCH):
                last = nc.gpsimd.memset(steps[:, i:i + 1], float(np.expm1(SPAN / 2.0 ** (i + 1))))
            last.then_inc(s_ones, 1)

            def any_row(s):
                pool.wait_ge(s_flags, s + 1)
                nc.gpsimd.partition_all_reduce(flags_all, flags, P, bass.bass_isa.ReduceOp.max).then_inc(s_flags_all, 1)

            pool.wait_ge(s_x_out, 32)
            n = 0
            for stage in range(6):
                for t in range(T):
                    pool.wait_ge(s_part, n + 1)
                    if stage:
                        pool.wait_ge(s_y_add, n - T + 1)
                    nc.gpsimd.tensor_tensor(y[0:ROWS[t], t, :], (y if stage else h)[0:ROWS[t], t, :],
                                            rings[0:ROWS[t], n % 4, :], ALU.add).then_inc(s_y_add, 1)
                    n += 1
                if stage == 3:
                    any_row(0)
                if stage == 4:
                    pool.wait_ge(s_y_add, n)
                    pool.wait_ge(s_adj_again, 32)
                    for k in range(T):
                        r = ROWS[k]
                        for c, w in CHUNKS:
                            part = adjT[0:r, k, c:c + w]
                            hole = tmp[0:r, 2 * D:2 * D + w]
                            link(nc.gpsimd.tensor_scalar(hole, part, 0.0, MASKED, ALU.is_equal, ALU.mult))
                            link(nc.gpsimd.tensor_tensor(part, part, part, ALU.add))
                            link(nc.gpsimd.tensor_tensor(part, part, hole, ALU.add))
                    pool.sem_inc(s_bias, 1)
                    any_row(1)
            pool.wait_ge(s_x_back, 32)
            pool.wait_ge(s_gb_in, 32)
            for t in range(T):
                nc.gpsimd.tensor_tensor(h[0:ROWS[t], t, :], h[0:ROWS[t], t, :], beta_b[0:ROWS[t], :],
                                        ALU.add).then_inc(s_y_add, 1)

            for t in range(T):
                r = ROWS[t]
                pool.wait_ge(s_sig, t + 1)
                nc.gpsimd.tensor_tensor(x[0:r, t, :], x[0:r, t, :], conv[0:r, t, :], ALU.add).then_inc(s_done, 1)

        @block.tensor
        def _(pe):
            def transpose_rows(q, src, ready, base):
                for b, quad in enumerate(QUADS):
                    pe.wait_ge(ready, base + quad[-1] + 1)
                    for kd in range(KD):
                        for i, t in enumerate(quad):
                            last = nc.tensor.transpose(bank(2 * b + kd)[:, i * P:i * P + ROWS[t]],
                                                       src[0:ROWS[t], t, kd * P:(kd + 1) * P],
                                                       ident[0:ROWS[t], 0:ROWS[t]])
                        last.then_inc(s_tr, 1)

            def wait_hT(q):
                pe.wait_ge(s_hT_dve, 3 * (q + 1) + (3 if q > 3 else 0))
                pe.wait_ge(s_hT_act, 3 * (q + 1) + (3 if q > 3 else 0))

            def times_adjT(dst, rhs, t, lhs=adjT):
                for k in range(T):
                    last = nc.tensor.matmul(dst, lhs[0:ROWS[k], k, t * P:t * P + ROWS[t]], rhs[0:ROWS[k], k, :],
                                            start=(k == 0), stop=(k == T - 1))
                return last

            def times_hT(dst, w, t):
                for kd in range(KD):
                    last = nc.tensor.matmul(dst, hT[:, kd, t * P:t * P + ROWS[t]], w[:, kd, :],
                                            start=(kd == 0), stop=(kd == KD - 1))
                return last

            pe.wait_ge(s_ident, 1)
            transpose_rows(0, h, s_h_rows, 0)
            wait_hT(0)
            u = 0
            for b, quad in enumerate(QUADS):
                pe.wait_ge(s_adj_in[b], 16 if b < 2 else 32)
                for k in range(T):
                    if u >= 8:
                        pe.wait_ge(s_adjT_act if u % 2 == 0 else s_adjT_dve, (u - 8) // 2 + 1)
                    for i, t in enumerate(quad):
                        last = nc.tensor.transpose(bank(u % 8)[0:ROWS[k], i * P:i * P + ROWS[t]],
                                                   rows_b[0:ROWS[t], t, k * P:k * P + ROWS[k]],
                                                   ident[0:ROWS[t], 0:ROWS[t]])
                    last.then_inc(s_adj_tr, 1)
                    u += 1
            pe.wait_ge(s_adjT_act, 17)
            pe.wait_ge(s_adjT_dve, 16)
            pe.wait_ge(s_w_in, 16 * 5)
            for t in range(T):
                if t >= 8:
                    pe.wait_ge(s_sup_taken, t - 7)
                times_hT(bank(t % 8, D, ROWS[t]), w0, t).then_inc(s_sup, 1)
            pe.wait_ge(s_sup_taken, T)
            for t in range(T):
                if t >= 8:
                    pe.wait_ge(s_x0, t - 7)
                times_adjT(bank(t % 8, D, ROWS[t]), v, t).then_inc(s_mix0, 1)

            pe.wait_ge(s_x0, T)
            transpose_rows(1, h, s_h_rows, T)

            def project_qk(s):
                wait_hT(1 + s)
                for first, w in ((0, w1), (3, w3)):
                    for c, (c0, cw) in enumerate(CHUNKS):
                        for kd in range(KD):
                            last = nc.tensor.matmul(bank(first + c, cw, D_ATTN), w[:, kd, :], hT[:, kd, c0:c0 + cw],
                                                    start=(kd == 0), stop=(kd == KD - 1))
                        last.then_inc(s_proj, 1)
                for c, (c0, cw) in enumerate(CHUNKS):
                    pe.wait_ge(s_proj_taken, 9 * s + c + 1)
                    nc.tensor.matmul(bank(c, cw, D_ATTN), w2, q1T[:, c0:c0 + cw],
                                     start=True, stop=True).then_inc(s_proj, 1)

            def logits(s):
                pe.wait_ge(s_proj_taken, 9 * (s + 1))
                for t in range(T):
                    i = T * s + t
                    if t >= 2:
                        pe.wait_ge(s_exp, i - 1)
                    for c, (c0, cw) in enumerate(CHUNKS):
                        last = nc.tensor.matmul(bank(3 * (t % 2) + c, cw, ROWS[t]), qwT[:, t * P:t * P + ROWS[t]],
                                                kT1[:, c0:c0 + cw], start=True, stop=True)
                    last.then_inc(s_logit, 1)

            steps_made = [0]

            def step_done(last):
                last.then_inc(s_step, 1)
                steps_made[0] += 1

            def step_bank():
                if steps_made[0] >= 2:
                    pe.wait_ge(*step_freed(steps_made[0] - 2))
                return 6 + steps_made[0] % 2

            def attention_step(s, rhs):
                def product(t):
                    i = T * s + t
                    pe.wait_ge(s_pt_act, i + 1)
                    pe.wait_ge(s_pt_dve, i + 1)
                    dst = bank(step_bank(), D, ROWS[t])
                    for k in range(T):
                        last = nc.tensor.matmul(dst, pT[0:ROWS[k], t % 2, k, 0:ROWS[t]], rhs[0:ROWS[k], k, :],
                                                start=(k == 0), stop=(k == T - 1))
                    step_done(last)

                for t in range(T):
                    pe.wait_ge(s_a_rows, T * s + t + 1)
                    for b, quad in enumerate(QUADS):
                        for i, k in enumerate(quad):
                            last = nc.tensor.transpose(
                                bank(3 * (t % 2) + b)[0:ROWS[k], i * P:i * P + ROWS[t]],
                                rows_b[0:ROWS[t], t, k * P:k * P + ROWS[k]], ident[0:ROWS[t], 0:ROWS[t]])
                        last.then_inc(s_a_tr, 1)
                    if t:
                        product(t - 1)
                product(T - 1)

            project_qk(0)
            logits(0)
            pe.wait_ge(s_s_ready, 1)
            for kd in range(KD):
                for c0, cw in CHUNKS:
                    dst = bank(step_bank(), cw)
                    for k in range(T):
                        last = nc.tensor.matmul(dst, h[0:ROWS[k], k, kd * P:(kd + 1) * P],
                                                adjT[0:ROWS[k], k, c0:c0 + cw], start=(k == 0), stop=(k == T - 1))
                    step_done(last)
            pe.wait_ge(s_step_taken, 6)
            pe.wait_ge(s_u_in, 16 * 6)
            for u in (u1, u2):
                for t in range(T):
                    step_done(times_hT(bank(step_bank(), 2 * D, ROWS[t]), u.rearrange("p k s d -> p k (s d)"), t))
                pe.wait_ge(*step_freed(steps_made[0] - 1))
                for t in range(T):
                    step_done(times_adjT(bank(step_bank(), D, ROWS[t]), v, t))
            attention_step(0, h)
            transpose_rows(2, v, s_step_taken, DIFFUSED - 2 * T)
            wait_hT(2)
            for t in range(T):
                step_done(times_hT(bank(step_bank(), 2 * D, ROWS[t]), u3.rearrange("p k s d -> p k (s d)"), t))
            project_qk(1)
            logits(1)
            attention_step(1, v)

            transpose_rows(3, h, s_h_rows, 2 * T)
            pe.wait_ge(s_hT_dve, 15)
            pe.wait_ge(s_bias, 1)

            def split_product(dst, pieces, last_of=None):
                for n, (lhs, rhs) in enumerate(pieces):
                    for m, (pl, pr) in enumerate(PASSES):
                        last = nc.tensor.matmul(dst, lhs(pl), rhs(pr), start=(n == 0 and m == 0),
                                                stop=(n == len(pieces) - 1 and m == len(PASSES) - 1))
                return last

            def head(a, base):
                def project(which, w):
                    pe.wait_ge(s_w_lo, KD * (which + 1))
                    for half in range(KD):
                        for g, group in enumerate(CGROUPS):
                            if which:
                                pe.wait_ge(s_hproj_dve, a * 18 + (6 * (which - 1) + 3 * half + g + 1))
                            for i, c in enumerate(group):
                                c0 = c * D + half * P
                                last = split_product(
                                    bank(3 * half + g)[:, i * HN:(i + 1) * HN],
                                    [(lambda p, kd=kd: w[:, p, kd, c0:c0 + P],
                                      lambda p, kd=kd: hT2[:, p, kd, bass.ds(base, HN)]) for kd in range(KD)])
                            last.then_inc(s_hproj, 1)

                project(0, wv)
                project(1, wk)
                pe.wait_ge(s_hproj_dve, a * 18 + 6)
                pe.wait_ge(s_wout_lo, a + 2)
                pe.wait_ge(s_x_add, a * T + 1)
                for t in range(T):
                    if t >= 2:
                        pe.wait_ge(s_vw_dve, a * T + (t - 1))
                    split_product(bank(6 + t % 2, D, ROWS[t]),
                                  [(lambda p, kd=kd: vT[:, p, kd, LEAD + t * P:LEAD + t * P + ROWS[t]],
                                    lambda p, kd=kd: wout[:, p, kd, :]) for kd in range(KD)]).then_inc(s_vw, 1)
                project(2, wq)
                pe.wait_ge(s_hproj_dve, a * 18 + 18)
                for t in range(T + 2):
                    if t < T:
                        if t:
                            pe.wait_ge(s_biased, a * T + t)
                        for c, (c0, cw) in enumerate(CHUNKS):
                            last = split_product(
                                bank(c, cw, ROWS[t]),
                                [(lambda p, kd=kd: qT[:, p, kd, LEAD + t * P:LEAD + t * P + ROWS[t]],
                                  lambda p, kd=kd: kT[:, p, kd, LEAD + c0:LEAD + c0 + cw]) for kd in range(KD)])
                        last.then_inc(s_qk, 1)
                    if 1 <= t <= T:
                        i = t - 1
                        pe.wait_ge(s_masked, a * T + (i + 1))
                        if i:
                            pe.wait_ge(s_hpt_dve, a * T + i)
                        for b, quad in enumerate(QUADS):
                            for j, k in enumerate(quad):
                                last = nc.tensor.transpose(
                                    bank(3 + b)[0:ROWS[k], j * P:j * P + ROWS[i]],
                                    att[0:ROWS[i], i % 2, k * P:k * P + ROWS[k]], ident[0:ROWS[i], 0:ROWS[i]])
                            last.then_inc(s_htr, 1)
                    if t >= 2:
                        i = t - 2
                        pe.wait_ge(s_hpt_dve, a * T + (i + 1))
                        if i == 0:
                            pe.wait_ge(s_vw_dve, a * T + T)
                        if i >= 2:
                            pe.wait_ge(s_x_add, a * T + i)
                        split_product(bank(6 + i % 2, D, ROWS[i]),
                                      [(lambda p, k=k: pT2[i % 2][0:ROWS[k], p, k, 0:ROWS[i]],
                                        lambda p, k=k: vw[0:ROWS[k], p, k, :]) for k in range(T)]).then_inc(s_pv, 1)

            with pe.Fori(0, 2) as g:
                with pe.Fori(0, 4) as b:
                    head(g * 4 + b, g * 677 + b * 169)

            pe.wait_ge(s_x_add, 1 + HEADS * T)
            transpose_rows(4, h, s_h_rows, 3 * T)
            wait_hT(4)
            u = 0
            for b, quad in enumerate(QUADS):
                pe.wait_ge(s_unbias, quad[-1] + 1)
                for k in range(T):
                    if u >= 6:
                        pe.wait_ge(s_adjT_act if u % 2 == 0 else s_adjT_dve, (17 if u % 2 == 0 else 16) + (u - 6) // 2 + 1)
                    for i, t in enumerate(quad):
                        last = nc.tensor.transpose(bank(u % 6)[0:ROWS[k], i * P:i * P + ROWS[t]],
                                                   bias[0:ROWS[t], t, k * P:k * P + ROWS[k]],
                                                   ident[0:ROWS[t], 0:ROWS[t]])
                    last.then_inc(s_adj_tr, 1)
                    u += 1
            pe.wait_ge(s_adjT_act, 34)
            pe.wait_ge(s_adjT_dve, 32)
            pe.wait_ge(s_l3w, 1)
            for c, (c0, cw) in enumerate(CHUNKS):
                for kd in range(KD):
                    last = nc.tensor.matmul(bank(c, cw), w_rep[:, kd, :], hT[:, kd, c0:c0 + cw],
                                            start=(kd == 0), stop=(kd == KD - 1))
                last.then_inc(s_left, 1)
            for t in range(T):
                if t >= 2:
                    pe.wait_ge(s_l3proj_taken, t - 1)
                    pe.wait_ge(s_hg, t - 1)
                b0 = (4, 6)[t % 2]
                times_hT(bank(b0, 257, ROWS[t]), w_s, t)
                times_hT(bank(b0 + 1, 260, ROWS[t]), w_c, t).then_inc(s_l3proj, 1)
            pe.wait_ge(s_l3proj_taken, T)
            pe.wait_ge(s_hg, T)
            pe.wait_ge(s_left_taken, 3)
            for t in range(T):
                if t >= 2:
                    pe.wait_ge(s_conv_taken, t - 1)
                times_adjT(bank(t % 2, 258, ROWS[t]), hg[:, :, 0:258], t, adjT3).then_inc(s_conv, 1)
            pe.wait_ge(s_edge, T)
            for t in range(T):
                if t >= 2:
                    pe.wait_ge(s_mixed, t - 1)
                times_adjT(bank(2 + t % 2, 257, ROWS[t]), hs[:, :, 0:257], t, edge).then_inc(s_gat, 1)

        @block.scalar
        def _(act):
            def norm_rows(n):
                act.wait_ge(s_ln_var, n + 1)
                nc.scalar.activation(std, var_eps, ACT.Sqrt).then_inc(s_ln_std, 1)
                if n == 2:
                    return
                act.wait_ge(s_ln_coef, n + 1)
                for t in range(T):
                    nc.scalar.activation(h[:, t, :], x[:, t, :], ACT.Relu, bias=nmean[:, t:t + 1],
                                         scale=rstd[:, t:t + 1]).then_inc(s_h_rows, 1)

            def take_hT(q):
                for b, (c0, cw) in enumerate(CHUNKS):
                    act.wait_ge(s_tr, 6 * q + 2 * b + 2)
                    nc.scalar.activation(hT[:, 1, c0:c0 + cw], bank(2 * b + 1, cw), ACT.Copy).then_inc(s_hT_act, 1)

            norm_rows(0)
            take_hT(0)
            u = 0
            for b, (c0, cw) in enumerate(CHUNKS):
                for k in range(T):
                    if u % 2 == 0:
                        act.wait_ge(s_adj_tr, u + 1)
                        nc.scalar.activation(adjT[0:ROWS[k], k, c0:c0 + cw], bank(u % 8, cw, ROWS[k]),
                                             ACT.Copy).then_inc(s_adjT_act, 1)
                    u += 1
            for t in range(T):
                act.wait_ge(s_sup, t + 1)
                nc.scalar.activation(v[0:ROWS[t], t, :], bank(t % 8, D, ROWS[t]), ACT.Copy).then_inc(s_sup_taken, 1)
            act.wait_ge(s_adjT_dve, 16)
            act.wait_ge(s_ones, 1)
            for t in range(T):
                r = ROWS[t]
                if t:
                    act.wait_ge(s_sums, 2 * t)
                nc.scalar.activation(junk_a[0:r, :], rows_b[0:r, t, :], ACT.Copy,
                                     accum_out=row_sum[0:r, t:t + 1]).then_inc(s_sums, 1)
                nc.scalar.activation(junk[0:r, :], adjT[0:r, t, :], ACT.Copy,
                                     accum_out=col_sum[0:r, t:t + 1]).then_inc(s_sums, 1)
            norm_rows(1)
            take_hT(1)

            def take_qk(s):
                for first, dst in ((0, q1T), (3, kT1), (0, qwT)):
                    for c, (c0, cw) in enumerate(CHUNKS):
                        n = 9 * s + (0 if dst is q1T else 3 if dst is kT1 else 6) + c
                        act.wait_ge(s_proj, n + 1)
                        nc.scalar.activation(dst[:, c0:c0 + cw], bank(first + c, cw, D_ATTN),
                                             ACT.Copy).then_inc(s_proj_taken, 1)

            def exps(s):
                for t in range(T):
                    r = ROWS[t]
                    act.wait_ge(s_top, T * s + t + 1)
                    b0 = 3 * (t % 2) * BANK
                    nc.scalar.activation(rows_b[0:r, t, :], psum[0:r, b0:b0 + N], ACT.Exp, bias=neg_top[0:r, t:t + 1],
                                         accum_out=total[0:r, t:t + 1]).then_inc(s_exp, 1)

            taken = [0]
            parts = [0]

            def part(src, scale, r):
                if parts[0] >= 4:
                    act.wait_ge(s_y_add, parts[0] - 3)
                parts[0] += 1
                nc.scalar.activation(rings[0:r, (parts[0] - 1) % 4, :], src, ACT.Copy,
                                     scale=scale).then_inc(s_part, 1)

            def next_step():
                act.wait_ge(s_step, taken[0] + 1)
                taken[0] += 1
                return 6 + (taken[0] - 1) % 2

            take_qk(0)
            exps(0)
            for kd in range(KD):
                for c0, cw in CHUNKS:
                    b = next_step()
                    nc.scalar.activation(hT[:, kd, c0:c0 + cw], bank(b, cw), ACT.Copy).then_inc(s_step_taken, 1)
            act.wait_ge(s_inv, 1)
            for inv in (row_inv, col_inv):
                for t in range(T):
                    r = ROWS[t]
                    b = next_step()
                    part(bank(b, D, r), inv[0:r, t:t + 1], r)
                    nc.scalar.activation(v[0:r, t, :], psum[0:r, b * BANK + D:b * BANK + 2 * D], ACT.Copy,
                                         scale=inv[0:r, t:t + 1]).then_inc(s_step_taken, 1)
                for t in range(T):
                    r = ROWS[t]
                    b = next_step()
                    part(bank(b, D, r), inv[0:r, t:t + 1], r)

            def take_pT(s, t):
                i = T * s + t
                act.wait_ge(s_a_tr, 3 * i + 3)
                b0 = 3 * (t % 2)
                r = ROWS[t]
                nc.scalar.activation(pT[:, t % 2, 0:4, 0:r],
                                     bank(b0).rearrange("p (k n) -> p k n", n=P)[:, :, 0:r], ACT.Copy)
                nc.scalar.activation(pT[:, t % 2, 8:10, 0:r],
                                     bank(b0 + 2, 2 * P).rearrange("p (k n) -> p k n", n=P)[:, :, 0:r], ACT.Copy)
                nc.scalar.activation(pT[0:RL, t % 2, TL, 0:r], bank(b0 + 2)[0:RL, 2 * P:2 * P + r],
                                     ACT.Copy).then_inc(s_pt_act, 1)

            def attention(s):
                def product(t):
                    r = ROWS[t]
                    b = next_step()
                    act.wait_ge(s_kept_inv, T * s + t + 1)
                    if s == 0:
                        nc.scalar.activation(v[0:r, t, :], bank(b, D, r), ACT.Copy,
                                             scale=kept_inv[0:r, t:t + 1]).then_inc(s_step_taken, 1)
                    else:
                        act.wait_ge(s_bias, 1)
                        part(bank(b, D, r), kept_inv[0:r, t:t + 1], r)

                for t in range(T):
                    take_pT(s, t)
                    if t:
                        product(t - 1)
                product(T - 1)

            attention(0)
            take_hT(2)
            for t in range(T):
                r = ROWS[t]
                b = next_step()
                part(bank(b, D, r), 1.0, r)
                nc.scalar.activation(v[0:r, t, :], psum[0:r, b * BANK + D:b * BANK + 2 * D],
                                     ACT.Copy).then_inc(s_step_taken, 1)
            take_qk(1)
            exps(1)
            attention(1)
            norm_rows(2)

            norm_rows(3)
            for b, (c0, cw) in enumerate(CHUNKS):
                for kd in range(KD):
                    act.wait_ge(s_tr, 6 * 3 + 2 * b + kd + 1)
                    nc.scalar.activation(hT2[:, HI, kd, c0:c0 + cw], bank(2 * b + kd, cw),
                                         ACT.Copy).then_inc(s_hT_act, 1)
            for u in range(6):
                act.wait_ge(s_stage[u % 2], 16 * (u // 2 + 1))
                nc.scalar.activation((wv, wk, wq)[u // KD][:, HI, u % KD, :], stage_in[u % 2], ACT.Copy,
                                     scale=W_SCALE).then_inc(s_w_hi, 1)

            def head(a, b):
                act.wait_ge(s_wout, a * 16 + 16)
                nc.scalar.activation(wout[:, HI, :, :], wout_in, ACT.Copy, scale=W_SCALE).then_inc(s_wout_hi, 1)
                for which, dst in enumerate((vT, kT, qT)):
                    for half in range(KD):
                        for g, group in enumerate(CGROUPS):
                            own_wait(act, s_hproj, a * 18 + (6 * which + 3 * half + g + 1), s_act_passed)
                            nc.scalar.activation(head_cols(dst, HI, half, b, group), head_bank(half, g, group),
                                                 ACT.Copy, scale=UNSCALE[which]).then_inc(s_hproj_act, 1)
                    if which == 1:
                        for t in range(T):
                            act.wait_ge(s_vw, a * T + (t + 1))
                            nc.scalar.activation(vw[0:ROWS[t], HI, t, :], bank(6 + t % 2, D, ROWS[t]),
                                                 ACT.Copy, scale=1 / W_SCALE).then_inc(s_vw_act, 1)
                for t in range(T + 1):
                    if t < T:
                        r = ROWS[t]
                        act.wait_ge(s_neg, a * T + (t + 1))
                        nc.scalar.activation(att[0:r, t % 2, :], att[0:r, t % 2, :], ACT.Exp,
                                             bias=neg_top[0:r, t:t + 1],
                                             accum_out=total[0:r, t:t + 1]).then_inc(s_hexp, 1)
                    if t:
                        i = t - 1
                        r = ROWS[i]
                        for b_, (rows, k0, k1) in enumerate(PT_PIECES):
                            if b_ < 3:
                                act.wait_ge(s_htr, a * (3 * T) + (3 * i + b_ + 1))
                            nc.scalar.activation(pT2[i % 2][0:rows, HI, k0:k1, 0:r], pt_bank(k0, k1, rows, r),
                                                 ACT.Copy).then_inc(s_hpt_act, 1)

            with act.Fori(0, 2) as g:
                with act.Fori(0, 4) as b:
                    head(g * 4 + b, b)

            norm_rows(4)
            take_hT(4)
            u = 0
            for b, (c0, cw) in enumerate(CHUNKS):
                for k in range(T):
                    if u % 2 == 0:
                        act.wait_ge(s_adj_tr, 33 + u + 1)
                        nc.scalar.activation(adjT3[0:ROWS[k], k, c0:c0 + cw], bank(u % 6, cw, ROWS[k]),
                                             ACT.Copy).then_inc(s_adjT_act, 1)
                    u += 1
            for c, (c0, cw) in enumerate(CHUNKS):
                act.wait_ge(s_left, c + 1)
                nc.scalar.activation(left[:, c0:c0 + cw], bank(c, cw), ACT.Copy).then_inc(s_left_taken, 1)
            for t in range(T):
                act.wait_ge(s_l3proj, t + 1)
                r = ROWS[t]
                nc.scalar.activation(hg[0:r, t, :], bank((4, 6)[t % 2] + 1, 260, r), ACT.Copy).then_inc(s_hg, 1)
            for k in range(T):
                act.wait_ge(s_z, k + 1)
                nc.scalar.activation(edge[0:ROWS[k], k, :], z[0:ROWS[k], k % 2, :], ACT.Exp,
                                     scale=-1.0).then_inc(s_e, 1)
            act.wait_ge(s_conv_taken, T)
            nc.scalar.activation(gate_a, gate_a, ACT.Sigmoid, bias=ba_b)
            nc.scalar.activation(gate_b, gate_b, ACT.Sigmoid, bias=bb_b).then_inc(s_gate, 1)
            for t in range(T):
                r = ROWS[t]
                act.wait_ge(s_mixed, t + 1)
                nc.scalar.activation(conv[0:r, t, :], conv[0:r, t, :], ACT.Sigmoid).then_inc(s_sig, 1)

        @block.vector
        def _(dve):
            chain = [0]

            def link(ins):
                chain[0] += 1
                ins.then_inc(s_dve, 1)
                dve.wait_ge(s_dve, chain[0])

            def norm_stats(n, ready, count):
                dve.wait_ge(ready, count)
                for t in range(T):
                    last = nc.vector.bn_stats(stats[:, t, :], x[:, t, :])
                link(last)
                for t in range(T):
                    last = nc.vector.bn_aggr(mean_var[:, t, :], stats[:, t, :])
                link(last)
                nc.vector.tensor_scalar(var_eps, mean_var[:, :, 1], LN_EPS, None, ALU.add).then_inc(s_ln_var, 1)
                dve.wait_ge(s_ln_std, n + 1)
                link(nc.vector.reciprocal(rstd, std))
                nc.vector.scalar_tensor_tensor(out=nmean, in0=mean_var[:, :, 0], scalar=-1.0, in1=rstd,
                                               op0=ALU.mult, op1=ALU.mult).then_inc(s_ln_coef, 1)

            def take_hT(q):
                for b, (c0, cw) in enumerate(CHUNKS):
                    dve.wait_ge(s_tr, 6 * q + 2 * b + 1)
                    nc.vector.tensor_copy(hT[:, 0, c0:c0 + cw], bank(2 * b, cw)).then_inc(s_hT_dve, 1)

            norm_stats(0, s_x_in, 32)
            take_hT(0)
            u = 0
            for b, (c0, cw) in enumerate(CHUNKS):
                for k in range(T):
                    if u % 2:
                        dve.wait_ge(s_adj_tr, u + 1)
                        nc.vector.tensor_copy(adjT[0:ROWS[k], k, c0:c0 + cw],
                                              bank(u % 8, cw, ROWS[k])).then_inc(s_adjT_dve, 1)
                    u += 1
            dve.wait_ge(s_w_in, 16 * 5)
            link(nc.vector.tensor_scalar(one_minus_ts, ts, -1.0, 1.0, ALU.mult, ALU.add))
            dve.wait_ge(s_sup_taken, T)
            for t in range(T):
                r = ROWS[t]
                last = nc.vector.scalar_tensor_tensor(out=x[0:r, t, :], in0=v[0:r, t, :], scalar=one_minus_ts[0:r, :],
                                                      in1=x[0:r, t, :], op0=ALU.mult, op1=ALU.add)
            link(last)
            for t in range(T):
                r = ROWS[t]
                dve.wait_ge(s_mix0, t + 1)
                nc.vector.scalar_tensor_tensor(out=x[0:r, t, :], in0=bank(t % 8, D, r), scalar=ts[0:r, :],
                                               in1=x[0:r, t, :], op0=ALU.mult, op1=ALU.add).then_inc(s_x0, 1)
            norm_stats(1, s_x0, T)

            dve.wait_ge(s_sums, 2 * T)
            for sums in (row_sum, col_sum):
                last = nc.vector.tensor_scalar(sums, sums, 1.0, 1e-12, ALU.add, ALU.max)
            link(last)
            nc.vector.reciprocal(row_inv, row_sum)
            nc.vector.reciprocal(col_inv, col_sum).then_inc(s_inv, 1)
            for k in range(T):
                r = ROWS[k]
                dst = adjT[0:r, k, k * P:k * P + r]
                last = nc.vector.tensor_tensor(dst, dst, ident[0:r, 0:r], ALU.add)
            last.then_inc(s_s_ready, 1)
            take_hT(1)

            def tops(s):
                for t in range(T):
                    r = ROWS[t]
                    dve.wait_ge(s_logit, T * s + t + 1)
                    b0 = 3 * (t % 2) * BANK
                    link(nc.vector.reduce_max(top[0:r, t:t + 1], psum[0:r, b0:b0 + N], AX_X))
                    nc.vector.tensor_scalar(neg_top[0:r, t:t + 1], top[0:r, t:t + 1], -1.0, None,
                                            ALU.mult).then_inc(s_top, 1)

            def halve(s, first, count, done):
                with dve.Fori(0, count) as i:
                    base = i * (T + 5)
                    nc.vector.tensor_copy(step_now, steps[:, bass.ds(i + first, 1)]).then_inc(done, 1)
                    dve.wait_ge(done, base + 1)
                    nc.vector.scalar_tensor_tensor(out=cand, in0=low, scalar=step_now, in1=low,
                                                   op0=ALU.mult, op1=ALU.add).then_inc(done, 1)
                    dve.wait_ge(done, base + 2)
                    for t in range(T):
                        r = ROWS[t]
                        if t >= 2:
                            dve.wait_ge(done, base + (t + 1))
                        nc.vector.scalar_tensor_tensor(
                            out=(junk, junk_a)[t % 2][0:r, :], in0=rows_b[0:r, t, :], scalar=cand[0:r, t:t + 1],
                            in1=rows_b[0:r, t, :], op0=ALU.is_gt, op1=ALU.mult,
                            accum_out=mass[0:r, t:t + 1]).then_inc(done, 1)
                    dve.wait_ge(done, base + (T + 2))
                    nc.vector.tensor_tensor(good, mass, goal, ALU.is_ge).then_inc(done, 1)
                    dve.wait_ge(done, base + (T + 3))
                    nc.vector.tensor_tensor(good, good, cand, ALU.mult).then_inc(done, 1)
                    dve.wait_ge(done, base + (T + 4))
                    nc.vector.tensor_tensor(low, low, good, ALU.max).then_inc(done, 1)
                    dve.wait_ge(done, base + (T + 5))

            def threshold(halvings, done):
                n = [0]

                def then(ins):
                    n[0] += 1
                    ins.then_inc(done, 1)
                    dve.wait_ge(done, n[0])

                ratio = float(np.exp(SPAN / 2.0 ** halvings) * (1 + 2e-6))
                then(nc.vector.tensor_scalar(cand, low, ratio, None, ALU.mult))
                for t in range(T):
                    r = ROWS[t]
                    part = (junk, junk_a)[t % 2]
                    then(nc.vector.scalar_tensor_tensor(
                        out=part[0:r, :], in0=rows_b[0:r, t, :], scalar=cand[0:r, t:t + 1], in1=rows_b[0:r, t, :],
                        op0=ALU.is_le, op1=ALU.mult, accum_out=mass[0:r, t:t + 1]))
                    then(nc.vector.max(top8[0:r, t, :], part[0:r, :]))
                then(nc.vector.tensor_tensor(above, total, mass, ALU.subtract))
                then(nc.vector.tensor_tensor(sum8[:, :, 0], above, top8[:, :, 0], ALU.add))
                for j in range(1, 8):
                    then(nc.vector.tensor_tensor(sum8[:, :, j], sum8[:, :, j - 1], top8[:, :, j], ALU.add))
                wide = [P, T, 8]
                then(nc.vector.tensor_tensor(sum8, sum8, goal.unsqueeze(2).broadcast_to(wide), ALU.is_ge))
                then(nc.vector.tensor_tensor(sum8, sum8, top8, ALU.mult))
                then(nc.vector.reduce_max(cut, sum8, AX_X))
                then(nc.vector.tensor_tensor(cut, cut, top8[:, :, 7], ALU.max))
                then(nc.vector.tensor_tensor(sum8, top8, cut.unsqueeze(2).broadcast_to(wide), ALU.is_gt))
                then(nc.vector.tensor_tensor(sum8, sum8, top8, ALU.mult))
                then(nc.vector.reduce_sum(good, sum8, AX_X))
                then(nc.vector.tensor_tensor(quota, goal, above, ALU.subtract))
                then(nc.vector.tensor_tensor(quota, quota, good, ALU.subtract))
                then(nc.vector.tensor_tensor(quota, quota, cut, ALU.add))

            def search(s):
                dve.wait_ge(s_exp, T * (s + 1))
                link(nc.vector.tensor_scalar(goal, total, P_NUC, None, ALU.mult))
                link(nc.vector.memset(low, float(np.exp(-SPAN))))
                halve(s, 0, FAST[s], s_halve[s])
                threshold(FAST[s], s_cut[s])
                for t in range(T):
                    r = ROWS[t]
                    last = nc.vector.scalar_tensor_tensor(
                        out=(junk, junk_a)[t % 2][0:r, :], in0=rows_b[0:r, t, :], scalar=cut[0:r, t:t + 1],
                        in1=rows_b[0:r, t, :], op0=ALU.is_ge, op1=ALU.mult, accum_out=down_to[0:r, t:t + 1])
                    link(last)
                link(nc.vector.tensor_scalar(good, goal, 1 - 1e-6, None, ALU.mult))
                link(nc.vector.tensor_tensor(good, down_to, good, ALU.is_lt))
                link(nc.vector.reduce_max(flags[:, 0:1], good, AX_X))
                link(nc.vector.tensor_tensor(good, goal, cut, ALU.add))
                link(nc.vector.tensor_tensor(good, down_to, good, ALU.is_ge))
                nc.vector.reduce_max(flags[:, 1:2], good, AX_X).then_inc(s_flags, 1)
                dve.wait_ge(s_flags_all, s + 1)
                link(nc.vector.tensor_copy(flags_int, flags_all))
                lower = dve.value_load(flags_int[0:1, 0:1], min_val=0, max_val=1)
                tied = dve.value_load(flags_int[0:1, 1:2], min_val=0, max_val=1)
                with dve.If(lower > 0):
                    halve(s, FAST[s], SEARCH - FAST[s], s_halve_on[s])
                    threshold(SEARCH, s_cut_on[s])
                with dve.If(lower + tied > 0):
                    n = [0]

                    def then(ins):
                        n[0] += 1
                        ins.then_inc(s_tied[s], 1)
                        dve.wait_ge(s_tied[s], n[0])

                    for t in range(T):
                        r = ROWS[t]
                        row = rows_b[0:r, t, :]
                        then(nc.vector.tensor_scalar(junk[0:r, :], row, cut[0:r, t:t + 1], cut[0:r, t:t + 1],
                                                     ALU.is_equal, ALU.mult))
                        then(nc.vector.tensor_tensor_scan(junk_a[0:r, :], ones_row[0:r, :].broadcast_to([r, N]),
                                                          junk[0:r, :], 0.0, ALU.mult, ALU.add))
                        then(nc.vector.scalar_tensor_tensor(
                            out=junk[0:r, :], in0=junk_a[0:r, :], scalar=quota[0:r, t:t + 1], in1=junk[0:r, :],
                            op0=ALU.is_ge, op1=ALU.mult))
                        then(nc.vector.tensor_tensor(row, row, junk[0:r, :], ALU.subtract))

            def attention(s):
                def keep(t):
                    r = ROWS[t]
                    nc.vector.scalar_tensor_tensor(
                        out=rows_b[0:r, t, :], in0=rows_b[0:r, t, :], scalar=cut[0:r, t:t + 1], in1=rows_b[0:r, t, :],
                        op0=ALU.is_ge, op1=ALU.mult, accum_out=kept[0:r, t:t + 1]).then_inc(s_a_rows, 1)
                    dve.wait_ge(s_a_rows, T * s + t + 1)
                    nc.vector.reciprocal(kept_inv[0:r, t:t + 1], kept[0:r, t:t + 1]).then_inc(s_kept_inv, 1)

                keep(0)
                for t in range(T):
                    if t + 1 < T:
                        keep(t + 1)
                    r = ROWS[t]
                    i = T * s + t
                    b0 = 3 * (t % 2)
                    dve.wait_ge(s_a_tr, 3 * i + 2)
                    nc.vector.tensor_copy(pT[:, t % 2, 4:8, 0:r],
                                          bank(b0 + 1).rearrange("p (k n) -> p k n", n=P)[:, :, 0:r]
                                          ).then_inc(s_pt_dve, 1)

            tops(0)
            search(0)
            attention(0)
            take_hT(2)
            tops(1)
            search(1)
            attention(1)
            norm_stats(2, s_y_add, 6 * T)
            dve.wait_ge(s_ln_coef, 3)
            for t in range(T):
                last = nc.vector.tensor_scalar(x[:, t, :], x[:, t, :], rstd[:, t:t + 1], nmean[:, t:t + 1],
                                               ALU.mult, ALU.add)
            link(last)
            dve.wait_ge(s_gb_in, 32)
            for t in range(T):
                r = ROWS[t]
                last = nc.vector.tensor_tensor(x[0:r, t, :], x[0:r, t, :], gamma_b[0:r, :], ALU.mult)
            link(last)
            dve.wait_ge(s_y_add, 7 * T)
            for t in range(T):
                r = ROWS[t]
                nc.vector.tensor_tensor(x[0:r, t, :], x[0:r, t, :], h[0:r, t, :], ALU.add).then_inc(s_x_final, 1)

            norm_stats(3, s_x_final, T)
            for b, (c0, cw) in enumerate(CHUNKS):
                for kd in range(KD):
                    dve.wait_ge(s_hT_act, 9 + 2 * b + kd + 1)
                    nc.vector.tensor_tensor(hT2[:, LO, kd, c0:c0 + cw], bank(2 * b + kd, cw),
                                            hT2[:, HI, kd, c0:c0 + cw], ALU.subtract).then_inc(s_hT_dve, 1)
            for u in range(6):
                w = (wv, wk, wq)[u // KD]
                dve.wait_ge(s_w_hi, u + 1)
                nc.vector.scalar_tensor_tensor(out=w[:, LO, u % KD, :], in0=stage_in[u % 2], scalar=W_SCALE,
                                               in1=w[:, HI, u % KD, :], op0=ALU.mult,
                                               op1=ALU.subtract).then_inc(s_w_lo, 1)

            def head(a, b):
                dve.wait_ge(s_wout_hi, a + 1)
                nc.vector.scalar_tensor_tensor(out=wout[:, LO, :, :], in0=wout_in, scalar=W_SCALE,
                                               in1=wout[:, HI, :, :], op0=ALU.mult,
                                               op1=ALU.subtract).then_inc(s_wout_lo, 1)
                for which, dst in enumerate((vT, kT, qT)):
                    for half in range(KD):
                        for g, group in enumerate(CGROUPS):
                            dve.wait_ge(s_hproj_act, a * 18 + (6 * which + 3 * half + g + 1))
                            nc.vector.scalar_tensor_tensor(
                                out=head_cols(dst, LO, half, b, group), in0=head_bank(half, g, group),
                                scalar=UNSCALE[which], in1=head_cols(dst, HI, half, b, group),
                                op0=ALU.mult, op1=ALU.subtract).then_inc(s_hproj_dve, 1)
                    if which == 1:
                        for t in range(T):
                            dve.wait_ge(s_vw_act, a * T + (t + 1))
                            nc.vector.scalar_tensor_tensor(
                                out=vw[0:ROWS[t], LO, t, :], in0=bank(6 + t % 2, D, ROWS[t]), scalar=1 / W_SCALE,
                                in1=vw[0:ROWS[t], HI, t, :], op0=ALU.mult, op1=ALU.subtract).then_inc(s_vw_dve, 1)
                for t in range(T + 2):
                    if 1 <= t <= T:
                        i = t - 1
                        r = ROWS[i]
                        dve.wait_ge(s_hexp, a * T + (i + 1))
                        nc.vector.reciprocal(kept_inv[0:r, i:i + 1], total[0:r, i:i + 1]).then_inc(s_hinv, 1)
                        nc.vector.scalar_tensor_tensor(out=att[0:r, i % 2, :], in0=bias[0:r, i, :], scalar=MASKED / 2,
                                                       in1=att[0:r, i % 2, :], op0=ALU.is_gt,
                                                       op1=ALU.mult).then_inc(s_masked, 1)
                    if t < T:
                        r = ROWS[t]
                        own_wait(dve, s_qk, a * T + (t + 1), s_dve_passed)
                        nc.vector.tensor_tensor_reduce(out=att[0:r, t % 2, :], in0=psum[0:r, 0:N], in1=bias[0:r, t, :],
                                                       scale=1.0, scalar=-3.0e38, op0=ALU.add, op1=ALU.max,
                                                       accum_out=top[0:r, t:t + 1]).then_inc(s_biased, 1)
                        dve.wait_ge(s_biased, a * T + (t + 1))
                        nc.vector.tensor_scalar(neg_top[0:r, t:t + 1], top[0:r, t:t + 1], -1.0, LOG_P_SCALE,
                                                ALU.mult, ALU.add).then_inc(s_neg, 1)
                    if 1 <= t <= T:
                        i = t - 1
                        r = ROWS[i]
                        for b_, (rows, k0, k1) in enumerate(PT_PIECES):
                            if b_ < 3:
                                dve.wait_ge(s_hpt_act, a * (4 * T) + (4 * i + (1, 2, 4)[b_]))
                            last = nc.vector.tensor_tensor(
                                pT2[i % 2][0:rows, LO, k0:k1, 0:r], pt_bank(k0, k1, rows, r),
                                pT2[i % 2][0:rows, HI, k0:k1, 0:r], ALU.subtract)
                        last.then_inc(s_hpt_dve, 1)
                    if t >= 2:
                        i = t - 2
                        r = ROWS[i]
                        dve.wait_ge(s_pv, a * T + (i + 1))
                        dve.wait_ge(s_hinv, a * T + (i + 1))
                        dve.wait_ge(s_x_add, a * T + (i + 1))
                        nc.vector.scalar_tensor_tensor(out=x[0:r, i, :], in0=bank(6 + i % 2, D, r),
                                                       scalar=kept_inv[0:r, i:i + 1], in1=x[0:r, i, :],
                                                       op0=ALU.mult, op1=ALU.add).then_inc(s_x_add, 1)

            dve.sem_inc(s_x_add, 1)
            dve.sem_inc(s_wout_lo, 1)
            with dve.Fori(0, 2) as g:
                with dve.Fori(0, 4) as b:
                    head(g * 4 + b, b)

            norm_stats(4, s_x_add, 1 + HEADS * T)
            for t in range(T):
                nc.vector.scalar_tensor_tensor(out=bias[0:ROWS[t], t, :], in0=bias[0:ROWS[t], t, :], scalar=MASKED / 2,
                                               in1=bias[0:ROWS[t], t, :], op0=ALU.is_gt,
                                               op1=ALU.mult).then_inc(s_unbias, 1)
            take_hT(4)
            dve.wait_ge(s_l3_in, L3_LOADS)
            for kd in range(KD):
                for a_row, dst in ((a_left, w_left[:, kd:kd + 1]), (a_right, w_s[:, kd, D:D + 1])):
                    link(nc.vector.scalar_tensor_tensor(out=dot_junk, in0=w_s[:, kd, 0:D], scalar=1.0, in1=a_row,
                                                        op0=ALU.mult, op1=ALU.mult, accum_out=dst))
            for kd in range(KD):
                last = nc.vector.tensor_scalar(w_rep[:, kd, :], ident[:, :], 0.0, w_left[:, kd:kd + 1],
                                               ALU.mult, ALU.add)
            last.then_inc(s_l3w, 1)
            u = 0
            for b, (c0, cw) in enumerate(CHUNKS):
                for k in range(T):
                    if u % 2:
                        dve.wait_ge(s_adj_tr, 33 + u + 1)
                        nc.vector.tensor_copy(adjT3[0:ROWS[k], k, c0:c0 + cw],
                                              bank(u % 6, cw, ROWS[k])).then_inc(s_adjT_dve, 1)
                    u += 1
            nc.vector.memset(gate_a, 0.0)
            nc.vector.memset(gate_b, 0.0)
            link(nc.vector.memset(hs[:, :, D], 1.0))
            for t in range(T):
                dve.wait_ge(s_l3proj, t + 1)
                r = ROWS[t]
                b0 = (4, 6)[t % 2]
                nc.vector.tensor_copy(right[0:r, t:t + 1], psum[0:r, b0 * BANK + D:b0 * BANK + D + 1])
                nc.vector.tensor_copy(hs[0:r, t, 0:D], bank(b0, D, r)).then_inc(s_l3proj_taken, 1)
            dve.wait_ge(s_left_taken, 3)
            dve.wait_ge(s_l3proj_taken, T)

            def mask_edge(k):
                r = ROWS[k]
                dve.wait_ge(s_e, k + 1)
                nc.vector.scalar_tensor_tensor(out=edge[0:r, k, :], in0=adjT3[0:r, k, :], scalar=0.0,
                                               in1=edge[0:r, k, :], op0=ALU.not_equal, op1=ALU.mult).then_inc(s_edge, 1)

            for k in range(T):
                r = ROWS[k]
                if k >= 2:
                    dve.wait_ge(s_e, k - 1)
                link(nc.vector.tensor_scalar(z[0:r, k % 2, :], left[0:r, :], right[0:r, k:k + 1], 0.01,
                                             ALU.add, ALU.mult))
                nc.vector.scalar_tensor_tensor(out=z[0:r, k % 2, :], in0=left[0:r, :], scalar=right[0:r, k:k + 1],
                                               in1=z[0:r, k % 2, :], op0=ALU.add, op1=ALU.max).then_inc(s_z, 1)
                if k:
                    mask_edge(k - 1)
                dve.wait_ge(s_conv, k + 1)
                b0 = (k % 2) * BANK
                nc.vector.scalar_tensor_tensor(out=conv[0:r, k, :], in0=bank(k % 2, D, r), scalar=0.5,
                                               in1=bg_b[0:r, :], op0=ALU.mult, op1=ALU.add)
                for j, gate in enumerate((gate_a, gate_b)):
                    last = nc.vector.scalar_tensor_tensor(
                        out=gate[0:r, k:k + 1], in0=psum[0:r, b0 + D + j:b0 + D + j + 1], scalar=0.5,
                        in1=hg[0:r, k, D + 2 + j:D + 3 + j], op0=ALU.mult, op1=ALU.add)
                last.then_inc(s_conv_taken, 1)
            mask_edge(T - 1)
            dve.wait_ge(s_gate, 1)
            for t in range(T):
                r = ROWS[t]
                last = nc.vector.tensor_scalar(conv[0:r, t, :], conv[0:r, t, :], gate_b[0:r, t:t + 1], None, ALU.mult)
            link(last)
            for t in range(T):
                r = ROWS[t]
                dve.wait_ge(s_gat, t + 1)
                s1 = (2 + t % 2) * BANK + D
                link(nc.vector.tensor_scalar(den[0:r, t:t + 1], psum[0:r, s1:s1 + 1], 1e-5, None, ALU.add))
                link(nc.vector.reciprocal(den[0:r, t:t + 1], den[0:r, t:t + 1]))
                link(nc.vector.tensor_tensor(den[0:r, t:t + 1], den[0:r, t:t + 1], gate_a[0:r, t:t + 1], ALU.mult))
                nc.vector.scalar_tensor_tensor(out=conv[0:r, t, :], in0=bank(2 + t % 2, D, r),
                                               scalar=den[0:r, t:t + 1], in1=conv[0:r, t, :],
                                               op0=ALU.mult, op1=ALU.add).then_inc(s_mixed, 1)


_INS = ['x', 'adj', 'L0_gnn_t', 'L0_gnn_weight', 'L1_gnn_W1', 'L1_gnn_W2', 'L1_gnn_W3', 'L1_gnn_U1', 'L1_gnn_U2',
        'L1_gnn_U3', 'L1_gnn_gamma', 'L1_gnn_beta', 'L2_gnn_Wq', 'L2_gnn_Wk', 'L2_gnn_Wv', 'L2_gnn_Wout',
        'L3_gnn_W_sa', 'L3_gnn_a_sa', 'L3_gnn_W_gcnb', 'L3_gnn_b_gcnb', 'L3_gnn_Wa', 'L3_gnn_ba', 'L3_gnn_Wb',
        'L3_gnn_bb']


def kernel(**inputs):
    import numpy as _np
    import concourse.bacc as _bacc
    from concourse import mybir as _mybir
    from concourse.bass_utils import run_bass_kernel_spmd as _run

    nc = _bacc.Bacc("TRN2", target_bir_lowering=False, num_devices=1)
    arrays, args = {}, []
    for name in _INS:
        a = _np.ascontiguousarray(inputs[name])
        arrays[f"in_{name}"] = a
        args.append(nc.dram_tensor(f"in_{name}", a.shape, _mybir.dt.from_np(a.dtype), kind="ExternalInput").ap())
    args.append(nc.dram_tensor("out_x", (N, D), _mybir.dt.float32, kind="ExternalOutput").ap())
    graph_layers(nc, *args)
    r = _run(nc, [arrays], core_ids=[0])
    return r.results[0]["out_x"]
```

```python
import numpy as np
import concourse.bass as bass
from concourse import mybir
from contextlib import ExitStack

N, D, HEADS, D_ATTN, STEPS = 1354, 256, 8, 64, 2
P = 128
T = -(-N // P)
KD = D // P
ROWS = [min(P, N - t * P) for t in range(T)]
BANK = 512
CHUNKS = [(c * BANK, min(BANK, N - c * BANK)) for c in range(-(-N // BANK))]
QUADS = [range(4 * b, min(4 * b + 4, T)) for b in range(len(CHUNKS))]
LN_EPS = 1e-5
P_NUC = 0.9
MASKED = -1e6
SPAN = float(np.log(N / (1 - P_NUC)) + 0.05)
SEARCH = 24
FAST = (8, 10)
FLOOR = (1 - P_NUC) * 0.999 / N
MINE = (T, 7)
HN = (N + HEADS - 2 + HEADS - 1) // HEADS
LEAD = 8
PADDED = LEAD + HN * HEADS + 8
CGROUPS = [range(0, 3), range(3, 6), range(6, 8)]

HI, LO = 0, 1
PASSES = ((HI, HI), (HI, LO), (LO, HI))
W_SCALE = 64.0
LOG_P_SCALE = float(np.log(1024.0))
STAGE = HEADS * D

fp32 = mybir.dt.float32
fp16 = mybir.dt.float16
ALU = mybir.AluOpType
ACT = mybir.ActivationFunctionType
AX_X = mybir.AxisListType.X


def graph_layers(nc, x_in, adj, t_gate, W0, W1, W2, W3, U1, U2, U3, gamma, beta, Wq, Wk, Wv, Wout,
                 W_sa, a_sa, W_g, b_g, Wa, ba, Wb, bb, out):
    ctx = ExitStack()
    with ctx:
        def sb(name, cols):
            return ctx.enter_context(nc.sbuf_tensor(name, [P, cols], fp32))

        def sem(name):
            return ctx.enter_context(nc.semaphore(name))

        slot_a = sb("slot_a", T * N)
        slot_b = sb("slot_b", T * N)
        slot_x = sb("slot_x", T * D)
        slot_h = sb("slot_h", T * 257)
        slot_t = sb("slot_t", KD * N)
        slot_v = sb("slot_v", T * 260)
        slot_k = sb("slot_k", KD * PADDED)
        slot_p = sb("slot_p", 2 * T * P)
        slot_u = sb("slot_u", 12 * D)
        slot_w = sb("slot_w", 1024)
        slot_r = sb("slot_r", 4 * D + 4 * P)
        ident = sb("ident", P)
        small = sb("small", 800)

        tmp = slot_r[:, 0:4 * D]
        ab = slot_r[:, 4 * D:4 * D + 4 * P]
        adjT = slot_a[:, :].rearrange("p (k n) -> p k n", k=T)
        rows_b = slot_b[:, :].rearrange("p (k n) -> p k n", k=T)
        x = slot_x[:, :].rearrange("p (t d) -> p t d", t=T)
        y = x
        h = slot_h[:, 0:T * D].rearrange("p (t d) -> p t d", t=T)
        hT = slot_t[:, :].rearrange("p (k n) -> p k n", k=KD)
        v = slot_v[:, 0:T * D].rearrange("p (t d) -> p t d", t=T)
        pT = slot_p[:, :].rearrange("p (s k n) -> p s k n", s=2, k=T)
        rings = tmp.rearrange("p (r d) -> p r d", r=4)
        qwT = slot_k[0:D_ATTN, 0:N]
        kT1 = slot_k[0:D_ATTN, N:2 * N]
        q1T = slot_p[0:D_ATTN, 0:N]
        junk = slot_p[:, 0:N]
        junk_a = slot_p[:, N:2 * N]
        u1 = slot_u[:, 0:4 * D].rearrange("p (k s d) -> p k s d", k=KD, s=STEPS)
        u2 = slot_u[:, 4 * D:8 * D].rearrange("p (k s d) -> p k s d", k=KD, s=STEPS)
        u3 = slot_u[:, 8 * D:12 * D].rearrange("p (k s d) -> p k s d", k=KD, s=STEPS)
        w0 = slot_w[:, 0:2 * D].rearrange("p (k d) -> p k d", k=KD)
        w1 = slot_w[:, 512:640].rearrange("p (k d) -> p k d", k=KD)
        w3 = slot_w[:, 640:768].rearrange("p (k d) -> p k d", k=KD)
        w2 = slot_w[0:D_ATTN, 768:832]
        gamma_b = ab[:, 0:D]
        beta_b = ab[:, D:2 * D]
        def parts(slot, cols, pattern, **sizes):
            return slot[:, 0:cols].bitcast(fp16).rearrange(pattern, s=2, **sizes)

        def weight(m):
            return parts(slot_b[:, 2 * STAGE * m:2 * STAGE * (m + 1)], 2 * STAGE, "p (s k n) -> p s k n", k=KD)

        wk, wq, wv = (weight(m) for m in range(3))
        stage_in = (slot_u[:, 0:STAGE], slot_b[:, 6 * STAGE:7 * STAGE])
        wout_in = slot_w[:, 0:2 * D].rearrange("p (k d) -> p k d", k=KD)
        wout = parts(slot_w[:, 2 * D:4 * D], 2 * D, "p (s k d) -> p s k d", k=KD)
        bias = adjT
        hT2 = parts(slot_t, KD * N, "p (s k n) -> p s k n", k=KD)
        qT = parts(slot_v, KD * PADDED, "p (s k n) -> p s k n", k=KD)
        vT = parts(slot_p, KD * PADDED, "p (s k n) -> p s k n", k=KD)
        kT = parts(slot_k, KD * PADDED, "p (s k n) -> p s k n", k=KD)
        vw = parts(slot_h, T * D, "p (s t d) -> p s t d", t=T)
        pT2 = [parts(slot_p[:, i * T * P:(i + 1) * T * P], T * P, "p (s k n) -> p s k n", k=T) for i in range(2)]
        att = slot_u[:, 0:2 * N].rearrange("p (s n) -> p s n", s=2)
        att16 = (slot_r[:, 0:N].bitcast(fp16).rearrange("p (s n) -> p s n", s=2),
                 slot_u[:, 0:2 * N].bitcast(fp16).rearrange("p (s n) -> p s n", s=2)[:, :, 0:N])
        ident16 = slot_r[:, N:N + P // 2].bitcast(fp16)
        edge = adjT
        adjT3 = rows_b
        hs = slot_h[:, :].rearrange("p (t d) -> p t d", t=T)
        hg = slot_v[:, :].rearrange("p (t d) -> p t d", t=T)
        w_s = slot_u[:, N:N + 2 * 257].rearrange("p (k d) -> p k d", k=KD)
        w_c = slot_u[:, N + 514:N + 514 + 2 * 260].rearrange("p (k d) -> p k d", k=KD)
        left = slot_u[:, 0:N]
        z = slot_k[:, 0:2 * N].rearrange("p (s n) -> p s n", s=2)
        a_left = slot_w[:, 0:D]
        a_right = slot_w[:, D:2 * D]
        bg_b = slot_w[:, 2 * D:3 * D]
        dot_junk = slot_w[:, 3 * D:4 * D]
        w_rep = ab[:, 0:2 * P].rearrange("p (k d) -> p k d", k=KD)
        conv = slot_p[:, 0:T * D].rearrange("p (t d) -> p t d", t=T)

        at = [0]

        def table(cols):
            at[0] += cols
            return small[:, at[0] - cols:at[0]]

        stats = table(6 * T).rearrange("p (t s) -> p t s", t=T)
        mean_var = table(2 * T).rearrange("p (t s) -> p t s", t=T)
        var_eps, std, rstd, nmean = table(T), table(T), table(T), table(T)
        row_sum, col_sum, row_inv, col_inv = table(T), table(T), table(T), table(T)
        top, neg_top, total, goal, low, cand, mass, good = (table(T) for _ in range(8))
        kept, kept_inv, above, cut, quota, down_to = (table(T) for _ in range(6))
        top8, sum8 = (table(8 * T).rearrange("p (t s) -> p t s", t=T) for _ in range(2))
        ratios, span0, neg_cand, signs, excess = table(max(FAST) * T), table(T), table(T), table(T), table(T)
        ones_row, flags, flags_all = table(1), table(2), table(2)
        flags_int = table(2).bitcast(mybir.dt.int32)
        steps = table(SEARCH)
        step_now = table(1)
        ts, one_minus_ts = table(1), table(1)
        right, gate_a, gate_b, den = table(T), table(T), table(T), table(T)
        ba_b, bb_b, w_left = table(1), table(1), table(KD)

        psum = ctx.enter_context(nc.psum_tensor("psum", [P, 8 * BANK], fp32))

        def bank(b, w=BANK, rows=P):
            return psum[0:rows, b * BANK:b * BANK + w]

        UNSCALE = (1 / W_SCALE, D ** -0.5 / W_SCALE, 1 / W_SCALE)

        PT8 = 2 * BANK // P

        def pt_bank(b, tiles=PT8):
            return bank(b).bitcast(fp16)[:, 0:tiles * P].rearrange("p (k n) -> p k n", n=P)

        pt_rest = pt_bank(4, 2 * (T - PT8)).rearrange("p (s k) n -> p s k n", s=2)

        def own_wait(engine, signal, value, passed):
            engine.wait_ge(signal, value)
            engine.sem_inc(passed, 1)

        def head_bank(half, g, group):
            return psum[:, (3 * half + g) * BANK:(3 * half + g) * BANK + len(group) * HN].rearrange(
                "p (c i) -> p c i", i=HN)

        def head_cols(dst, part, half, b, group):
            start = b * -2 + (LEAD + group[0])
            run = dst[:, part, half, bass.ds(start, HN * HEADS)].rearrange("p (i c) -> p c i", c=HEADS)
            return run[:, 0:len(group), :]

        y_dram = nc.dram_tensor("x_after_layer_0", (N, D), fp32, kind="Internal").ap()

        s_x_pad, s_x_in, s_w_in, s_ident, s_ones = (sem(n) for n in ("x_pad", "x_in", "w_in", "ident", "ones"))
        s_adj_in = [sem(f"adj_in{b}") for b in range(3)]
        s_u_in, s_gb_in, s_x_out, s_x_back, s_adj_again = (
            sem(n) for n in ("u_in", "gamma_beta_in", "x_spilled", "x_back", "adj_again"))
        s_stage = [sem("stage_in0"), sem("stage_in1")]
        s_w_hi, s_w_lo, s_wout_hi, s_wout_lo = (sem(n) for n in ("w_hi", "w_lo", "wout_hi", "wout_lo"))
        s_wout, s_l3_in, s_out = (sem(n) for n in ("wout_in", "layer3_in", "out"))
        s_ln_var, s_ln_std, s_ln_coef, s_h_rows = (sem(n) for n in ("ln_var", "ln_std", "ln_coef", "h_rows"))
        s_tr, s_hT_dve, s_hT_act = (sem(n) for n in ("transposed", "hT_dve", "hT_act"))
        s_adj_tr, s_adjT_dve, s_adjT_act = (sem(n) for n in ("adj_tr", "adjT_dve", "adjT_act"))
        s_sup, s_sup_taken, s_mix0, s_x0 = (sem(n) for n in ("support", "support_taken", "layer0_product", "x0"))
        s_sums, s_inv, s_s_ready = (sem(n) for n in ("sums", "inv", "s_ready"))
        s_proj, s_proj_taken = sem("l1_proj"), sem("l1_proj_taken")
        s_logit, s_top, s_exp = sem("logits"), sem("top"), sem("exp")
        s_a_rows, s_kept_inv = sem("a_rows"), sem("kept_inv")
        s_a_tr, s_pt_act, s_pt_dve = sem("a_transposed"), sem("pT_act"), sem("pT_dve")
        s_step, s_step_taken = sem("l1_step"), sem("l1_step_taken")
        s_part, s_y_add = sem("y_part"), sem("y_added")
        s_bias = sem("bias")
        s_hproj, s_hproj_dve, s_hproj_act = sem("head_proj"), sem("head_proj_lo"), sem("head_proj_hi")
        s_vw, s_vw_act, s_vw_dve = sem("vw"), sem("vw_act"), sem("vw_dve")
        s_qk, s_biased, s_neg, s_hexp, s_masked = (
            sem(n) for n in ("qk", "biased", "neg_max", "head_exp", "masked"))
        s_htr, s_hpt_act, s_hpt_dve = sem("head_tr"), sem("head_pT_act"), sem("head_pT_dve")
        s_hinv, s_pv, s_x_add = sem("head_inv"), sem("pv"), sem("x_added")
        s_unbias, s_l3w, s_l3proj, s_l3proj_taken = sem("unbiased"), sem("l3_w"), sem("l3_proj"), sem("l3_proj_taken")
        s_left, s_left_taken = sem("left"), sem("left_taken")
        s_z, s_e, s_edge = sem("z"), sem("edge_exp"), sem("edge")
        s_conv, s_conv_taken, s_gate = sem("conv"), sem("conv_taken"), sem("gate")
        s_gat, s_mixed, s_sig, s_done = sem("gat"), sem("mixed"), sem("sigmoid"), sem("done")
        s_dve, s_act_passed, s_pool = sem("dve_chain"), sem("act_passed"), sem("pool_chain")
        s_halve, s_cut, s_halve_on, s_cut_on, s_tied = (
            [sem(f"{n}_step{i}") for i in range(STEPS)] for n in ("halve", "cut", "halve_on", "cut_on", "tied"))
        s_span, s_ratio, s_cand, s_excess = sem("span"), sem("ratio"), sem("cand"), sem("excess")
        s_flags, s_flags_all = sem("flags"), sem("flags_all")
        s_x_final, s_hg, s_dve_passed, s_pool_passed = (sem(n) for n in ("x_final", "hg", "dve_passed", "pool_passed"))
        s_att_hi, s_att_lo, s_ident16 = sem("attention_hi"), sem("attention_lo"), sem("ident16")

        block = ctx.enter_context(nc.Block())

        def rows_of(dram, t0, t1):
            return dram[t0 * P:t1 * P, :].rearrange("(t p) d -> p t d", p=P)

        def col_tiles(w):
            return w.rearrange("(k p) d -> p k d", p=P)

        TL, RL = T - 1, ROWS[-1]

        DIFFUSED = 6 + 4 * T
        L3_LOADS = 16 * (2 + 4 * KD + 5)
        KEEP, PART, BOTH = range(3)
        kinds = [KEEP] * 6 + ([BOTH] * T + [PART] * T) * 2 + [KEEP] * T + [BOTH] * T + [PART] * T

        def step_freed(n):
            if kinds[n] == PART:
                return s_part, sum(k != KEEP for k in kinds[:n + 1])
            return s_step_taken, sum(k != PART for k in kinds[:n + 1])


        @block.sync
        def _(sp):
            sp.dma_start(x[:, 0:TL, :], rows_of(x_in, 0, TL)).then_inc(s_x_in, 16)
            sp.wait_ge(s_x_pad, 1)
            sp.dma_start(x[0:RL, TL, :], x_in[TL * P:N, :]).then_inc(s_x_in, 16)
            sp.dma_start(w0, col_tiles(W0)).then_inc(s_w_in, 16)
            for b, quad in enumerate(QUADS):
                full = [t for t in quad if t < TL]
                sp.dma_start(rows_b[:, full[0]:full[-1] + 1, :],
                             rows_of(adj, full[0], full[-1] + 1)).then_inc(s_adj_in[b], 16)
            sp.dma_start(rows_b[0:RL, TL, :], adj[TL * P:N, :]).then_inc(s_adj_in[2], 16)
            sp.dma_start(ts, t_gate.partition_broadcast(P)).then_inc(s_w_in, 16)
            sp.dma_start(w1, col_tiles(W1)).then_inc(s_w_in, 16)
            sp.dma_start(w3, col_tiles(W3)).then_inc(s_w_in, 16)
            sp.dma_start(w2, W2).then_inc(s_w_in, 16)
            for u, src in ((u1, U1), (u2, U2), (u3, U3)):
                for s in range(STEPS):
                    sp.dma_start(u[:, :, s, :], col_tiles(src[s, :, :])).then_inc(s_u_in, 16)
            sp.dma_start(gamma_b, gamma.partition_broadcast(P)).then_inc(s_gb_in, 16)
            sp.dma_start(beta_b, beta.partition_broadcast(P)).then_inc(s_gb_in, 16)
            sp.wait_ge(s_x0, T)
            sp.dma_start(rows_of(y_dram, 0, TL), x[:, 0:TL, :]).then_inc(s_x_out, 16)
            sp.dma_start(y_dram[TL * P:N, :], x[0:RL, TL, :]).then_inc(s_x_out, 16)
            sp.wait_ge(s_step, DIFFUSED)
            sp.dma_start(adjT[:, 0:TL, :], rows_of(adj, 0, TL)).then_inc(s_adj_again, 16)
            sp.dma_start(adjT[0:RL, TL, :], adj[TL * P:N, :]).then_inc(s_adj_again, 16)
            sp.wait_ge(s_x_out, 32)
            sp.wait_ge(s_step, DIFFUSED + T)
            sp.wait_ge(s_y_add, T)
            sp.dma_start(h[:, 0:TL, :], rows_of(y_dram, 0, TL)).then_inc(s_x_back, 16)
            sp.dma_start(h[0:RL, TL, :], y_dram[TL * P:N, :]).then_inc(s_x_back, 16)
            for u in range(6):
                if u == 0:
                    sp.wait_ge(s_step, DIFFUSED)
                elif u == 1:
                    sp.wait_ge(s_a_tr, 2 * 3 * T)
                else:
                    sp.wait_ge(s_w_lo, u - 1)
                w = (Wk, Wq, Wv)[u // KD]
                sp.dma_start(stage_in[u % 2], w[(u % KD) * P:(u % KD + 1) * P, :]).then_inc(s_stage[u % 2], 16)
            with sp.Fori(0, HEADS) as a:
                sp.wait_ge(s_wout_lo, a + 1)
                sp.dma_start(wout_in, Wout[bass.ds(a * D, D), :].rearrange("(k p) d -> p k d", p=P)).then_inc(s_wout, 16)
            sp.wait_ge(s_x_add, 1 + HEADS * T)
            sp.dma_start(w_s[:, :, 0:D], col_tiles(W_sa)).then_inc(s_l3_in, 16)
            sp.dma_start(w_c[:, :, 0:D], col_tiles(W_g)).then_inc(s_l3_in, 16)
            for j, (w, half) in enumerate(((Wa, 0), (Wb, 0), (Wa, 1), (Wb, 1))):
                src = w[0, half * D:(half + 1) * D].rearrange("(k p a) -> p k a", p=P, a=1)
                for kd in range(KD):
                    sp.dma_start(w_c[:, kd, D + j:D + j + 1], src[:, kd, :]).then_inc(s_l3_in, 16)
            sp.dma_start(a_left, a_sa[0, 0:D].partition_broadcast(P)).then_inc(s_l3_in, 16)
            sp.dma_start(a_right, a_sa[0, D:2 * D].partition_broadcast(P)).then_inc(s_l3_in, 16)
            sp.dma_start(bg_b, b_g.partition_broadcast(P)).then_inc(s_l3_in, 16)
            sp.dma_start(ba_b, ba.partition_broadcast(P)).then_inc(s_l3_in, 16)
            sp.dma_start(bb_b, bb.partition_broadcast(P)).then_inc(s_l3_in, 16)
            for t in range(T):
                sp.wait_ge(s_done, t + 1)
                sp.dma_start(out[t * P:t * P + ROWS[t], :], x[0:ROWS[t], t, :]).then_inc(s_out, 16)
            sp.wait_ge(s_out, 16 * T)

        @block.gpsimd
        def _(pool):
            chain = [0]

            def link(ins):
                chain[0] += 1
                ins.then_inc(s_pool, 1)
                pool.wait_ge(s_pool, chain[0])

            nc.gpsimd.memset(x[:, TL, :], 0.0).then_inc(s_x_pad, 1)
            link(nc.gpsimd.memset(ident[:, :], 0.0))
            nc.gpsimd.affine_select(out=ident[:, :], in_=ident[:, :], compare_op=ALU.not_equal, fill=1.0, base=0,
                                    pattern=[[-1, P]], channel_multiplier=1).then_inc(s_ident, 1)
            for table_, value in ((row_sum, 1.0), (col_sum, 1.0), (total, 1.0), (mass, 0.0), (kept, 1.0),
                                  (ones_row, 1.0), (top8, 1.0), (down_to, 1.0),
                                  (signs, 0.0), (excess, 0.0)):
                nc.gpsimd.memset(table_, value)
            for i in range(SEARCH):
                last = nc.gpsimd.memset(steps[:, i:i + 1], float(np.expm1(SPAN / 2.0 ** (i + 1))))
            last.then_inc(s_ones, 1)

            def any_row(s):
                pool.wait_ge(s_flags, s + 1)
                nc.gpsimd.partition_all_reduce(flags_all, flags, P, bass.bass_isa.ReduceOp.max).then_inc(s_flags_all, 1)

            pool.wait_ge(s_x_out, 32)
            n = 0
            for stage in range(6):
                for t in range(T):
                    pool.wait_ge(s_part, n + 1)
                    if stage:
                        pool.wait_ge(s_y_add, n - T + 1)
                    nc.gpsimd.tensor_tensor(y[0:ROWS[t], t, :], (y if stage else h)[0:ROWS[t], t, :],
                                            rings[0:ROWS[t], n % 4, :], ALU.add).then_inc(s_y_add, 1)
                    n += 1
                if stage == 3:
                    any_row(0)
                if stage == 4:
                    pool.wait_ge(s_y_add, n)
                    pool.wait_ge(s_adj_again, 32)
                    for k in range(T):
                        r = ROWS[k]
                        for c, w in CHUNKS:
                            part = adjT[0:r, k, c:c + w]
                            hole = tmp[0:r, 2 * D:2 * D + w]
                            link(nc.gpsimd.tensor_scalar(hole, part, 0.0, MASKED, ALU.is_equal, ALU.mult))
                            link(nc.gpsimd.tensor_tensor(part, part, part, ALU.add))
                            link(nc.gpsimd.tensor_tensor(part, part, hole, ALU.add))
                    pool.sem_inc(s_bias, 1)
                    any_row(1)
            pool.wait_ge(s_x_back, 32)
            pool.wait_ge(s_gb_in, 32)
            for t in range(T):
                nc.gpsimd.tensor_tensor(h[0:ROWS[t], t, :], h[0:ROWS[t], t, :], beta_b[0:ROWS[t], :],
                                        ALU.add).then_inc(s_y_add, 1)

            def head(a):
                for t in range(T):
                    r = ROWS[t]
                    own_wait(pool, s_att_hi, a * T + (t + 1), s_pool_passed)
                    nc.gpsimd.tensor_tensor(att16[LO][0:r, t % 2, :], att[0:r, t % 2, :], att16[HI][0:r, t % 2, :],
                                            ALU.subtract).then_inc(s_att_lo, 1)

            with pool.Fori(0, HEADS) as a:
                head(a)

            for t in range(T):
                r = ROWS[t]
                pool.wait_ge(s_sig, t + 1)
                nc.gpsimd.tensor_tensor(x[0:r, t, :], x[0:r, t, :], conv[0:r, t, :], ALU.add).then_inc(s_done, 1)

        @block.tensor
        def _(pe):
            def transpose_rows(q, src, ready, base):
                for b, quad in enumerate(QUADS):
                    pe.wait_ge(ready, base + quad[-1] + 1)
                    for kd in range(KD):
                        for i, t in enumerate(quad):
                            last = nc.tensor.transpose(bank(2 * b + kd)[:, i * P:i * P + ROWS[t]],
                                                       src[0:ROWS[t], t, kd * P:(kd + 1) * P],
                                                       ident[0:ROWS[t], 0:ROWS[t]])
                        last.then_inc(s_tr, 1)

            def wait_hT(q):
                pe.wait_ge(s_hT_dve, 3 * (q + 1) + (3 if q > 3 else 0))
                pe.wait_ge(s_hT_act, 3 * (q + 1) + (3 if q > 3 else 0))

            def times_adjT(dst, rhs, t, lhs=adjT):
                for k in range(T):
                    last = nc.tensor.matmul(dst, lhs[0:ROWS[k], k, t * P:t * P + ROWS[t]], rhs[0:ROWS[k], k, :],
                                            start=(k == 0), stop=(k == T - 1))
                return last

            def times_hT(dst, w, t):
                for kd in range(KD):
                    last = nc.tensor.matmul(dst, hT[:, kd, t * P:t * P + ROWS[t]], w[:, kd, :],
                                            start=(kd == 0), stop=(kd == KD - 1))
                return last

            pe.wait_ge(s_ident, 1)
            transpose_rows(0, h, s_h_rows, 0)
            wait_hT(0)
            u = 0
            for b, quad in enumerate(QUADS):
                pe.wait_ge(s_adj_in[b], 16 if b < 2 else 32)
                for k in range(T):
                    if u >= 8:
                        pe.wait_ge(s_adjT_act if u % 2 == 0 else s_adjT_dve, (u - 8) // 2 + 1)
                    for i, t in enumerate(quad):
                        last = nc.tensor.transpose(bank(u % 8)[0:ROWS[k], i * P:i * P + ROWS[t]],
                                                   rows_b[0:ROWS[t], t, k * P:k * P + ROWS[k]],
                                                   ident[0:ROWS[t], 0:ROWS[t]])
                    last.then_inc(s_adj_tr, 1)
                    u += 1
            pe.wait_ge(s_adjT_act, 17)
            pe.wait_ge(s_adjT_dve, 16)
            pe.wait_ge(s_w_in, 16 * 5)
            for t in range(T):
                if t >= 8:
                    pe.wait_ge(s_sup_taken, t - 7)
                times_hT(bank(t % 8, D, ROWS[t]), w0, t).then_inc(s_sup, 1)
            pe.wait_ge(s_sup_taken, T)
            for t in range(T):
                if t >= 8:
                    pe.wait_ge(s_x0, t - 7)
                times_adjT(bank(t % 8, D, ROWS[t]), v, t).then_inc(s_mix0, 1)

            pe.wait_ge(s_x0, T)
            transpose_rows(1, h, s_h_rows, T)

            def project_qk(s):
                wait_hT(1 + s)
                for first, w in ((0, w1), (3, w3)):
                    for c, (c0, cw) in enumerate(CHUNKS):
                        for kd in range(KD):
                            last = nc.tensor.matmul(bank(first + c, cw, D_ATTN), w[:, kd, :], hT[:, kd, c0:c0 + cw],
                                                    start=(kd == 0), stop=(kd == KD - 1))
                        last.then_inc(s_proj, 1)
                for c, (c0, cw) in enumerate(CHUNKS):
                    pe.wait_ge(s_proj_taken, 9 * s + c + 1)
                    nc.tensor.matmul(bank(c, cw, D_ATTN), w2, q1T[:, c0:c0 + cw],
                                     start=True, stop=True).then_inc(s_proj, 1)

            def logits(s):
                pe.wait_ge(s_proj_taken, 9 * (s + 1))
                for t in range(T):
                    i = T * s + t
                    if t >= 2:
                        pe.wait_ge(s_exp, i - 1)
                    for c, (c0, cw) in enumerate(CHUNKS):
                        last = nc.tensor.matmul(bank(3 * (t % 2) + c, cw, ROWS[t]), qwT[:, t * P:t * P + ROWS[t]],
                                                kT1[:, c0:c0 + cw], start=True, stop=True)
                    last.then_inc(s_logit, 1)

            steps_made = [0]

            def step_done(last):
                last.then_inc(s_step, 1)
                steps_made[0] += 1

            def step_bank():
                if steps_made[0] >= 2:
                    pe.wait_ge(*step_freed(steps_made[0] - 2))
                return 6 + steps_made[0] % 2

            def attention_step(s, rhs):
                def product(t):
                    i = T * s + t
                    pe.wait_ge(s_pt_act, i + 1)
                    pe.wait_ge(s_pt_dve, i + 1)
                    dst = bank(step_bank(), D, ROWS[t])
                    for k in range(T):
                        last = nc.tensor.matmul(dst, pT[0:ROWS[k], t % 2, k, 0:ROWS[t]], rhs[0:ROWS[k], k, :],
                                                start=(k == 0), stop=(k == T - 1))
                    step_done(last)

                for t in range(T):
                    pe.wait_ge(s_a_rows, T * s + t + 1)
                    for b, quad in enumerate(QUADS):
                        for i, k in enumerate(quad):
                            last = nc.tensor.transpose(
                                bank(3 * (t % 2) + b)[0:ROWS[k], i * P:i * P + ROWS[t]],
                                rows_b[0:ROWS[t], t, k * P:k * P + ROWS[k]], ident[0:ROWS[t], 0:ROWS[t]])
                        last.then_inc(s_a_tr, 1)
                    if t:
                        product(t - 1)
                product(T - 1)

            project_qk(0)
            logits(0)
            pe.wait_ge(s_s_ready, 1)
            for kd in range(KD):
                for c0, cw in CHUNKS:
                    dst = bank(step_bank(), cw)
                    for k in range(T):
                        last = nc.tensor.matmul(dst, h[0:ROWS[k], k, kd * P:(kd + 1) * P],
                                                adjT[0:ROWS[k], k, c0:c0 + cw], start=(k == 0), stop=(k == T - 1))
                    step_done(last)
            pe.wait_ge(s_step_taken, 6)
            pe.wait_ge(s_u_in, 16 * 6)
            for u in (u1, u2):
                for t in range(T):
                    step_done(times_hT(bank(step_bank(), 2 * D, ROWS[t]), u.rearrange("p k s d -> p k (s d)"), t))
                pe.wait_ge(*step_freed(steps_made[0] - 1))
                for t in range(T):
                    step_done(times_adjT(bank(step_bank(), D, ROWS[t]), v, t))
            attention_step(0, h)
            transpose_rows(2, v, s_step_taken, DIFFUSED - 2 * T)
            wait_hT(2)
            for t in range(T):
                step_done(times_hT(bank(step_bank(), 2 * D, ROWS[t]), u3.rearrange("p k s d -> p k (s d)"), t))
            project_qk(1)
            logits(1)
            attention_step(1, v)

            transpose_rows(3, h, s_h_rows, 2 * T)
            pe.wait_ge(s_hT_dve, 15)
            pe.wait_ge(s_bias, 1)
            pe.wait_ge(s_ident16, 1)

            def split_product(dst, pieces, last_of=None):
                for n, (lhs, rhs) in enumerate(pieces):
                    for m, (pl, pr) in enumerate(PASSES):
                        last = nc.tensor.matmul(dst, lhs(pl), rhs(pr), start=(n == 0 and m == 0),
                                                stop=(n == len(pieces) - 1 and m == len(PASSES) - 1))
                return last

            def head(a, base):
                def project(which, w):
                    pe.wait_ge(s_w_lo, KD * (which + 1))
                    for half in range(KD):
                        for g, group in enumerate(CGROUPS):
                            if which:
                                pe.wait_ge(s_hproj_dve, a * 18 + (6 * (which - 1) + 3 * half + g + 1))
                            for i, c in enumerate(group):
                                c0 = c * D + half * P
                                last = split_product(
                                    bank(3 * half + g)[:, i * HN:(i + 1) * HN],
                                    [(lambda p, kd=kd: w[:, p, kd, c0:c0 + P],
                                      lambda p, kd=kd: hT2[:, p, kd, bass.ds(base, HN)]) for kd in range(KD)])
                            last.then_inc(s_hproj, 1)

                project(0, wk)
                project(1, wq)
                project(2, wv)
                for t in range(T + 2):
                    if t < T:
                        pe.wait_ge(s_hproj_dve, a * 18 + (15 if t == 0 else 18))
                        if t:
                            pe.wait_ge(s_biased, a * T + t)
                        for c, (c0, cw) in enumerate(CHUNKS):
                            last = split_product(
                                bank(c, cw, ROWS[t]),
                                [(lambda p, kd=kd: qT[:, p, kd, LEAD + t * P:LEAD + t * P + ROWS[t]],
                                  lambda p, kd=kd: kT[:, p, kd, LEAD + c0:LEAD + c0 + cw]) for kd in range(KD)])
                        last.then_inc(s_qk, 1)
                    if t == 0:
                        pe.wait_ge(s_hproj_dve, a * 18 + 18)
                        pe.wait_ge(s_wout_lo, a + 2)
                        pe.wait_ge(s_x_add, a * T + 1)
                        for i in range(T):
                            if i >= 5:
                                pe.wait_ge(s_vw_dve, a * T + (i - 4))
                            split_product(bank(3 + i % 5, D, ROWS[i]),
                                          [(lambda p, kd=kd: vT[:, p, kd, LEAD + i * P:LEAD + i * P + ROWS[i]],
                                            lambda p, kd=kd: wout[:, p, kd, :]) for kd in range(KD)]
                                          ).then_inc(s_vw, 1)
                    if t >= 2:
                        i = t - 2
                        pe.wait_ge(s_hpt_act, a * T + (i + 1))
                        pe.wait_ge(s_hpt_dve, a * T + (i + 1))
                        if i >= 2:
                            pe.wait_ge(s_x_add, a * T + i)
                        split_product(bank(6 + i % 2, D, ROWS[i]),
                                      [(lambda p, k=k: pT2[i % 2][0:ROWS[k], p, k, 0:ROWS[i]],
                                        lambda p, k=k: vw[0:ROWS[k], p, k, :]) for k in range(T)]).then_inc(s_pv, 1)
                    if 1 <= t <= T:
                        i = t - 1
                        r = ROWS[i]
                        if i == 0:
                            pe.wait_ge(s_vw_dve, a * T + T)
                        for part, b, ks in ((HI, 3, range(PT8)), (LO, 5, range(PT8)), (HI, 4, range(PT8, T)),
                                            (LO, 4, range(PT8, T))):
                            if ks[0] == 0:
                                pe.wait_ge((s_att_hi, s_att_lo)[part], a * T + (i + 1))
                            for j, k in enumerate(ks):
                                dst = pt_rest[0:ROWS[k], part, j, 0:r] if b == 4 else pt_bank(b)[0:ROWS[k], j, 0:r]
                                last = nc.tensor.transpose(
                                    dst, att16[part][0:r, i % 2, k * P:k * P + ROWS[k]], ident16[0:r, 0:r])
                            if (part, b) != (HI, 4):
                                last.then_inc(s_htr, 1)

            with pe.Fori(0, 2) as g:
                with pe.Fori(0, 4) as b:
                    head(g * 4 + b, g * 677 + b * 169)

            pe.wait_ge(s_x_add, 1 + HEADS * T)
            transpose_rows(4, h, s_h_rows, 3 * T)
            wait_hT(4)
            u = 0
            for b, quad in enumerate(QUADS):
                pe.wait_ge(s_unbias, quad[-1] + 1)
                for k in range(T):
                    if u >= 6:
                        pe.wait_ge(s_adjT_act if u % 2 == 0 else s_adjT_dve, (17 if u % 2 == 0 else 16) + (u - 6) // 2 + 1)
                    for i, t in enumerate(quad):
                        last = nc.tensor.transpose(bank(u % 6)[0:ROWS[k], i * P:i * P + ROWS[t]],
                                                   bias[0:ROWS[t], t, k * P:k * P + ROWS[k]],
                                                   ident[0:ROWS[t], 0:ROWS[t]])
                    last.then_inc(s_adj_tr, 1)
                    u += 1
            pe.wait_ge(s_adjT_act, 34)
            pe.wait_ge(s_adjT_dve, 32)
            pe.wait_ge(s_l3w, 1)
            for c, (c0, cw) in enumerate(CHUNKS):
                for kd in range(KD):
                    last = nc.tensor.matmul(bank(c, cw), w_rep[:, kd, :], hT[:, kd, c0:c0 + cw],
                                            start=(kd == 0), stop=(kd == KD - 1))
                last.then_inc(s_left, 1)
            for t in range(T):
                if t >= 2:
                    pe.wait_ge(s_l3proj_taken, t - 1)
                    pe.wait_ge(s_hg, t - 1)
                b0 = (4, 6)[t % 2]
                times_hT(bank(b0, 257, ROWS[t]), w_s, t)
                times_hT(bank(b0 + 1, 260, ROWS[t]), w_c, t).then_inc(s_l3proj, 1)
            pe.wait_ge(s_l3proj_taken, T)
            pe.wait_ge(s_hg, T)
            pe.wait_ge(s_left_taken, 3)
            for t in range(T):
                if t >= 2:
                    pe.wait_ge(s_conv_taken, t - 1)
                times_adjT(bank(t % 2, 258, ROWS[t]), hg[:, :, 0:258], t, adjT3).then_inc(s_conv, 1)
            pe.wait_ge(s_edge, T)
            for t in range(T):
                if t >= 2:
                    pe.wait_ge(s_mixed, t - 1)
                times_adjT(bank(2 + t % 2, 257, ROWS[t]), hs[:, :, 0:257], t, edge).then_inc(s_gat, 1)

        @block.scalar
        def _(act):
            def norm_rows(n):
                act.wait_ge(s_ln_var, n + 1)
                nc.scalar.activation(std, var_eps, ACT.Sqrt).then_inc(s_ln_std, 1)
                if n == 2:
                    return
                act.wait_ge(s_ln_coef, n + 1)
                for t in range(T):
                    nc.scalar.activation(h[:, t, :], x[:, t, :], ACT.Relu, bias=nmean[:, t:t + 1],
                                         scale=rstd[:, t:t + 1]).then_inc(s_h_rows, 1)

            def take_hT(q):
                for b, (c0, cw) in enumerate(CHUNKS):
                    act.wait_ge(s_tr, 6 * q + 2 * b + 2)
                    nc.scalar.activation(hT[:, 1, c0:c0 + cw], bank(2 * b + 1, cw), ACT.Copy).then_inc(s_hT_act, 1)

            norm_rows(0)
            take_hT(0)
            u = 0
            for b, (c0, cw) in enumerate(CHUNKS):
                for k in range(T):
                    if u % 2 == 0:
                        act.wait_ge(s_adj_tr, u + 1)
                        nc.scalar.activation(adjT[0:ROWS[k], k, c0:c0 + cw], bank(u % 8, cw, ROWS[k]),
                                             ACT.Copy).then_inc(s_adjT_act, 1)
                    u += 1
            for t in range(T):
                act.wait_ge(s_sup, t + 1)
                nc.scalar.activation(v[0:ROWS[t], t, :], bank(t % 8, D, ROWS[t]), ACT.Copy).then_inc(s_sup_taken, 1)
            act.wait_ge(s_adjT_dve, 16)
            act.wait_ge(s_ones, 1)
            for t in range(T):
                r = ROWS[t]
                if t:
                    act.wait_ge(s_sums, 2 * t)
                nc.scalar.activation(junk_a[0:r, :], rows_b[0:r, t, :], ACT.Copy,
                                     accum_out=row_sum[0:r, t:t + 1]).then_inc(s_sums, 1)
                nc.scalar.activation(junk[0:r, :], adjT[0:r, t, :], ACT.Copy,
                                     accum_out=col_sum[0:r, t:t + 1]).then_inc(s_sums, 1)
            norm_rows(1)
            take_hT(1)

            def take_qk(s):
                for first, dst in ((0, q1T), (3, kT1), (0, qwT)):
                    for c, (c0, cw) in enumerate(CHUNKS):
                        n = 9 * s + (0 if dst is q1T else 3 if dst is kT1 else 6) + c
                        act.wait_ge(s_proj, n + 1)
                        nc.scalar.activation(dst[:, c0:c0 + cw], bank(first + c, cw, D_ATTN),
                                             ACT.Copy).then_inc(s_proj_taken, 1)

            def exps(s):
                for t in range(T):
                    r = ROWS[t]
                    act.wait_ge(s_top, T * s + t + 1)
                    b0 = 3 * (t % 2) * BANK
                    nc.scalar.activation(rows_b[0:r, t, :], psum[0:r, b0:b0 + N], ACT.Exp, bias=neg_top[0:r, t:t + 1],
                                         accum_out=total[0:r, t:t + 1]).then_inc(s_exp, 1)

            def halved_ratios(s):
                act.wait_ge(s_span, s + 1)
                for i in range(FAST[s]):
                    n = sum(FAST[:s]) + i
                    if i:
                        act.wait_ge(s_ratio, n)
                    nc.scalar.activation(ratios[:, i * T:(i + 1) * T],
                                         ratios[:, (i - 1) * T:i * T] if i else span0, ACT.Sqrt).then_inc(s_ratio, 1)

            def share_search(s):
                with act.Fori(0, FAST[s]) as i:
                    act.wait_ge(s_cand, i + 1)
                    base = i * (2 * (T - MINE[s]))
                    for n, t in enumerate(range(MINE[s], T)):
                        r = ROWS[t]
                        for m, (func, sums) in enumerate(((ACT.Relu, excess), (ACT.Sign, signs))):
                            if n:
                                act.wait_ge(s_excess, base + (2 * n + m - 1))
                            nc.scalar.activation(psum[0:r, 3 * m * BANK:3 * m * BANK + N], rows_b[0:r, t, :], func,
                                                 bias=neg_cand[0:r, t:t + 1],
                                                 accum_out=sums[0:r, t:t + 1]).then_inc(s_excess, 1)

            taken = [0]
            parts = [0]

            def part(src, scale, r):
                if parts[0] >= 4:
                    act.wait_ge(s_y_add, parts[0] - 3)
                parts[0] += 1
                nc.scalar.activation(rings[0:r, (parts[0] - 1) % 4, :], src, ACT.Copy,
                                     scale=scale).then_inc(s_part, 1)

            def next_step():
                act.wait_ge(s_step, taken[0] + 1)
                taken[0] += 1
                return 6 + (taken[0] - 1) % 2

            take_qk(0)
            exps(0)
            halved_ratios(0)
            for kd in range(KD):
                for c0, cw in CHUNKS:
                    b = next_step()
                    nc.scalar.activation(hT[:, kd, c0:c0 + cw], bank(b, cw), ACT.Copy).then_inc(s_step_taken, 1)
            act.wait_ge(s_inv, 1)
            for inv in (row_inv, col_inv):
                for t in range(T):
                    r = ROWS[t]
                    b = next_step()
                    part(bank(b, D, r), inv[0:r, t:t + 1], r)
                    nc.scalar.activation(v[0:r, t, :], psum[0:r, b * BANK + D:b * BANK + 2 * D], ACT.Copy,
                                         scale=inv[0:r, t:t + 1]).then_inc(s_step_taken, 1)
                for t in range(T):
                    r = ROWS[t]
                    b = next_step()
                    part(bank(b, D, r), inv[0:r, t:t + 1], r)

            def take_pT(s, t):
                i = T * s + t
                act.wait_ge(s_a_tr, 3 * i + 3)
                b0 = 3 * (t % 2)
                r = ROWS[t]
                nc.scalar.activation(pT[:, t % 2, 0:4, 0:r],
                                     bank(b0).rearrange("p (k n) -> p k n", n=P)[:, :, 0:r], ACT.Copy)
                nc.scalar.activation(pT[:, t % 2, 8:10, 0:r],
                                     bank(b0 + 2, 2 * P).rearrange("p (k n) -> p k n", n=P)[:, :, 0:r], ACT.Copy)
                nc.scalar.activation(pT[0:RL, t % 2, TL, 0:r], bank(b0 + 2)[0:RL, 2 * P:2 * P + r],
                                     ACT.Copy).then_inc(s_pt_act, 1)

            def attention(s):
                def product(t):
                    r = ROWS[t]
                    b = next_step()
                    act.wait_ge(s_kept_inv, T * s + t + 1)
                    if s == 0:
                        nc.scalar.activation(v[0:r, t, :], bank(b, D, r), ACT.Copy,
                                             scale=kept_inv[0:r, t:t + 1]).then_inc(s_step_taken, 1)
                    else:
                        act.wait_ge(s_bias, 1)
                        part(bank(b, D, r), kept_inv[0:r, t:t + 1], r)

                for t in range(T):
                    take_pT(s, t)
                    if t:
                        product(t - 1)
                product(T - 1)

            attention(0)
            take_hT(2)
            for t in range(T):
                r = ROWS[t]
                b = next_step()
                part(bank(b, D, r), 1.0, r)
                nc.scalar.activation(v[0:r, t, :], psum[0:r, b * BANK + D:b * BANK + 2 * D],
                                     ACT.Copy).then_inc(s_step_taken, 1)
            take_qk(1)
            exps(1)
            halved_ratios(1)
            share_search(1)
            attention(1)
            norm_rows(2)

            norm_rows(3)
            for b, (c0, cw) in enumerate(CHUNKS):
                for kd in range(KD):
                    act.wait_ge(s_tr, 6 * 3 + 2 * b + kd + 1)
                    nc.scalar.activation(hT2[:, HI, kd, c0:c0 + cw], bank(2 * b + kd, cw),
                                         ACT.Copy).then_inc(s_hT_act, 1)
            for u in range(6):
                act.wait_ge(s_stage[u % 2], 16 * (u // 2 + 1))
                nc.scalar.activation((wk, wq, wv)[u // KD][:, HI, u % KD, :], stage_in[u % 2], ACT.Copy,
                                     scale=W_SCALE).then_inc(s_w_hi, 1)

            def head(a, b):
                act.wait_ge(s_wout, a * 16 + 16)
                nc.scalar.activation(wout[:, HI, :, :], wout_in, ACT.Copy, scale=W_SCALE).then_inc(s_wout_hi, 1)
                for which, dst in enumerate((kT, qT, vT)):
                    for half in range(KD):
                        for g, group in enumerate(CGROUPS):
                            own_wait(act, s_hproj, a * 18 + (6 * which + 3 * half + g + 1), s_act_passed)
                            nc.scalar.activation(head_cols(dst, HI, half, b, group), head_bank(half, g, group),
                                                 ACT.Copy, scale=UNSCALE[which]).then_inc(s_hproj_act, 1)

                def take_vw(tiles):
                    for i in tiles:
                        act.wait_ge(s_vw, a * T + (i + 1))
                        nc.scalar.activation(vw[0:ROWS[i], HI, i, :], bank(3 + i % 5, D, ROWS[i]),
                                             ACT.Copy, scale=1 / W_SCALE).then_inc(s_vw_act, 1)

                for t in range(T + 1):
                    if t == 0:
                        take_vw(range(0, 2))
                    if t < T:
                        r = ROWS[t]
                        act.wait_ge(s_neg, a * T + (t + 1))
                        nc.scalar.activation(att[0:r, t % 2, :], att[0:r, t % 2, :], ACT.Exp,
                                             bias=neg_top[0:r, t:t + 1],
                                             accum_out=total[0:r, t:t + 1]).then_inc(s_hexp, 1)
                    if t == 0:
                        take_vw(range(2, T // 2))
                    else:
                        i = t - 1
                        ri = ROWS[i]
                        act.wait_ge(s_htr, a * (3 * T) + (3 * i + 1))
                        nc.scalar.activation(pT2[i % 2][:, HI, 0:PT8, 0:ri], pt_bank(3)[:, :, 0:ri], ACT.Copy)
                        act.wait_ge(s_htr, a * (3 * T) + (3 * i + 3))
                        nc.scalar.activation(pT2[i % 2][:, :, PT8:TL, 0:ri], pt_rest[:, :, 0:TL - PT8, 0:ri], ACT.Copy)
                        nc.scalar.activation(pT2[i % 2][0:RL, :, TL, 0:ri], pt_rest[0:RL, :, TL - PT8, 0:ri],
                                             ACT.Copy).then_inc(s_hpt_act, 1)
                    if t < T:
                        act.wait_ge(s_masked, a * T + (t + 1))
                        nc.scalar.activation(att16[HI][0:r, t % 2, :], att[0:r, t % 2, :],
                                             ACT.Copy).then_inc(s_att_hi, 1)
                    if t == 0:
                        take_vw(range(T // 2, T))

            with act.Fori(0, 2) as g:
                with act.Fori(0, 4) as b:
                    head(g * 4 + b, b)

            norm_rows(4)
            take_hT(4)
            u = 0
            for b, (c0, cw) in enumerate(CHUNKS):
                for k in range(T):
                    if u % 2 == 0:
                        act.wait_ge(s_adj_tr, 33 + u + 1)
                        nc.scalar.activation(adjT3[0:ROWS[k], k, c0:c0 + cw], bank(u % 6, cw, ROWS[k]),
                                             ACT.Copy).then_inc(s_adjT_act, 1)
                    u += 1
            for c, (c0, cw) in enumerate(CHUNKS):
                act.wait_ge(s_left, c + 1)
                nc.scalar.activation(left[:, c0:c0 + cw], bank(c, cw), ACT.Copy).then_inc(s_left_taken, 1)
            for t in range(T):
                act.wait_ge(s_l3proj, t + 1)
                r = ROWS[t]
                nc.scalar.activation(hg[0:r, t, :], bank((4, 6)[t % 2] + 1, 260, r), ACT.Copy).then_inc(s_hg, 1)
            for k in range(T):
                act.wait_ge(s_z, k + 1)
                nc.scalar.activation(edge[0:ROWS[k], k, :], z[0:ROWS[k], k % 2, :], ACT.Exp,
                                     scale=-1.0).then_inc(s_e, 1)
            act.wait_ge(s_conv_taken, T)
            nc.scalar.activation(gate_a, gate_a, ACT.Sigmoid, bias=ba_b)
            nc.scalar.activation(gate_b, gate_b, ACT.Sigmoid, bias=bb_b).then_inc(s_gate, 1)
            for t in range(T):
                r = ROWS[t]
                act.wait_ge(s_mixed, t + 1)
                nc.scalar.activation(conv[0:r, t, :], conv[0:r, t, :], ACT.Sigmoid).then_inc(s_sig, 1)

        @block.vector
        def _(dve):
            chain = [0]

            def link(ins):
                chain[0] += 1
                ins.then_inc(s_dve, 1)
                dve.wait_ge(s_dve, chain[0])

            def norm_stats(n, ready, count):
                dve.wait_ge(ready, count)
                for t in range(T):
                    last = nc.vector.bn_stats(stats[:, t, :], x[:, t, :])
                link(last)
                for t in range(T):
                    last = nc.vector.bn_aggr(mean_var[:, t, :], stats[:, t, :])
                link(last)
                nc.vector.tensor_scalar(var_eps, mean_var[:, :, 1], LN_EPS, None, ALU.add).then_inc(s_ln_var, 1)
                dve.wait_ge(s_ln_std, n + 1)
                link(nc.vector.reciprocal(rstd, std))
                nc.vector.scalar_tensor_tensor(out=nmean, in0=mean_var[:, :, 0], scalar=-1.0, in1=rstd,
                                               op0=ALU.mult, op1=ALU.mult).then_inc(s_ln_coef, 1)

            def take_hT(q):
                for b, (c0, cw) in enumerate(CHUNKS):
                    dve.wait_ge(s_tr, 6 * q + 2 * b + 1)
                    nc.vector.tensor_copy(hT[:, 0, c0:c0 + cw], bank(2 * b, cw)).then_inc(s_hT_dve, 1)

            norm_stats(0, s_x_in, 32)
            take_hT(0)
            u = 0
            for b, (c0, cw) in enumerate(CHUNKS):
                for k in range(T):
                    if u % 2:
                        dve.wait_ge(s_adj_tr, u + 1)
                        nc.vector.tensor_copy(adjT[0:ROWS[k], k, c0:c0 + cw],
                                              bank(u % 8, cw, ROWS[k])).then_inc(s_adjT_dve, 1)
                    u += 1
            dve.wait_ge(s_w_in, 16 * 5)
            link(nc.vector.tensor_scalar(one_minus_ts, ts, -1.0, 1.0, ALU.mult, ALU.add))
            dve.wait_ge(s_sup_taken, T)
            for t in range(T):
                r = ROWS[t]
                last = nc.vector.scalar_tensor_tensor(out=x[0:r, t, :], in0=v[0:r, t, :], scalar=one_minus_ts[0:r, :],
                                                      in1=x[0:r, t, :], op0=ALU.mult, op1=ALU.add)
            link(last)
            for t in range(T):
                r = ROWS[t]
                dve.wait_ge(s_mix0, t + 1)
                nc.vector.scalar_tensor_tensor(out=x[0:r, t, :], in0=bank(t % 8, D, r), scalar=ts[0:r, :],
                                               in1=x[0:r, t, :], op0=ALU.mult, op1=ALU.add).then_inc(s_x0, 1)
            norm_stats(1, s_x0, T)

            dve.wait_ge(s_sums, 2 * T)
            for sums in (row_sum, col_sum):
                last = nc.vector.tensor_scalar(sums, sums, 1.0, 1e-12, ALU.add, ALU.max)
            link(last)
            nc.vector.reciprocal(row_inv, row_sum)
            nc.vector.reciprocal(col_inv, col_sum).then_inc(s_inv, 1)
            for k in range(T):
                r = ROWS[k]
                dst = adjT[0:r, k, k * P:k * P + r]
                last = nc.vector.tensor_tensor(dst, dst, ident[0:r, 0:r], ALU.add)
            last.then_inc(s_s_ready, 1)
            take_hT(1)

            def tops(s):
                for t in range(T):
                    r = ROWS[t]
                    dve.wait_ge(s_logit, T * s + t + 1)
                    b0 = 3 * (t % 2) * BANK
                    link(nc.vector.reduce_max(top[0:r, t:t + 1], psum[0:r, b0:b0 + N], AX_X))
                    nc.vector.tensor_scalar(neg_top[0:r, t:t + 1], top[0:r, t:t + 1], -1.0, None,
                                            ALU.mult).then_inc(s_top, 1)

            def halve(count, first, mine, done):
                per = mine + (4 if first is None else 5) + (3 if mine < T else 0)
                with dve.Fori(0, count) as i:
                    base = i * per
                    n = 0
                    if first is None:
                        nc.vector.tensor_tensor(cand, low, ratios[:, bass.ds(i * T, T)], ALU.mult).then_inc(done, 1)
                        n += 1
                    else:
                        nc.vector.tensor_copy(step_now, steps[:, bass.ds(i + first, 1)]).then_inc(done, 1)
                        dve.wait_ge(done, base + 1)
                        nc.vector.scalar_tensor_tensor(out=cand, in0=low, scalar=step_now, in1=low,
                                                       op0=ALU.mult, op1=ALU.add).then_inc(done, 1)
                        n += 2
                    dve.wait_ge(done, base + n)
                    if mine < T:
                        nc.vector.tensor_scalar(neg_cand, cand, -1.0, None, ALU.mult).then_inc(s_cand, 1)
                    for t in range(mine):
                        r = ROWS[t]
                        if t >= 2:
                            dve.wait_ge(done, base + (n + t - 1))
                        nc.vector.scalar_tensor_tensor(
                            out=(junk, junk_a)[t % 2][0:r, :], in0=rows_b[0:r, t, :], scalar=cand[0:r, t:t + 1],
                            in1=rows_b[0:r, t, :], op0=ALU.is_gt, op1=ALU.mult,
                            accum_out=mass[0:r, t:t + 1]).then_inc(done, 1)
                    n += mine
                    if mine < T:
                        hers = slice(mine, T)
                        dve.wait_ge(s_excess, i * (2 * (T - mine)) + 2 * (T - mine))
                        nc.vector.tensor_scalar(signs[:, hers], signs[:, hers], float(N), 0.5,
                                                ALU.add, ALU.mult).then_inc(done, 1)
                        dve.wait_ge(done, base + (n + 1))
                        nc.vector.tensor_tensor(signs[:, hers], signs[:, hers], cand[:, hers],
                                                ALU.mult).then_inc(done, 1)
                        dve.wait_ge(done, base + (n + 2))
                        nc.vector.tensor_tensor(mass[:, hers], signs[:, hers], excess[:, hers],
                                                ALU.add).then_inc(done, 1)
                        n += 3
                    dve.wait_ge(done, base + n)
                    nc.vector.tensor_tensor(good, mass, goal, ALU.is_ge).then_inc(done, 1)
                    dve.wait_ge(done, base + (n + 1))
                    nc.vector.tensor_tensor(good, good, cand, ALU.mult).then_inc(done, 1)
                    dve.wait_ge(done, base + (n + 2))
                    nc.vector.tensor_tensor(low, low, good, ALU.max).then_inc(done, 1)
                    dve.wait_ge(done, base + (n + 3))

            def threshold(upper, done):
                n = [0]

                def then(ins):
                    n[0] += 1
                    ins.then_inc(done, 1)
                    dve.wait_ge(done, n[0])

                upper(then)
                for t in range(T):
                    r = ROWS[t]
                    part = (junk, junk_a)[t % 2]
                    then(nc.vector.scalar_tensor_tensor(
                        out=part[0:r, :], in0=rows_b[0:r, t, :], scalar=cand[0:r, t:t + 1], in1=rows_b[0:r, t, :],
                        op0=ALU.is_le, op1=ALU.mult, accum_out=mass[0:r, t:t + 1]))
                    then(nc.vector.max(top8[0:r, t, :], part[0:r, :]))
                then(nc.vector.tensor_tensor(above, total, mass, ALU.subtract))
                then(nc.vector.tensor_tensor(sum8[:, :, 0], above, top8[:, :, 0], ALU.add))
                for j in range(1, 8):
                    then(nc.vector.tensor_tensor(sum8[:, :, j], sum8[:, :, j - 1], top8[:, :, j], ALU.add))
                wide = [P, T, 8]
                then(nc.vector.tensor_tensor(sum8, sum8, goal.unsqueeze(2).broadcast_to(wide), ALU.is_ge))
                then(nc.vector.tensor_tensor(sum8, sum8, top8, ALU.mult))
                then(nc.vector.reduce_max(cut, sum8, AX_X))
                then(nc.vector.tensor_tensor(cut, cut, top8[:, :, 7], ALU.max))
                then(nc.vector.tensor_tensor(sum8, top8, cut.unsqueeze(2).broadcast_to(wide), ALU.is_gt))
                then(nc.vector.tensor_tensor(sum8, sum8, top8, ALU.mult))
                then(nc.vector.reduce_sum(good, sum8, AX_X))
                then(nc.vector.tensor_tensor(quota, goal, above, ALU.subtract))
                then(nc.vector.tensor_tensor(quota, quota, good, ALU.subtract))
                then(nc.vector.tensor_tensor(quota, quota, cut, ALU.add))

            def search(s):
                dve.wait_ge(s_exp, T * (s + 1))
                link(nc.vector.tensor_scalar(goal, total, P_NUC, None, ALU.mult))
                link(nc.vector.tensor_scalar(low, total, FLOOR, None, ALU.mult))
                nc.vector.reciprocal(span0, low).then_inc(s_span, 1)
                dve.wait_ge(s_ratio, sum(FAST[:s + 1]))
                halve(FAST[s], None, MINE[s], s_halve[s])
                threshold(lambda then: then(nc.vector.scalar_tensor_tensor(
                    out=cand, in0=low, scalar=1 + 2e-5, in1=ratios[:, (FAST[s] - 1) * T:FAST[s] * T],
                    op0=ALU.mult, op1=ALU.mult)), s_cut[s])
                for t in range(T):
                    r = ROWS[t]
                    last = nc.vector.scalar_tensor_tensor(
                        out=(junk, junk_a)[t % 2][0:r, :], in0=rows_b[0:r, t, :], scalar=cut[0:r, t:t + 1],
                        in1=rows_b[0:r, t, :], op0=ALU.is_ge, op1=ALU.mult, accum_out=down_to[0:r, t:t + 1])
                    link(last)
                link(nc.vector.tensor_scalar(good, goal, 1 - 1e-6, None, ALU.mult))
                link(nc.vector.tensor_tensor(good, down_to, good, ALU.is_lt))
                link(nc.vector.reduce_max(flags[:, 0:1], good, AX_X))
                link(nc.vector.tensor_tensor(good, goal, cut, ALU.add))
                link(nc.vector.tensor_tensor(good, down_to, good, ALU.is_ge))
                nc.vector.reduce_max(flags[:, 1:2], good, AX_X).then_inc(s_flags, 1)
                dve.wait_ge(s_flags_all, s + 1)
                link(nc.vector.tensor_copy(flags_int, flags_all))
                lower = dve.value_load(flags_int[0:1, 0:1], min_val=0, max_val=1)
                tied = dve.value_load(flags_int[0:1, 1:2], min_val=0, max_val=1)
                with dve.If(lower > 0):
                    halve(SEARCH - FAST[s], FAST[s], T, s_halve_on[s])
                    threshold(lambda then: then(nc.vector.tensor_scalar(
                        cand, low, float(np.exp(SPAN / 2.0 ** SEARCH) * (1 + 2e-6)), None, ALU.mult)), s_cut_on[s])
                with dve.If(lower + tied > 0):
                    n = [0]

                    def then(ins):
                        n[0] += 1
                        ins.then_inc(s_tied[s], 1)
                        dve.wait_ge(s_tied[s], n[0])

                    for t in range(T):
                        r = ROWS[t]
                        row = rows_b[0:r, t, :]
                        then(nc.vector.tensor_scalar(junk[0:r, :], row, cut[0:r, t:t + 1], cut[0:r, t:t + 1],
                                                     ALU.is_equal, ALU.mult))
                        then(nc.vector.tensor_tensor_scan(junk_a[0:r, :], ones_row[0:r, :].broadcast_to([r, N]),
                                                          junk[0:r, :], 0.0, ALU.mult, ALU.add))
                        then(nc.vector.scalar_tensor_tensor(
                            out=junk[0:r, :], in0=junk_a[0:r, :], scalar=quota[0:r, t:t + 1], in1=junk[0:r, :],
                            op0=ALU.is_ge, op1=ALU.mult))
                        then(nc.vector.tensor_tensor(row, row, junk[0:r, :], ALU.subtract))

            def attention(s):
                def keep(t):
                    r = ROWS[t]
                    nc.vector.scalar_tensor_tensor(
                        out=rows_b[0:r, t, :], in0=rows_b[0:r, t, :], scalar=cut[0:r, t:t + 1], in1=rows_b[0:r, t, :],
                        op0=ALU.is_ge, op1=ALU.mult, accum_out=kept[0:r, t:t + 1]).then_inc(s_a_rows, 1)
                    dve.wait_ge(s_a_rows, T * s + t + 1)
                    nc.vector.reciprocal(kept_inv[0:r, t:t + 1], kept[0:r, t:t + 1]).then_inc(s_kept_inv, 1)

                keep(0)
                for t in range(T):
                    if t + 1 < T:
                        keep(t + 1)
                    r = ROWS[t]
                    i = T * s + t
                    b0 = 3 * (t % 2)
                    dve.wait_ge(s_a_tr, 3 * i + 2)
                    nc.vector.tensor_copy(pT[:, t % 2, 4:8, 0:r],
                                          bank(b0 + 1).rearrange("p (k n) -> p k n", n=P)[:, :, 0:r]
                                          ).then_inc(s_pt_dve, 1)

            tops(0)
            search(0)
            attention(0)
            take_hT(2)
            tops(1)
            search(1)
            attention(1)
            norm_stats(2, s_y_add, 6 * T)
            dve.wait_ge(s_ln_coef, 3)
            for t in range(T):
                last = nc.vector.tensor_scalar(x[:, t, :], x[:, t, :], rstd[:, t:t + 1], nmean[:, t:t + 1],
                                               ALU.mult, ALU.add)
            link(last)
            dve.wait_ge(s_gb_in, 32)
            for t in range(T):
                r = ROWS[t]
                last = nc.vector.tensor_tensor(x[0:r, t, :], x[0:r, t, :], gamma_b[0:r, :], ALU.mult)
            link(last)
            dve.wait_ge(s_y_add, 7 * T)
            for t in range(T):
                r = ROWS[t]
                nc.vector.tensor_tensor(x[0:r, t, :], x[0:r, t, :], h[0:r, t, :], ALU.add).then_inc(s_x_final, 1)
            nc.vector.tensor_copy(ident16, ident[:, :]).then_inc(s_ident16, 1)

            norm_stats(3, s_x_final, T)
            for b, (c0, cw) in enumerate(CHUNKS):
                for kd in range(KD):
                    dve.wait_ge(s_hT_act, 9 + 2 * b + kd + 1)
                    nc.vector.tensor_tensor(hT2[:, LO, kd, c0:c0 + cw], bank(2 * b + kd, cw),
                                            hT2[:, HI, kd, c0:c0 + cw], ALU.subtract).then_inc(s_hT_dve, 1)
            for u in range(6):
                w = (wk, wq, wv)[u // KD]
                dve.wait_ge(s_w_hi, u + 1)
                nc.vector.scalar_tensor_tensor(out=w[:, LO, u % KD, :], in0=stage_in[u % 2], scalar=W_SCALE,
                                               in1=w[:, HI, u % KD, :], op0=ALU.mult,
                                               op1=ALU.subtract).then_inc(s_w_lo, 1)

            def head(a, b):
                dve.wait_ge(s_wout_hi, a + 1)
                nc.vector.scalar_tensor_tensor(out=wout[:, LO, :, :], in0=wout_in, scalar=W_SCALE,
                                               in1=wout[:, HI, :, :], op0=ALU.mult,
                                               op1=ALU.subtract).then_inc(s_wout_lo, 1)
                for which, dst in enumerate((kT, qT, vT)):
                    for half in range(KD):
                        for g, group in enumerate(CGROUPS):
                            dve.wait_ge(s_hproj_act, a * 18 + (6 * which + 3 * half + g + 1))
                            nc.vector.scalar_tensor_tensor(
                                out=head_cols(dst, LO, half, b, group), in0=head_bank(half, g, group),
                                scalar=UNSCALE[which], in1=head_cols(dst, HI, half, b, group),
                                op0=ALU.mult, op1=ALU.subtract).then_inc(s_hproj_dve, 1)

                def take_vw(tiles):
                    for i in tiles:
                        dve.wait_ge(s_vw_act, a * T + (i + 1))
                        nc.vector.scalar_tensor_tensor(
                            out=vw[0:ROWS[i], LO, i, :], in0=bank(3 + i % 5, D, ROWS[i]), scalar=1 / W_SCALE,
                            in1=vw[0:ROWS[i], HI, i, :], op0=ALU.mult, op1=ALU.subtract).then_inc(s_vw_dve, 1)

                for t in range(T + 2):
                    if t < T:
                        r = ROWS[t]
                        own_wait(dve, s_qk, a * T + (t + 1), s_dve_passed)
                        nc.vector.tensor_tensor_reduce(out=att[0:r, t % 2, :], in0=psum[0:r, 0:N], in1=bias[0:r, t, :],
                                                       scale=1.0, scalar=-3.0e38, op0=ALU.add, op1=ALU.max,
                                                       accum_out=top[0:r, t:t + 1]).then_inc(s_biased, 1)
                        dve.wait_ge(s_biased, a * T + (t + 1))
                        nc.vector.tensor_scalar(neg_top[0:r, t:t + 1], top[0:r, t:t + 1], -1.0, LOG_P_SCALE,
                                                ALU.mult, ALU.add).then_inc(s_neg, 1)
                    if t == 0:
                        take_vw(range(0, T // 3))
                    if t >= 2:
                        i = t - 2
                        ri = ROWS[i]
                        dve.wait_ge(s_pv, a * T + (i + 1))
                        dve.wait_ge(s_hinv, a * T + (i + 1))
                        dve.wait_ge(s_x_add, a * T + (i + 1))
                        nc.vector.scalar_tensor_tensor(out=x[0:ri, i, :], in0=bank(6 + i % 2, D, ri),
                                                       scalar=kept_inv[0:ri, i:i + 1], in1=x[0:ri, i, :],
                                                       op0=ALU.mult, op1=ALU.add).then_inc(s_x_add, 1)
                    if t < T:
                        dve.wait_ge(s_hexp, a * T + (t + 1))
                        nc.vector.scalar_tensor_tensor(out=att[0:r, t % 2, :], in0=bias[0:r, t, :], scalar=MASKED / 2,
                                                       in1=att[0:r, t % 2, :], op0=ALU.is_gt,
                                                       op1=ALU.mult).then_inc(s_masked, 1)
                        nc.vector.reciprocal(kept_inv[0:r, t:t + 1], total[0:r, t:t + 1]).then_inc(s_hinv, 1)
                    if t == 0:
                        take_vw(range(T // 3, T))
                    if 1 <= t <= T:
                        i = t - 1
                        ri = ROWS[i]
                        dve.wait_ge(s_htr, a * (3 * T) + (3 * i + 2))
                        nc.vector.tensor_copy(pT2[i % 2][:, LO, 0:PT8, 0:ri],
                                              pt_bank(5)[:, :, 0:ri]).then_inc(s_hpt_dve, 1)

            dve.sem_inc(s_x_add, 1)
            dve.sem_inc(s_wout_lo, 1)
            with dve.Fori(0, 2) as g:
                with dve.Fori(0, 4) as b:
                    head(g * 4 + b, b)

            norm_stats(4, s_x_add, 1 + HEADS * T)
            for t in range(T):
                nc.vector.scalar_tensor_tensor(out=bias[0:ROWS[t], t, :], in0=bias[0:ROWS[t], t, :], scalar=MASKED / 2,
                                               in1=bias[0:ROWS[t], t, :], op0=ALU.is_gt,
                                               op1=ALU.mult).then_inc(s_unbias, 1)
            take_hT(4)
            dve.wait_ge(s_l3_in, L3_LOADS)
            for kd in range(KD):
                for a_row, dst in ((a_left, w_left[:, kd:kd + 1]), (a_right, w_s[:, kd, D:D + 1])):
                    link(nc.vector.scalar_tensor_tensor(out=dot_junk, in0=w_s[:, kd, 0:D], scalar=1.0, in1=a_row,
                                                        op0=ALU.mult, op1=ALU.mult, accum_out=dst))
            for kd in range(KD):
                last = nc.vector.tensor_scalar(w_rep[:, kd, :], ident[:, :], 0.0, w_left[:, kd:kd + 1],
                                               ALU.mult, ALU.add)
            last.then_inc(s_l3w, 1)
            u = 0
            for b, (c0, cw) in enumerate(CHUNKS):
                for k in range(T):
                    if u % 2:
                        dve.wait_ge(s_adj_tr, 33 + u + 1)
                        nc.vector.tensor_copy(adjT3[0:ROWS[k], k, c0:c0 + cw],
                                              bank(u % 6, cw, ROWS[k])).then_inc(s_adjT_dve, 1)
                    u += 1
            nc.vector.memset(gate_a, 0.0)
            nc.vector.memset(gate_b, 0.0)
            link(nc.vector.memset(hs[:, :, D], 1.0))
            for t in range(T):
                dve.wait_ge(s_l3proj, t + 1)
                r = ROWS[t]
                b0 = (4, 6)[t % 2]
                nc.vector.tensor_copy(right[0:r, t:t + 1], psum[0:r, b0 * BANK + D:b0 * BANK + D + 1])
                nc.vector.tensor_copy(hs[0:r, t, 0:D], bank(b0, D, r)).then_inc(s_l3proj_taken, 1)
            dve.wait_ge(s_left_taken, 3)
            dve.wait_ge(s_l3proj_taken, T)

            def mask_edge(k):
                r = ROWS[k]
                dve.wait_ge(s_e, k + 1)
                nc.vector.scalar_tensor_tensor(out=edge[0:r, k, :], in0=adjT3[0:r, k, :], scalar=0.0,
                                               in1=edge[0:r, k, :], op0=ALU.not_equal, op1=ALU.mult).then_inc(s_edge, 1)

            for k in range(T):
                r = ROWS[k]
                if k >= 2:
                    dve.wait_ge(s_e, k - 1)
                link(nc.vector.tensor_scalar(z[0:r, k % 2, :], left[0:r, :], right[0:r, k:k + 1], 0.01,
                                             ALU.add, ALU.mult))
                nc.vector.scalar_tensor_tensor(out=z[0:r, k % 2, :], in0=left[0:r, :], scalar=right[0:r, k:k + 1],
                                               in1=z[0:r, k % 2, :], op0=ALU.add, op1=ALU.max).then_inc(s_z, 1)
                if k:
                    mask_edge(k - 1)
                dve.wait_ge(s_conv, k + 1)
                b0 = (k % 2) * BANK
                nc.vector.scalar_tensor_tensor(out=conv[0:r, k, :], in0=bank(k % 2, D, r), scalar=0.5,
                                               in1=bg_b[0:r, :], op0=ALU.mult, op1=ALU.add)
                for j, gate in enumerate((gate_a, gate_b)):
                    last = nc.vector.scalar_tensor_tensor(
                        out=gate[0:r, k:k + 1], in0=psum[0:r, b0 + D + j:b0 + D + j + 1], scalar=0.5,
                        in1=hg[0:r, k, D + 2 + j:D + 3 + j], op0=ALU.mult, op1=ALU.add)
                last.then_inc(s_conv_taken, 1)
            mask_edge(T - 1)
            dve.wait_ge(s_gate, 1)
            for t in range(T):
                r = ROWS[t]
                last = nc.vector.tensor_scalar(conv[0:r, t, :], conv[0:r, t, :], gate_b[0:r, t:t + 1], None, ALU.mult)
            link(last)
            for t in range(T):
                r = ROWS[t]
                dve.wait_ge(s_gat, t + 1)
                s1 = (2 + t % 2) * BANK + D
                link(nc.vector.tensor_scalar(den[0:r, t:t + 1], psum[0:r, s1:s1 + 1], 1e-5, None, ALU.add))
                link(nc.vector.reciprocal(den[0:r, t:t + 1], den[0:r, t:t + 1]))
                link(nc.vector.tensor_tensor(den[0:r, t:t + 1], den[0:r, t:t + 1], gate_a[0:r, t:t + 1], ALU.mult))
                nc.vector.scalar_tensor_tensor(out=conv[0:r, t, :], in0=bank(2 + t % 2, D, r),
                                               scalar=den[0:r, t:t + 1], in1=conv[0:r, t, :],
                                               op0=ALU.mult, op1=ALU.add).then_inc(s_mixed, 1)


_INS = ['x', 'adj', 'L0_gnn_t', 'L0_gnn_weight', 'L1_gnn_W1', 'L1_gnn_W2', 'L1_gnn_W3', 'L1_gnn_U1', 'L1_gnn_U2',
        'L1_gnn_U3', 'L1_gnn_gamma', 'L1_gnn_beta', 'L2_gnn_Wq', 'L2_gnn_Wk', 'L2_gnn_Wv', 'L2_gnn_Wout',
        'L3_gnn_W_sa', 'L3_gnn_a_sa', 'L3_gnn_W_gcnb', 'L3_gnn_b_gcnb', 'L3_gnn_Wa', 'L3_gnn_ba', 'L3_gnn_Wb',
        'L3_gnn_bb']


def kernel(**inputs):
    import numpy as _np
    import concourse.bacc as _bacc
    from concourse import mybir as _mybir
    from concourse.bass_utils import run_bass_kernel_spmd as _run

    nc = _bacc.Bacc("TRN2", target_bir_lowering=False, num_devices=1)
    arrays, args = {}, []
    for name in _INS:
        a = _np.ascontiguousarray(inputs[name])
        arrays[f"in_{name}"] = a
        args.append(nc.dram_tensor(f"in_{name}", a.shape, _mybir.dt.from_np(a.dtype), kind="ExternalInput").ap())
    args.append(nc.dram_tensor("out_x", (N, D), _mybir.dt.float32, kind="ExternalOutput").ap())
    graph_layers(nc, *args)
    r = _run(nc, [arrays], core_ids=[0])
    return r.results[0]["out_x"]
```

```python
import numpy as np
import concourse.bass as bass
from concourse import mybir
from contextlib import ExitStack

N, D, HEADS, D_ATTN, STEPS = 1354, 256, 8, 64, 2
P = 128
T = -(-N // P)
KD = D // P
ROWS = [min(P, N - t * P) for t in range(T)]
BANK = 512
CHUNKS = [(c * BANK, min(BANK, N - c * BANK)) for c in range(-(-N // BANK))]
QUADS = [range(4 * b, min(4 * b + 4, T)) for b in range(len(CHUNKS))]
LN_EPS = 1e-5
P_NUC = 0.9
MASKED = -1e6
SPAN = float(np.log(N / (1 - P_NUC)) + 0.05)
SEARCH = 24
FAST = (7, 10)
FLOOR = (1 - P_NUC) * 0.999 / N
MINE = (T, 7)
HN = (N + HEADS - 2 + HEADS - 1) // HEADS
LEAD = 8
PADDED = LEAD + HN * HEADS + 8
CGROUPS = [range(0, 3), range(3, 6), range(6, 8)]

HI, LO = 0, 1
PASSES = ((HI, HI), (HI, LO), (LO, HI))
W_SCALE = 64.0
LOG_P_SCALE = float(np.log(1024.0))
STAGE = HEADS * D

fp32 = mybir.dt.float32
fp16 = mybir.dt.float16
ALU = mybir.AluOpType
ACT = mybir.ActivationFunctionType
AX_X = mybir.AxisListType.X


def graph_layers(nc, x_in, adj, t_gate, W0, W1, W2, W3, U1, U2, U3, gamma, beta, Wq, Wk, Wv, Wout,
                 W_sa, a_sa, W_g, b_g, Wa, ba, Wb, bb, out):
    ctx = ExitStack()
    with ctx:
        def sb(name, cols):
            return ctx.enter_context(nc.sbuf_tensor(name, [P, cols], fp32))

        def sem(name):
            return ctx.enter_context(nc.semaphore(name))

        slot_a = sb("slot_a", T * N)
        slot_b = sb("slot_b", T * N)
        slot_x = sb("slot_x", T * D)
        slot_h = sb("slot_h", T * 257)
        slot_t = sb("slot_t", KD * N)
        slot_v = sb("slot_v", T * 260)
        slot_k = sb("slot_k", KD * PADDED)
        slot_p = sb("slot_p", 2 * T * P)
        slot_u = sb("slot_u", 12 * D)
        slot_w = sb("slot_w", 1024)
        slot_r = sb("slot_r", 4 * D + 4 * P)
        ident = sb("ident", P)
        small = sb("small", 800)

        tmp = slot_r[:, 0:4 * D]
        ab = slot_r[:, 4 * D:4 * D + 4 * P]
        adjT = slot_a[:, :].rearrange("p (k n) -> p k n", k=T)
        rows_b = slot_b[:, :].rearrange("p (k n) -> p k n", k=T)
        x = slot_x[:, :].rearrange("p (t d) -> p t d", t=T)
        y = x
        h = slot_h[:, 0:T * D].rearrange("p (t d) -> p t d", t=T)
        hT = slot_t[:, :].rearrange("p (k n) -> p k n", k=KD)
        v = slot_v[:, 0:T * D].rearrange("p (t d) -> p t d", t=T)
        pT = slot_p[:, :].rearrange("p (s k n) -> p s k n", s=2, k=T)
        rings = tmp.rearrange("p (r d) -> p r d", r=4)
        qwT = slot_k[0:D_ATTN, 0:N]
        kT1 = slot_k[0:D_ATTN, N:2 * N]
        q1T = slot_p[0:D_ATTN, 0:N]
        junk = slot_p[:, 0:N]
        junk_a = slot_p[:, N:2 * N]
        equal = slot_k[:, 0:N]
        equal_sums = slot_k[:, N:2 * N]
        u1 = slot_u[:, 0:4 * D].rearrange("p (k s d) -> p k s d", k=KD, s=STEPS)
        u2 = slot_u[:, 4 * D:8 * D].rearrange("p (k s d) -> p k s d", k=KD, s=STEPS)
        u3 = slot_u[:, 8 * D:12 * D].rearrange("p (k s d) -> p k s d", k=KD, s=STEPS)
        w0 = slot_w[:, 0:2 * D].rearrange("p (k d) -> p k d", k=KD)
        w1 = slot_w[:, 512:640].rearrange("p (k d) -> p k d", k=KD)
        w3 = slot_w[:, 640:768].rearrange("p (k d) -> p k d", k=KD)
        w2 = slot_w[0:D_ATTN, 768:832]
        gamma_b = ab[:, 0:D]
        beta_b = ab[:, D:2 * D]
        def parts(slot, cols, pattern, **sizes):
            return slot[:, 0:cols].bitcast(fp16).rearrange(pattern, s=2, **sizes)

        def weight(m):
            return parts(slot_b[:, 2 * STAGE * m:2 * STAGE * (m + 1)], 2 * STAGE, "p (s k n) -> p s k n", k=KD)

        wk, wq, wv = (weight(m) for m in range(3))
        stage_in = (slot_t[:, 0:STAGE], slot_u[:, 0:STAGE])
        wout_in = slot_w[:, 0:2 * D].rearrange("p (k d) -> p k d", k=KD)
        wout = parts(slot_w[:, 2 * D:4 * D], 2 * D, "p (s k d) -> p s k d", k=KD)
        bias = adjT
        hT2 = parts(slot_t, KD * N, "p (s k n) -> p s k n", k=KD)
        qT = parts(slot_v, KD * PADDED, "p (s k n) -> p s k n", k=KD)
        vT = parts(slot_p, KD * PADDED, "p (s k n) -> p s k n", k=KD)
        kT = parts(slot_k, KD * PADDED, "p (s k n) -> p s k n", k=KD)
        vw = parts(slot_h, T * D, "p (s t d) -> p s t d", t=T)
        pT2 = [parts(slot_p[:, i * T * P:(i + 1) * T * P], T * P, "p (s k n) -> p s k n", k=T) for i in range(2)]
        att = slot_u[:, 0:2 * N].rearrange("p (s n) -> p s n", s=2)
        att16 = (slot_r[:, 0:N].bitcast(fp16).rearrange("p (s n) -> p s n", s=2),
                 slot_u[:, 0:2 * N].bitcast(fp16).rearrange(
                     "p (s n w) -> p s n w", s=2, w=2)[:, :, :, 0])
        ident16 = slot_r[:, N:N + P // 2].bitcast(fp16)
        edge = adjT
        adjT3 = rows_b
        hs = slot_h[:, :].rearrange("p (t d) -> p t d", t=T)
        hg = slot_v[:, :].rearrange("p (t d) -> p t d", t=T)
        w_s = slot_u[:, N:N + 2 * 257].rearrange("p (k d) -> p k d", k=KD)
        w_c = slot_u[:, N + 514:N + 514 + 2 * 260].rearrange("p (k d) -> p k d", k=KD)
        left = slot_u[:, 0:N]
        z = slot_k[:, 0:2 * N].rearrange("p (s n) -> p s n", s=2)
        a_left = slot_w[:, 0:D]
        a_right = slot_w[:, D:2 * D]
        bg_b = slot_w[:, 2 * D:3 * D]
        dot_junk = slot_w[:, 3 * D:4 * D]
        w_rep = ab[:, 0:2 * P].rearrange("p (k d) -> p k d", k=KD)
        conv = slot_p[:, 0:T * D].rearrange("p (t d) -> p t d", t=T)

        at = [0]

        def table(cols):
            at[0] += cols
            return small[:, at[0] - cols:at[0]]

        stats = table(6 * T).rearrange("p (t s) -> p t s", t=T)
        mean_var = table(2 * T).rearrange("p (t s) -> p t s", t=T)
        var_eps, std, rstd, nmean = table(T), table(T), table(T), table(T)
        row_sum, col_sum, row_inv, col_inv = table(T), table(T), table(T), table(T)
        top, neg_top, total, goal, low, cand, mass, good = (table(T) for _ in range(8))
        kept, kept_inv, above, cut, quota, down_to = (table(T) for _ in range(6))
        top8, sum8 = (table(8 * T).rearrange("p (t s) -> p t s", t=T) for _ in range(2))
        ratios, span0, target, signs, excess = table(max(FAST) * T), table(T), table(T), table(T), table(T)
        ones_row, flags, flags_all = table(1), table(2), table(2)
        flags_int = table(2).bitcast(mybir.dt.int32)
        steps = table(SEARCH)
        step_now = table(1)
        ts, one_minus_ts = table(1), table(1)
        right, gate_a, gate_b, den = table(T), table(T), table(T), table(T)
        ba_b, bb_b, w_left = table(1), table(1), table(KD)

        psum = ctx.enter_context(nc.psum_tensor("psum", [P, 8 * BANK], fp32))

        def bank(b, w=BANK, rows=P):
            return psum[0:rows, b * BANK:b * BANK + w]

        UNSCALE = (1 / W_SCALE, D ** -0.5 / W_SCALE, 1 / W_SCALE)

        PT8 = 2 * BANK // P

        def pt_bank(b, tiles=PT8):
            return bank(b).bitcast(fp16)[:, 0:tiles * P].rearrange("p (k n) -> p k n", n=P)

        pt_rest = pt_bank(4, 2 * (T - PT8)).rearrange("p (s k) n -> p s k n", s=2)

        def own_wait(engine, signal, value, passed):
            engine.wait_ge(signal, value)
            engine.sem_inc(passed, 1)

        def head_bank(half, g, group):
            return psum[:, (3 * half + g) * BANK:(3 * half + g) * BANK + len(group) * HN].rearrange(
                "p (c i) -> p c i", i=HN)

        def head_cols(dst, part, half, b, group):
            start = b * -2 + (LEAD + group[0])
            run = dst[:, part, half, bass.ds(start, HN * HEADS)].rearrange("p (i c) -> p c i", c=HEADS)
            return run[:, 0:len(group), :]

        assert at[0] <= 800
        y_dram = nc.dram_tensor("x_after_layer_0", (N, D), fp32, kind="Internal").ap()

        s_x_pad, s_w_in, s_ident, s_ones = (sem(n) for n in ("x_pad", "w_in", "ident", "ones"))
        s_x_in = [sem(f"x_in{b}") for b in range(3)]
        s_adj_in = [sem(f"adj_in{b}") for b in range(3)]
        s_u_in, s_gb_in, s_x_out, s_x_back, s_adj_again = (
            sem(n) for n in ("u_in", "gamma_beta_in", "x_spilled", "x_back", "adj_again"))
        s_stage = [sem("stage_in0"), sem("stage_in1")]
        s_w_hi, s_w_lo, s_wout_hi, s_wout_lo = (sem(n) for n in ("w_hi", "w_lo", "wout_hi", "wout_lo"))
        s_wout, s_l3_in, s_out = (sem(n) for n in ("wout_in", "layer3_in", "out"))
        s_ln_var, s_ln_std, s_ln_coef, s_h_rows = (sem(n) for n in ("ln_var", "ln_std", "ln_coef", "h_rows"))
        s_tr, s_hT_dve, s_hT_act = (sem(n) for n in ("transposed", "hT_dve", "hT_act"))
        s_adj_tr, s_adjT_dve, s_adjT_act = (sem(n) for n in ("adj_tr", "adjT_dve", "adjT_act"))
        s_sup, s_sup_taken, s_mix0, s_x0 = (sem(n) for n in ("support", "support_taken", "layer0_product", "x0"))
        s_sums, s_inv, s_s_ready = (sem(n) for n in ("sums", "inv", "s_ready"))
        s_proj, s_proj_taken = sem("l1_proj"), sem("l1_proj_taken")
        s_logit, s_top, s_exp = sem("logits"), sem("top"), sem("exp")
        s_a_rows, s_kept_inv = sem("a_rows"), sem("kept_inv")
        s_a_tr, s_pt_act, s_pt_dve = sem("a_transposed"), sem("pT_act"), sem("pT_dve")
        s_step, s_step_taken = sem("l1_step"), sem("l1_step_taken")
        s_part, s_y_add = sem("y_part"), sem("y_added")
        s_bias = sem("bias")
        s_hproj, s_hproj_dve, s_hproj_act = sem("head_proj"), sem("head_proj_lo"), sem("head_proj_hi")
        s_vw, s_vw_act, s_vw_dve = sem("vw"), sem("vw_act"), sem("vw_dve")
        s_qk, s_biased, s_neg, s_hexp, s_masked = (
            sem(n) for n in ("qk", "biased", "neg_max", "head_exp", "masked"))
        s_htr, s_hpt_act, s_hpt_dve = sem("head_tr"), sem("head_pT_act"), sem("head_pT_dve")
        s_hinv, s_pv, s_x_add = sem("head_inv"), sem("pv"), sem("x_added")
        s_unbias, s_l3w, s_l3proj, s_l3proj_taken = sem("unbiased"), sem("l3_w"), sem("l3_proj"), sem("l3_proj_taken")
        s_left, s_left_taken = sem("left"), sem("left_taken")
        s_z, s_e, s_edge = sem("z"), sem("edge_exp"), sem("edge")
        s_conv, s_conv_taken, s_gate = sem("conv"), sem("conv_taken"), sem("gate")
        s_gat, s_mixed, s_sig, s_done = sem("gat"), sem("mixed"), sem("sigmoid"), sem("done")
        s_dve, s_act_passed, s_pool = sem("dve_chain"), sem("act_passed"), sem("pool_chain")
        s_halve, s_cut, s_halve_on, s_cut_on, s_tied = (
            [sem(f"{n}_step{i}") for i in range(STEPS)] for n in ("halve", "cut", "halve_on", "cut_on", "tied"))
        s_span, s_ratio, s_cand, s_excess = sem("span"), sem("ratio"), sem("cand"), sem("excess")
        s_flags, s_flags_all = sem("flags"), sem("flags_all")
        s_x_final, s_hg, s_dve_passed, s_pool_passed = (sem(n) for n in ("x_final", "hg", "dve_passed", "pool_passed"))
        s_att_hi, s_att_lo, s_ident16 = sem("attention_hi"), sem("attention_lo"), sem("ident16")
        s_target = [sem(f"target_step{i}") for i in range(STEPS)]
        s_beta, s_w_scaled, s_wv_lo = sem("beta_added"), sem("w_scaled"), sem("wv_lo")

        block = ctx.enter_context(nc.Block())

        def rows_of(dram, t0, t1):
            return dram[t0 * P:t1 * P, :].rearrange("(t p) d -> p t d", p=P)

        def col_tiles(w):
            return w.rearrange("(k p) d -> p k d", p=P)

        TL, RL = T - 1, ROWS[-1]

        DIFFUSED = 6 + 4 * T
        L3_LOADS = 16 * (2 + 4 * KD + 5)
        KEEP, PART, BOTH = range(3)
        kinds = [KEEP] * 6 + ([BOTH] * T + [PART] * T) * 2 + [KEEP] * T + [BOTH] * T + [PART] * T

        def step_freed(n):
            if kinds[n] == PART:
                return s_part, sum(k != KEEP for k in kinds[:n + 1])
            return s_step_taken, sum(k != PART for k in kinds[:n + 1])


        NORM_0, NORM_1 = range(0, 3), range(3, 6)
        Y_NORM, X_NORM = range(6, 12, 2), range(7, 12, 2)
        LAST_NORM = 12
        ALL = slice(0, T)
        QUAD_TILES = [slice(quad[0], quad[-1] + 1) for quad in QUADS]
        SPLIT_AFTER = {4: 0, 5: 1, 7: 2, 8: 3, T - 1: 4}
        POOL_UNITS = 4
        NORM_Y, NORM_X, NORM_H = range(3)
        NORM_AT = {5: ((0, NORM_Y),), 6: ((0, NORM_X),), 7: ((0, NORM_H),), T - 2: ((1, NORM_Y),),
                   T - 1: ((1, NORM_X),), T: ((1, NORM_H), (2, NORM_Y), (2, NORM_X), (2, NORM_H))}

        @block.sync
        def _(sp):
            for b, quad in enumerate(QUADS):
                full = [t for t in quad if t < TL]
                sp.dma_start(x[:, full[0]:full[-1] + 1, :], rows_of(x_in, full[0], full[-1] + 1)).then_inc(s_x_in[b], 16)
            sp.wait_ge(s_x_pad, 1)
            sp.dma_start(x[0:RL, TL, :], x_in[TL * P:N, :]).then_inc(s_x_in[2], 16)
            sp.dma_start(w0, col_tiles(W0)).then_inc(s_w_in, 16)
            for b, quad in enumerate(QUADS):
                full = [t for t in quad if t < TL]
                sp.dma_start(rows_b[:, full[0]:full[-1] + 1, :],
                             rows_of(adj, full[0], full[-1] + 1)).then_inc(s_adj_in[b], 16)
            sp.dma_start(rows_b[0:RL, TL, :], adj[TL * P:N, :]).then_inc(s_adj_in[2], 16)
            sp.dma_start(ts, t_gate.partition_broadcast(P)).then_inc(s_w_in, 16)
            sp.dma_start(w1, col_tiles(W1)).then_inc(s_w_in, 16)
            sp.dma_start(w3, col_tiles(W3)).then_inc(s_w_in, 16)
            sp.dma_start(w2, W2).then_inc(s_w_in, 16)
            for u, src in ((u1, U1), (u2, U2), (u3, U3)):
                for s in range(STEPS):
                    sp.dma_start(u[:, :, s, :], col_tiles(src[s, :, :])).then_inc(s_u_in, 16)
            sp.dma_start(gamma_b, gamma.partition_broadcast(P)).then_inc(s_gb_in, 16)
            sp.dma_start(beta_b, beta.partition_broadcast(P)).then_inc(s_gb_in, 16)
            sp.wait_ge(s_x0, T)
            sp.dma_start(rows_of(y_dram, 0, TL), x[:, 0:TL, :]).then_inc(s_x_out, 16)
            sp.dma_start(y_dram[TL * P:N, :], x[0:RL, TL, :]).then_inc(s_x_out, 16)
            sp.wait_ge(s_step, DIFFUSED)
            sp.dma_start(adjT[:, 0:TL, :], rows_of(adj, 0, TL)).then_inc(s_adj_again, 16)
            sp.dma_start(adjT[0:RL, TL, :], adj[TL * P:N, :]).then_inc(s_adj_again, 16)
            sp.wait_ge(s_x_out, 32)
            sp.wait_ge(s_step, DIFFUSED + T)
            sp.wait_ge(s_y_add, T)
            sp.dma_start(h[:, 0:TL, :], rows_of(y_dram, 0, TL)).then_inc(s_x_back, 16)
            sp.dma_start(h[0:RL, TL, :], y_dram[TL * P:N, :]).then_inc(s_x_back, 16)
            for u in range(6):
                if u == 0:
                    sp.wait_ge(s_proj, 18)
                elif u == 1:
                    sp.wait_ge(s_step, DIFFUSED)
                else:
                    sp.wait_ge(s_w_lo, u - 1)
                w = (Wk, Wq, Wv)[u // KD]
                sp.dma_start(stage_in[u % 2], w[(u % KD) * P:(u % KD + 1) * P, :]).then_inc(s_stage[u % 2], 16)
            with sp.Fori(0, HEADS) as a:
                sp.wait_ge(s_wout_lo, a + 1)
                sp.dma_start(wout_in, Wout[bass.ds(a * D, D), :].rearrange("(k p) d -> p k d", p=P)).then_inc(s_wout, 16)
            sp.wait_ge(s_x_add, 1 + HEADS * T)
            sp.dma_start(w_s[:, :, 0:D], col_tiles(W_sa)).then_inc(s_l3_in, 16)
            sp.dma_start(w_c[:, :, 0:D], col_tiles(W_g)).then_inc(s_l3_in, 16)
            for j, (w, half) in enumerate(((Wa, 0), (Wb, 0), (Wa, 1), (Wb, 1))):
                src = w[0, half * D:(half + 1) * D].rearrange("(k p a) -> p k a", p=P, a=1)
                for kd in range(KD):
                    sp.dma_start(w_c[:, kd, D + j:D + j + 1], src[:, kd, :]).then_inc(s_l3_in, 16)
            sp.dma_start(a_left, a_sa[0, 0:D].partition_broadcast(P)).then_inc(s_l3_in, 16)
            sp.dma_start(a_right, a_sa[0, D:2 * D].partition_broadcast(P)).then_inc(s_l3_in, 16)
            sp.dma_start(bg_b, b_g.partition_broadcast(P)).then_inc(s_l3_in, 16)
            sp.dma_start(ba_b, ba.partition_broadcast(P)).then_inc(s_l3_in, 16)
            sp.dma_start(bb_b, bb.partition_broadcast(P)).then_inc(s_l3_in, 16)
            for t in range(T):
                sp.wait_ge(s_done, t + 1)
                sp.dma_start(out[t * P:t * P + ROWS[t], :], x[0:ROWS[t], t, :]).then_inc(s_out, 16)
            sp.wait_ge(s_out, 16 * T)

        @block.gpsimd
        def _(pool):
            chain = [0]

            def link(ins):
                chain[0] += 1
                ins.then_inc(s_pool, 1)
                pool.wait_ge(s_pool, chain[0])

            nc.gpsimd.memset(x[:, TL, :], 0.0).then_inc(s_x_pad, 1)
            link(nc.gpsimd.memset(ident[:, :], 0.0))
            nc.gpsimd.affine_select(out=ident[:, :], in_=ident[:, :], compare_op=ALU.not_equal, fill=1.0, base=0,
                                    pattern=[[-1, P]], channel_multiplier=1).then_inc(s_ident, 1)
            for table_, value in ((row_sum, 1.0), (col_sum, 1.0), (total, 1.0), (mass, 0.0), (kept, 1.0),
                                  (ones_row, 1.0), (top8, 1.0), (down_to, 1.0),
                                  (signs, 0.0), (excess, 0.0)):
                nc.gpsimd.memset(table_, value)
            for i in range(SEARCH):
                last = nc.gpsimd.memset(steps[:, i:i + 1], float(np.expm1(SPAN / 2.0 ** (i + 1))))
            last.then_inc(s_ones, 1)

            def any_row(s):
                pool.wait_ge(s_flags, s + 1)
                nc.gpsimd.partition_all_reduce(flags_all, flags, P, bass.bass_isa.ReduceOp.max).then_inc(s_flags_all, 1)

            pool.wait_ge(s_x_out, 32)
            n = 0
            for stage in range(6):
                for t in range(T):
                    pool.wait_ge(s_part, n + 1)
                    if stage:
                        pool.wait_ge(s_y_add, n - T + 1)
                    nc.gpsimd.tensor_tensor(y[0:ROWS[t], t, :], (y if stage else h)[0:ROWS[t], t, :],
                                            rings[0:ROWS[t], n % 4, :], ALU.add).then_inc(s_y_add, 1)
                    n += 1
                    if stage == 5 and SPLIT_AFTER.get(t, POOL_UNITS) < POOL_UNITS:
                        u = SPLIT_AFTER[t]
                        w = (wk, wq, wv)[u // KD]
                        pool.wait_ge(s_w_scaled, u + 1)
                        nc.gpsimd.tensor_tensor(w[:, LO, u % KD, :], stage_in[u % 2], w[:, HI, u % KD, :],
                                                ALU.subtract).then_inc(s_w_lo, 1)
                if stage == 3:
                    any_row(0)
                if stage == 4:
                    pool.wait_ge(s_y_add, n)
                    pool.wait_ge(s_adj_again, 32)
                    for k in range(T):
                        r = ROWS[k]
                        for c, w in CHUNKS:
                            part = adjT[0:r, k, c:c + w]
                            hole = tmp[0:r, 2 * D:2 * D + w]
                            link(nc.gpsimd.tensor_scalar(hole, part, 0.0, MASKED, ALU.is_equal, ALU.mult))
                            link(nc.gpsimd.tensor_tensor(part, part, part, ALU.add))
                            link(nc.gpsimd.tensor_tensor(part, part, hole, ALU.add))
                    pool.sem_inc(s_bias, 1)
                    any_row(1)
                    pool.wait_ge(s_x_back, 32)
                    pool.wait_ge(s_gb_in, 32)
                    for t in range(T):
                        nc.gpsimd.tensor_tensor(h[0:ROWS[t], t, :], h[0:ROWS[t], t, :], beta_b[0:ROWS[t], :],
                                                ALU.add).then_inc(s_beta, 1)
            def head(a):
                for t in range(T):
                    r = ROWS[t]
                    own_wait(pool, s_att_hi, a * T + (t + 1), s_pool_passed)
                    nc.gpsimd.tensor_tensor(att16[LO][0:r, t % 2, :], att[0:r, t % 2, :], att16[HI][0:r, t % 2, :],
                                            ALU.subtract).then_inc(s_att_lo, 1)

            with pool.Fori(0, HEADS) as a:
                head(a)

            for t in range(T):
                r = ROWS[t]
                pool.wait_ge(s_sig, t + 1)
                nc.gpsimd.tensor_tensor(x[0:r, t, :], x[0:r, t, :], conv[0:r, t, :], ALU.add).then_inc(s_done, 1)

        @block.tensor
        def _(pe):
            def transpose_rows(q, src, ready, base):
                for b, quad in enumerate(QUADS):
                    pe.wait_ge(ready, base + quad[-1] + 1)
                    for kd in range(KD):
                        for i, t in enumerate(quad):
                            last = nc.tensor.transpose(bank(2 * b + kd)[:, i * P:i * P + ROWS[t]],
                                                       src[0:ROWS[t], t, kd * P:(kd + 1) * P],
                                                       ident[0:ROWS[t], 0:ROWS[t]])
                        last.then_inc(s_tr, 1)

            def wait_hT(q):
                pe.wait_ge(s_hT_dve, 3 * (q + 1) + (3 if q > 3 else 0))
                pe.wait_ge(s_hT_act, 3 * (q + 1) + (3 if q > 3 else 0))

            def times_adjT(dst, rhs, t, lhs=adjT):
                for k in range(T):
                    last = nc.tensor.matmul(dst, lhs[0:ROWS[k], k, t * P:t * P + ROWS[t]], rhs[0:ROWS[k], k, :],
                                            start=(k == 0), stop=(k == T - 1))
                return last

            def times_hT(dst, w, t):
                for kd in range(KD):
                    last = nc.tensor.matmul(dst, hT[:, kd, t * P:t * P + ROWS[t]], w[:, kd, :],
                                            start=(kd == 0), stop=(kd == KD - 1))
                return last

            pe.wait_ge(s_ident, 1)
            transpose_rows(0, h, s_h_rows, 0)
            wait_hT(0)
            u = 0
            for b, quad in enumerate(QUADS):
                pe.wait_ge(s_adj_in[b], 16 if b < 2 else 32)
                for k in range(T):
                    if u >= 8:
                        pe.wait_ge(s_adjT_act if u % 2 == 0 else s_adjT_dve, (u - 8) // 2 + 1)
                    for i, t in enumerate(quad):
                        last = nc.tensor.transpose(bank(u % 8)[0:ROWS[k], i * P:i * P + ROWS[t]],
                                                   rows_b[0:ROWS[t], t, k * P:k * P + ROWS[k]],
                                                   ident[0:ROWS[t], 0:ROWS[t]])
                    last.then_inc(s_adj_tr, 1)
                    u += 1
            pe.wait_ge(s_adjT_act, 17)
            pe.wait_ge(s_adjT_dve, 16)
            pe.wait_ge(s_w_in, 16 * 5)
            for t in range(T):
                if t >= 8:
                    pe.wait_ge(s_sup_taken, t - 7)
                times_hT(bank(t % 8, D, ROWS[t]), w0, t).then_inc(s_sup, 1)
            pe.wait_ge(s_sup_taken, T)
            for t in range(T):
                if t >= 8:
                    pe.wait_ge(s_x0, t - 7)
                times_adjT(bank(t % 8, D, ROWS[t]), v, t).then_inc(s_mix0, 1)

            pe.wait_ge(s_x0, T)
            transpose_rows(1, h, s_h_rows, T)

            def project_qk(s):
                wait_hT(1 + s)
                for first, w in ((0, w1), (3, w3)):
                    for c, (c0, cw) in enumerate(CHUNKS):
                        for kd in range(KD):
                            last = nc.tensor.matmul(bank(first + c, cw, D_ATTN), w[:, kd, :], hT[:, kd, c0:c0 + cw],
                                                    start=(kd == 0), stop=(kd == KD - 1))
                        last.then_inc(s_proj, 1)
                for c, (c0, cw) in enumerate(CHUNKS):
                    pe.wait_ge(s_proj_taken, 9 * s + c + 1)
                    nc.tensor.matmul(bank(c, cw, D_ATTN), w2, q1T[:, c0:c0 + cw],
                                     start=True, stop=True).then_inc(s_proj, 1)

            def logits(s):
                pe.wait_ge(s_proj_taken, 9 * (s + 1))
                for t in range(T):
                    i = T * s + t
                    if t >= 2:
                        pe.wait_ge(s_exp, i - 1)
                    for c, (c0, cw) in enumerate(CHUNKS):
                        last = nc.tensor.matmul(bank(3 * (t % 2) + c, cw, ROWS[t]), qwT[:, t * P:t * P + ROWS[t]],
                                                kT1[:, c0:c0 + cw], start=True, stop=True)
                    last.then_inc(s_logit, 1)

            steps_made = [0]

            def step_done(last):
                last.then_inc(s_step, 1)
                steps_made[0] += 1

            def step_bank():
                if steps_made[0] >= 2:
                    pe.wait_ge(*step_freed(steps_made[0] - 2))
                return 6 + steps_made[0] % 2

            def attention_step(s, rhs):
                def product(t):
                    i = T * s + t
                    pe.wait_ge(s_pt_act, i + 1)
                    if s == 0:
                        pe.wait_ge(s_pt_dve, i + 1)
                    dst = bank(step_bank(), D, ROWS[t])
                    for k in range(T):
                        last = nc.tensor.matmul(dst, pT[0:ROWS[k], t % 2, k, 0:ROWS[t]], rhs[0:ROWS[k], k, :],
                                                start=(k == 0), stop=(k == T - 1))
                    step_done(last)

                for t in range(T):
                    pe.wait_ge(s_a_rows, T * s + t + 1)
                    for b, quad in enumerate(QUADS):
                        for i, k in enumerate(quad):
                            last = nc.tensor.transpose(
                                bank(3 * (t % 2) + b)[0:ROWS[k], i * P:i * P + ROWS[t]],
                                rows_b[0:ROWS[t], t, k * P:k * P + ROWS[k]], ident[0:ROWS[t], 0:ROWS[t]])
                        last.then_inc(s_a_tr, 1)
                    if t:
                        product(t - 1)
                product(T - 1)

            project_qk(0)
            logits(0)
            pe.wait_ge(s_s_ready, 1)
            for kd in range(KD):
                for c0, cw in CHUNKS:
                    dst = bank(step_bank(), cw)
                    for k in range(T):
                        last = nc.tensor.matmul(dst, h[0:ROWS[k], k, kd * P:(kd + 1) * P],
                                                adjT[0:ROWS[k], k, c0:c0 + cw], start=(k == 0), stop=(k == T - 1))
                    step_done(last)
            pe.wait_ge(s_step_taken, 6)
            pe.wait_ge(s_u_in, 16 * 6)
            for u in (u1, u2):
                for t in range(T):
                    step_done(times_hT(bank(step_bank(), 2 * D, ROWS[t]), u.rearrange("p k s d -> p k (s d)"), t))
                pe.wait_ge(*step_freed(steps_made[0] - 1))
                for t in range(T):
                    step_done(times_adjT(bank(step_bank(), D, ROWS[t]), v, t))
            attention_step(0, h)
            transpose_rows(2, v, s_step_taken, DIFFUSED - 2 * T)
            wait_hT(2)
            for t in range(T):
                step_done(times_hT(bank(step_bank(), 2 * D, ROWS[t]), u3.rearrange("p k s d -> p k (s d)"), t))
            project_qk(1)
            logits(1)
            attention_step(1, v)

            transpose_rows(3, h, s_h_rows, 2 * T)
            pe.wait_ge(s_hT_dve, 15)
            pe.wait_ge(s_bias, 1)
            pe.wait_ge(s_ident16, 1)

            def split_product(dst, pieces, first=True, final=True):
                for n, (lhs, rhs) in enumerate(pieces):
                    for m, (pl, pr) in enumerate(PASSES):
                        last = nc.tensor.matmul(dst, lhs(pl), rhs(pr), start=(first and n == 0 and m == 0),
                                                stop=(final and n == len(pieces) - 1 and m == len(PASSES) - 1))
                return last

            def head(a, base):
                def project(which, w):
                    if which < 2:
                        pe.wait_ge(s_w_lo, KD * (which + 1))
                    else:
                        pe.wait_ge(s_wv_lo, KD)
                    for half in range(KD):
                        for g, group in enumerate(CGROUPS):
                            if which:
                                pe.wait_ge(s_hproj_dve, a * 18 + (6 * (which - 1) + 3 * half + g + 1))
                            for i, c in enumerate(group):
                                c0 = c * D + half * P
                                last = split_product(
                                    bank(3 * half + g)[:, i * HN:(i + 1) * HN],
                                    [(lambda p, kd=kd: w[:, p, kd, c0:c0 + P],
                                      lambda p, kd=kd: hT2[:, p, kd, bass.ds(base, HN)]) for kd in range(KD)])
                            last.then_inc(s_hproj, 1)

                project(0, wk)
                project(1, wq)
                project(2, wv)
                for t in range(T + 2):
                    if t < T:
                        pe.wait_ge(s_hproj_dve, a * 18 + (15 if t == 0 else 18))
                        if t:
                            pe.wait_ge(s_biased, a * T + t)
                        for c, (c0, cw) in enumerate(CHUNKS):
                            last = split_product(
                                bank(c, cw, ROWS[t]),
                                [(lambda p, kd=kd: qT[:, p, kd, LEAD + t * P:LEAD + t * P + ROWS[t]],
                                  lambda p, kd=kd: kT[:, p, kd, LEAD + c0:LEAD + c0 + cw]) for kd in range(KD)])
                        last.then_inc(s_qk, 1)
                    if t == 0:
                        pe.wait_ge(s_hproj_dve, a * 18 + 18)
                        pe.wait_ge(s_wout_lo, a + 2)
                        pe.wait_ge(s_x_add, a * T + 1)
                        for i in range(T):
                            if i >= 5:
                                pe.wait_ge(s_vw_dve, a * T + (i - 4))
                            split_product(bank(3 + i % 5, D, ROWS[i]),
                                          [(lambda p, kd=kd: vT[:, p, kd, LEAD + i * P:LEAD + i * P + ROWS[i]],
                                            lambda p, kd=kd: wout[:, p, kd, :]) for kd in range(KD)]
                                          ).then_inc(s_vw, 1)
                    if t >= 2:
                        i = t - 2
                        pe.wait_ge(s_hpt_dve, a * T + (i + 1))
                        if i >= 2:
                            pe.wait_ge(s_x_add, a * T + i)
                        for part, ks in enumerate((range(PT8), range(PT8, T))):
                            pe.wait_ge(s_hpt_act, a * (2 * T) + (2 * i + part + 1))
                            last = split_product(bank(6 + i % 2, D, ROWS[i]),
                                                 [(lambda p, k=k: pT2[i % 2][0:ROWS[k], p, k, 0:ROWS[i]],
                                                   lambda p, k=k: vw[0:ROWS[k], p, k, :]) for k in ks],
                                                 first=(part == 0), final=(part == 1))
                        last.then_inc(s_pv, 1)
                    if 1 <= t <= T:
                        i = t - 1
                        r = ROWS[i]
                        if i == 0:
                            pe.wait_ge(s_vw_dve, a * T + T)
                        for part, b, ks in ((HI, 3, range(PT8)), (LO, 5, range(PT8)), (HI, 4, range(PT8, T)),
                                            (LO, 4, range(PT8, T))):
                            if ks[0] == 0:
                                pe.wait_ge((s_att_hi, s_att_lo)[part], a * T + (i + 1))
                            for j, k in enumerate(ks):
                                dst = pt_rest[0:ROWS[k], part, j, 0:r] if b == 4 else pt_bank(b)[0:ROWS[k], j, 0:r]
                                last = nc.tensor.transpose(
                                    dst, att16[part][0:r, i % 2, k * P:k * P + ROWS[k]], ident16[0:r, 0:r])
                            if (part, b) != (HI, 4):
                                last.then_inc(s_htr, 1)

            with pe.Fori(0, 2) as g:
                with pe.Fori(0, 4) as b:
                    head(g * 4 + b, g * 677 + b * 169)

            pe.wait_ge(s_x_add, 1 + HEADS * T)
            transpose_rows(4, h, s_h_rows, 3 * T)
            wait_hT(4)
            pe.wait_ge(s_l3w, 1)
            for c, (c0, cw) in enumerate(CHUNKS):
                for kd in range(KD):
                    last = nc.tensor.matmul(bank(c, cw), w_rep[:, kd, :], hT[:, kd, c0:c0 + cw],
                                            start=(kd == 0), stop=(kd == KD - 1))
                last.then_inc(s_left, 1)
            for t in range(T):
                if t >= 2:
                    pe.wait_ge(s_l3proj_taken, t - 1)
                    pe.wait_ge(s_hg, t - 1)
                b0 = (4, 6)[t % 2]
                times_hT(bank(b0, 257, ROWS[t]), w_s, t)
                times_hT(bank(b0 + 1, 260, ROWS[t]), w_c, t).then_inc(s_l3proj, 1)
            pe.wait_ge(s_l3proj_taken, T)
            pe.wait_ge(s_hg, T)
            pe.wait_ge(s_left_taken, 3)
            u = 0
            for b, quad in enumerate(QUADS):
                pe.wait_ge(s_unbias, quad[-1] + 1)
                for k in range(T):
                    if u >= 6:
                        pe.wait_ge(s_adjT_act if u % 2 == 0 else s_adjT_dve, (17 if u % 2 == 0 else 16) + (u - 6) // 2 + 1)
                    for i, t in enumerate(quad):
                        last = nc.tensor.transpose(bank(u % 6)[0:ROWS[k], i * P:i * P + ROWS[t]],
                                                   bias[0:ROWS[t], t, k * P:k * P + ROWS[k]],
                                                   ident[0:ROWS[t], 0:ROWS[t]])
                    last.then_inc(s_adj_tr, 1)
                    u += 1
            pe.wait_ge(s_adjT_act, 34)
            pe.wait_ge(s_adjT_dve, 32)
            for t in range(T):
                if t >= 2:
                    pe.wait_ge(s_conv_taken, t - 1)
                times_adjT(bank(t % 2, 258, ROWS[t]), hg[:, :, 0:258], t, adjT3).then_inc(s_conv, 1)
            pe.wait_ge(s_edge, T)
            for t in range(T):
                if t >= 2:
                    pe.wait_ge(s_mixed, t - 1)
                times_adjT(bank(2 + t % 2, 257, ROWS[t]), hs[:, :, 0:257], t, edge).then_inc(s_gat, 1)

        @block.scalar
        def _(act):
            def norm_std(n, tiles=ALL):
                act.wait_ge(s_ln_var, n + 1)
                nc.scalar.activation(std[:, tiles], var_eps[:, tiles], ACT.Sqrt).then_inc(s_ln_std, 1)

            def norm_rows(n, tiles=ALL):
                act.wait_ge(s_ln_coef, n + 1)
                for t in range(T)[tiles]:
                    nc.scalar.activation(h[:, t, :], x[:, t, :], ACT.Relu, bias=nmean[:, t:t + 1],
                                         scale=rstd[:, t:t + 1]).then_inc(s_h_rows, 1)

            def take_hT(q):
                for b, (c0, cw) in enumerate(CHUNKS):
                    act.wait_ge(s_tr, 6 * q + 2 * b + 2)
                    nc.scalar.activation(hT[:, 1, c0:c0 + cw], bank(2 * b + 1, cw), ACT.Copy).then_inc(s_hT_act, 1)

            norm_std(NORM_0[0], QUAD_TILES[0])
            for b in range(3):
                if b < 2:
                    norm_std(NORM_0[b + 1], QUAD_TILES[b + 1])
                norm_rows(NORM_0[b], QUAD_TILES[b])
            take_hT(0)
            u = 0
            for b, (c0, cw) in enumerate(CHUNKS):
                for k in range(T):
                    if u % 2 == 0:
                        act.wait_ge(s_adj_tr, u + 1)
                        nc.scalar.activation(adjT[0:ROWS[k], k, c0:c0 + cw], bank(u % 8, cw, ROWS[k]),
                                             ACT.Copy).then_inc(s_adjT_act, 1)
                    u += 1
            for t in range(T):
                act.wait_ge(s_sup, t + 1)
                nc.scalar.activation(v[0:ROWS[t], t, :], bank(t % 8, D, ROWS[t]), ACT.Copy).then_inc(s_sup_taken, 1)
            act.wait_ge(s_adjT_dve, 16)
            act.wait_ge(s_ones, 1)
            for t in range(T):
                r = ROWS[t]
                if t:
                    act.wait_ge(s_sums, 2 * t)
                nc.scalar.activation(junk_a[0:r, :], rows_b[0:r, t, :], ACT.Copy,
                                     accum_out=row_sum[0:r, t:t + 1]).then_inc(s_sums, 1)
                nc.scalar.activation(junk[0:r, :], adjT[0:r, t, :], ACT.Copy,
                                     accum_out=col_sum[0:r, t:t + 1]).then_inc(s_sums, 1)
                if t == 6:
                    norm_std(NORM_1[0], QUAD_TILES[0])
                if t == 7:
                    norm_rows(NORM_1[0], QUAD_TILES[0])
            norm_std(NORM_1[1], QUAD_TILES[1])
            norm_rows(NORM_1[1], QUAD_TILES[1])
            norm_std(NORM_1[2], QUAD_TILES[2])
            norm_rows(NORM_1[2], QUAD_TILES[2])
            take_hT(1)

            def take_qk(s):
                for first, dst in ((0, q1T), (3, kT1), (0, qwT)):
                    for c, (c0, cw) in enumerate(CHUNKS):
                        n = 9 * s + (0 if dst is q1T else 3 if dst is kT1 else 6) + c
                        act.wait_ge(s_proj, n + 1)
                        nc.scalar.activation(dst[:, c0:c0 + cw], bank(first + c, cw, D_ATTN),
                                             ACT.Copy).then_inc(s_proj_taken, 1)

            def exps(s):
                for t in range(T):
                    r = ROWS[t]
                    act.wait_ge(s_top, T * s + t + 1)
                    b0 = 3 * (t % 2) * BANK
                    nc.scalar.activation(rows_b[0:r, t, :], psum[0:r, b0:b0 + N], ACT.Exp, bias=neg_top[0:r, t:t + 1],
                                         accum_out=total[0:r, t:t + 1]).then_inc(s_exp, 1)

            def halved_ratios(s):
                act.wait_ge(s_span, s + 1)
                for i in range(FAST[s]):
                    n = sum(FAST[:s]) + i
                    if i:
                        act.wait_ge(s_ratio, n)
                    nc.scalar.activation(ratios[:, i * T:(i + 1) * T],
                                         ratios[:, (i - 1) * T:i * T] if i else span0, ACT.Sqrt).then_inc(s_ratio, 1)

            def share_search(s):
                with act.Fori(0, FAST[s]) as i:
                    act.wait_ge(s_cand, i + 1)
                    base = i * (2 * (T - MINE[s]))
                    for n, t in enumerate(range(MINE[s], T)):
                        r = ROWS[t]
                        for m, (func, sums) in enumerate(((ACT.Relu, excess), (ACT.Sign, signs))):
                            if n:
                                act.wait_ge(s_excess, base + (2 * n + m - 1))
                            nc.scalar.activation(psum[0:r, 3 * m * BANK:3 * m * BANK + N], rows_b[0:r, t, :], func,
                                                 bias=cand[0:r, t:t + 1], scale=-1.0,
                                                 accum_out=sums[0:r, t:t + 1]).then_inc(s_excess, 1)

            def split_high(u):
                act.wait_ge(s_stage[u % 2], 16 * (u // 2 + 1))
                nc.scalar.activation((wk, wq, wv)[u // KD][:, HI, u % KD, :], stage_in[u % 2], ACT.Copy,
                                     scale=W_SCALE).then_inc(s_w_hi, 1)

            taken = [0]
            parts = [0]

            def part(src, scale, r):
                if parts[0] >= 4:
                    act.wait_ge(s_y_add, parts[0] - 3)
                parts[0] += 1
                nc.scalar.activation(rings[0:r, (parts[0] - 1) % 4, :], src, ACT.Copy,
                                     scale=scale).then_inc(s_part, 1)

            def next_step():
                act.wait_ge(s_step, taken[0] + 1)
                taken[0] += 1
                return 6 + (taken[0] - 1) % 2

            take_qk(0)
            exps(0)
            halved_ratios(0)
            for kd in range(KD):
                for c0, cw in CHUNKS:
                    b = next_step()
                    nc.scalar.activation(hT[:, kd, c0:c0 + cw], bank(b, cw), ACT.Copy).then_inc(s_step_taken, 1)
            act.wait_ge(s_inv, 1)
            for inv in (row_inv, col_inv):
                for t in range(T):
                    r = ROWS[t]
                    b = next_step()
                    part(bank(b, D, r), inv[0:r, t:t + 1], r)
                    nc.scalar.activation(v[0:r, t, :], psum[0:r, b * BANK + D:b * BANK + 2 * D], ACT.Copy,
                                         scale=inv[0:r, t:t + 1]).then_inc(s_step_taken, 1)
                for t in range(T):
                    r = ROWS[t]
                    b = next_step()
                    part(bank(b, D, r), inv[0:r, t:t + 1], r)

            def take_pT(s, t):
                i = T * s + t
                act.wait_ge(s_a_tr, 3 * i + 3)
                b0 = 3 * (t % 2)
                r = ROWS[t]
                nc.scalar.activation(pT[:, t % 2, 0:4, 0:r],
                                     bank(b0).rearrange("p (k n) -> p k n", n=P)[:, :, 0:r], ACT.Copy)
                if s:
                    nc.scalar.activation(pT[:, t % 2, 4:8, 0:r],
                                         bank(b0 + 1).rearrange("p (k n) -> p k n", n=P)[:, :, 0:r], ACT.Copy)
                nc.scalar.activation(pT[:, t % 2, 8:10, 0:r],
                                     bank(b0 + 2, 2 * P).rearrange("p (k n) -> p k n", n=P)[:, :, 0:r], ACT.Copy)
                nc.scalar.activation(pT[0:RL, t % 2, TL, 0:r], bank(b0 + 2)[0:RL, 2 * P:2 * P + r],
                                     ACT.Copy).then_inc(s_pt_act, 1)

            def attention(s):
                def product(t):
                    r = ROWS[t]
                    b = next_step()
                    act.wait_ge(s_kept_inv, T * s + t + 1)
                    if s == 0:
                        nc.scalar.activation(v[0:r, t, :], bank(b, D, r), ACT.Copy,
                                             scale=kept_inv[0:r, t:t + 1]).then_inc(s_step_taken, 1)
                    else:
                        act.wait_ge(s_bias, 1)
                        part(bank(b, D, r), kept_inv[0:r, t:t + 1], r)

                def between(t):
                    if s == 0:
                        return
                    for b, stage in NORM_AT.get(t, ()):
                        quad = QUAD_TILES[b]
                        if stage == NORM_Y:
                            norm_std(Y_NORM[b], quad)
                        elif stage == NORM_X:
                            norm_std(X_NORM[b], quad)
                        else:
                            norm_rows(X_NORM[b], quad)
                    if t in SPLIT_AFTER:
                        u = SPLIT_AFTER[t]
                        act.wait_ge(s_a_tr, 3 * (T + t) + 1)
                        split_high(u)
                        if u < POOL_UNITS:
                            nc.scalar.activation(stage_in[u % 2], stage_in[u % 2], ACT.Copy,
                                                 scale=W_SCALE).then_inc(s_w_scaled, 1)

                for t in range(T):
                    take_pT(s, t)
                    if t:
                        product(t - 1)
                    between(t)
                product(T - 1)
                between(T)

            attention(0)
            take_hT(2)
            for t in range(T):
                r = ROWS[t]
                b = next_step()
                part(bank(b, D, r), 1.0, r)
                nc.scalar.activation(v[0:r, t, :], psum[0:r, b * BANK + D:b * BANK + 2 * D],
                                     ACT.Copy).then_inc(s_step_taken, 1)
            take_qk(1)
            exps(1)
            halved_ratios(1)
            share_search(1)
            attention(1)

            act.wait_ge(s_wv_lo, 1)
            for b, (c0, cw) in enumerate(CHUNKS):
                for kd in range(KD):
                    act.wait_ge(s_tr, 6 * 3 + 2 * b + kd + 1)
                    nc.scalar.activation(hT2[:, HI, kd, c0:c0 + cw], bank(2 * b + kd, cw),
                                         ACT.Copy).then_inc(s_hT_act, 1)
            split_high(5)

            def head(a, b):
                act.wait_ge(s_wout, a * 16 + 16)
                nc.scalar.activation(wout[:, HI, :, :], wout_in, ACT.Copy, scale=W_SCALE).then_inc(s_wout_hi, 1)
                for which, dst in enumerate((kT, qT, vT)):
                    for half in range(KD):
                        for g, group in enumerate(CGROUPS):
                            own_wait(act, s_hproj, a * 18 + (6 * which + 3 * half + g + 1), s_act_passed)
                            nc.scalar.activation(head_cols(dst, HI, half, b, group), head_bank(half, g, group),
                                                 ACT.Copy, scale=UNSCALE[which]).then_inc(s_hproj_act, 1)

                def take_vw(tiles):
                    for i in tiles:
                        act.wait_ge(s_vw, a * T + (i + 1))
                        nc.scalar.activation(vw[0:ROWS[i], HI, i, :], bank(3 + i % 5, D, ROWS[i]),
                                             ACT.Copy, scale=1 / W_SCALE).then_inc(s_vw_act, 1)

                for t in range(T + 1):
                    if t == 0:
                        take_vw(range(0, 2))
                    if t < T:
                        r = ROWS[t]
                        act.wait_ge(s_neg, a * T + (t + 1))
                        nc.scalar.activation(att[0:r, t % 2, :], att[0:r, t % 2, :], ACT.Exp,
                                             bias=neg_top[0:r, t:t + 1],
                                             accum_out=total[0:r, t:t + 1]).then_inc(s_hexp, 1)
                    if t == 0:
                        take_vw(range(2, T // 2))
                    else:
                        i = t - 1
                        ri = ROWS[i]
                        act.wait_ge(s_htr, a * (3 * T) + (3 * i + 1))
                        nc.scalar.activation(pT2[i % 2][:, HI, 0:PT8, 0:ri], pt_bank(3)[:, :, 0:ri],
                                             ACT.Copy).then_inc(s_hpt_act, 1)
                        act.wait_ge(s_htr, a * (3 * T) + (3 * i + 3))
                        nc.scalar.activation(pT2[i % 2][:, :, PT8:TL, 0:ri], pt_rest[:, :, 0:TL - PT8, 0:ri], ACT.Copy)
                        nc.scalar.activation(pT2[i % 2][0:RL, :, TL, 0:ri], pt_rest[0:RL, :, TL - PT8, 0:ri],
                                             ACT.Copy).then_inc(s_hpt_act, 1)
                    if t < T:
                        act.wait_ge(s_masked, a * T + (t + 1))
                        nc.scalar.activation(att16[HI][0:r, t % 2, :], att[0:r, t % 2, :],
                                             ACT.Copy).then_inc(s_att_hi, 1)
                    if t == 0:
                        take_vw(range(T // 2, T))

            with act.Fori(0, 2) as g:
                with act.Fori(0, 4) as b:
                    head(g * 4 + b, b)

            norm_std(LAST_NORM)
            norm_rows(LAST_NORM)
            take_hT(4)
            for c, (c0, cw) in enumerate(CHUNKS):
                act.wait_ge(s_left, c + 1)
                nc.scalar.activation(left[:, c0:c0 + cw], bank(c, cw), ACT.Copy).then_inc(s_left_taken, 1)
            for t in range(T):
                act.wait_ge(s_l3proj, t + 1)
                r = ROWS[t]
                nc.scalar.activation(hg[0:r, t, :], bank((4, 6)[t % 2] + 1, 260, r), ACT.Copy).then_inc(s_hg, 1)
            u = 0
            for b, (c0, cw) in enumerate(CHUNKS):
                for k in range(T):
                    if u % 2 == 0:
                        act.wait_ge(s_adj_tr, 33 + u + 1)
                        nc.scalar.activation(adjT3[0:ROWS[k], k, c0:c0 + cw], bank(u % 6, cw, ROWS[k]),
                                             ACT.Copy).then_inc(s_adjT_act, 1)
                    u += 1
            for k in range(T):
                act.wait_ge(s_z, k + 1)
                nc.scalar.activation(edge[0:ROWS[k], k, :], z[0:ROWS[k], k % 2, :], ACT.Exp,
                                     scale=-1.0).then_inc(s_e, 1)
            act.wait_ge(s_conv_taken, T)
            nc.scalar.activation(gate_a, gate_a, ACT.Sigmoid, bias=ba_b)
            nc.scalar.activation(gate_b, gate_b, ACT.Sigmoid, bias=bb_b).then_inc(s_gate, 1)
            for t in range(T):
                r = ROWS[t]
                act.wait_ge(s_mixed, t + 1)
                nc.scalar.activation(conv[0:r, t, :], conv[0:r, t, :], ACT.Sigmoid).then_inc(s_sig, 1)

        @block.vector
        def _(dve):
            chain = [0]

            def link(ins):
                chain[0] += 1
                ins.then_inc(s_dve, 1)
                dve.wait_ge(s_dve, chain[0])

            def norm_var(ready, count, tiles=ALL):
                dve.wait_ge(ready, count)
                for t in range(T)[tiles]:
                    last = nc.vector.bn_stats(stats[:, t, :], x[:, t, :])
                link(last)
                for t in range(T)[tiles]:
                    last = nc.vector.bn_aggr(mean_var[:, t, :], stats[:, t, :])
                link(last)
                nc.vector.tensor_scalar(var_eps[:, tiles], mean_var[:, tiles, 1], LN_EPS, None,
                                        ALU.add).then_inc(s_ln_var, 1)

            def norm_coef(n, tiles=ALL):
                dve.wait_ge(s_ln_std, n + 1)
                link(nc.vector.reciprocal(rstd[:, tiles], std[:, tiles]))
                nc.vector.scalar_tensor_tensor(out=nmean[:, tiles], in0=mean_var[:, tiles, 0], scalar=-1.0,
                                               in1=rstd[:, tiles], op0=ALU.mult, op1=ALU.mult).then_inc(s_ln_coef, 1)

            def take_hT(q):
                for b, (c0, cw) in enumerate(CHUNKS):
                    dve.wait_ge(s_tr, 6 * q + 2 * b + 1)
                    nc.vector.tensor_copy(hT[:, 0, c0:c0 + cw], bank(2 * b, cw)).then_inc(s_hT_dve, 1)

            norm_var(s_x_in[0], 16, QUAD_TILES[0])
            for b in range(3):
                if b < 2:
                    norm_var(s_x_in[b + 1], (16, 32)[b], QUAD_TILES[b + 1])
                norm_coef(NORM_0[b], QUAD_TILES[b])
            take_hT(0)
            u = 0
            for b, (c0, cw) in enumerate(CHUNKS):
                for k in range(T):
                    if u % 2:
                        dve.wait_ge(s_adj_tr, u + 1)
                        nc.vector.tensor_copy(adjT[0:ROWS[k], k, c0:c0 + cw],
                                              bank(u % 8, cw, ROWS[k])).then_inc(s_adjT_dve, 1)
                    u += 1
            dve.wait_ge(s_w_in, 16 * 5)
            link(nc.vector.tensor_scalar(one_minus_ts, ts, -1.0, 1.0, ALU.mult, ALU.add))
            dve.wait_ge(s_sup_taken, T)
            for t in range(T):
                r = ROWS[t]
                last = nc.vector.scalar_tensor_tensor(out=x[0:r, t, :], in0=v[0:r, t, :], scalar=one_minus_ts[0:r, :],
                                                      in1=x[0:r, t, :], op0=ALU.mult, op1=ALU.add)
            link(last)
            for t in range(T):
                r = ROWS[t]
                dve.wait_ge(s_mix0, t + 1)
                nc.vector.scalar_tensor_tensor(out=x[0:r, t, :], in0=bank(t % 8, D, r), scalar=ts[0:r, :],
                                               in1=x[0:r, t, :], op0=ALU.mult, op1=ALU.add).then_inc(s_x0, 1)
                for b in range(3):
                    if t == min(QUADS[b][-1] + 1, T - 1):
                        norm_var(s_x0, QUADS[b][-1] + 1, QUAD_TILES[b])
                    if t == min(QUADS[b][-1] + 2, T - 1):
                        norm_coef(NORM_1[b], QUAD_TILES[b])

            dve.wait_ge(s_sums, 2 * T)
            for sums in (row_sum, col_sum):
                last = nc.vector.tensor_scalar(sums, sums, 1.0, 1e-12, ALU.add, ALU.max)
            link(last)
            nc.vector.reciprocal(row_inv, row_sum)
            nc.vector.reciprocal(col_inv, col_sum).then_inc(s_inv, 1)
            for k in range(T):
                r = ROWS[k]
                dst = adjT[0:r, k, k * P:k * P + r]
                last = nc.vector.tensor_tensor(dst, dst, ident[0:r, 0:r], ALU.add)
            last.then_inc(s_s_ready, 1)
            take_hT(1)

            def split_low(u):
                dve.wait_ge(s_w_hi, u + 1)
                nc.vector.scalar_tensor_tensor(out=(wk, wq, wv)[u // KD][:, LO, u % KD, :], in0=stage_in[u % 2],
                                               scalar=W_SCALE, in1=(wk, wq, wv)[u // KD][:, HI, u % KD, :],
                                               op0=ALU.mult, op1=ALU.subtract).then_inc(s_wv_lo, 1)

            def tops(s):
                for t in range(T):
                    r = ROWS[t]
                    dve.wait_ge(s_logit, T * s + t + 1)
                    b0 = 3 * (t % 2) * BANK
                    link(nc.vector.reduce_max(top[0:r, t:t + 1], psum[0:r, b0:b0 + N], AX_X))
                    nc.vector.tensor_scalar(neg_top[0:r, t:t + 1], top[0:r, t:t + 1], -1.0, None,
                                            ALU.mult).then_inc(s_top, 1)

            def halve(count, first, mine, done):
                per = mine + (4 if first is None else 5) + (2 if mine < T else 0)
                with dve.Fori(0, count) as i:
                    base = i * per
                    n = 0
                    if first is None:
                        nc.vector.tensor_tensor(cand, low, ratios[:, bass.ds(i * T, T)], ALU.mult).then_inc(done, 1)
                        n += 1
                    else:
                        nc.vector.tensor_copy(step_now, steps[:, bass.ds(i + first, 1)]).then_inc(done, 1)
                        dve.wait_ge(done, base + 1)
                        nc.vector.scalar_tensor_tensor(out=cand, in0=low, scalar=step_now, in1=low,
                                                       op0=ALU.mult, op1=ALU.add).then_inc(done, 1)
                        n += 2
                    dve.wait_ge(done, base + n)
                    if mine < T:
                        dve.sem_inc(s_cand, 1)
                    for t in range(mine):
                        r = ROWS[t]
                        if t >= 2:
                            dve.wait_ge(done, base + (n + t - 1))
                        nc.vector.scalar_tensor_tensor(
                            out=(junk, junk_a)[t % 2][0:r, :], in0=rows_b[0:r, t, :], scalar=cand[0:r, t:t + 1],
                            in1=rows_b[0:r, t, :], op0=ALU.is_gt, op1=ALU.mult,
                            accum_out=mass[0:r, t:t + 1]).then_inc(done, 1)
                    n += mine
                    if mine < T:
                        hers = slice(mine, T)
                        dve.wait_ge(s_excess, i * (2 * (T - mine)) + 2 * (T - mine))
                        nc.vector.scalar_tensor_tensor(out=signs[:, hers], in0=signs[:, hers], scalar=float(N),
                                                       in1=cand[:, hers], op0=ALU.add, op1=ALU.mult).then_inc(done, 1)
                        dve.wait_ge(done, base + (n + 1))
                        nc.vector.scalar_tensor_tensor(out=mass[:, hers], in0=signs[:, hers], scalar=-0.5,
                                                       in1=excess[:, hers], op0=ALU.mult, op1=ALU.add).then_inc(done, 1)
                        n += 2
                    dve.wait_ge(done, base + n)
                    nc.vector.tensor_tensor(good, mass, target, ALU.is_ge).then_inc(done, 1)
                    dve.wait_ge(done, base + (n + 1))
                    nc.vector.tensor_tensor(good, good, cand, ALU.mult).then_inc(done, 1)
                    dve.wait_ge(done, base + (n + 2))
                    nc.vector.tensor_tensor(low, low, good, ALU.max).then_inc(done, 1)
                    dve.wait_ge(done, base + (n + 3))

            def threshold(upper, done):
                n = [0]

                def then(ins):
                    n[0] += 1
                    ins.then_inc(done, 1)
                    dve.wait_ge(done, n[0])

                upper(then)
                for t in range(T):
                    r = ROWS[t]
                    part = (junk, junk_a)[t % 2]
                    then(nc.vector.scalar_tensor_tensor(
                        out=part[0:r, :], in0=rows_b[0:r, t, :], scalar=cand[0:r, t:t + 1], in1=rows_b[0:r, t, :],
                        op0=ALU.is_le, op1=ALU.mult, accum_out=mass[0:r, t:t + 1]))
                    then(nc.vector.max(top8[0:r, t, :], part[0:r, :]))
                then(nc.vector.tensor_tensor(above, total, mass, ALU.subtract))
                then(nc.vector.tensor_tensor(sum8[:, :, 0], above, top8[:, :, 0], ALU.add))
                for j in range(1, 8):
                    then(nc.vector.tensor_tensor(sum8[:, :, j], sum8[:, :, j - 1], top8[:, :, j], ALU.add))
                wide = [P, T, 8]
                then(nc.vector.tensor_tensor(sum8, sum8, goal.unsqueeze(2).broadcast_to(wide), ALU.is_ge))
                then(nc.vector.tensor_tensor(sum8, sum8, top8, ALU.mult))
                then(nc.vector.reduce_max(cut, sum8, AX_X))
                then(nc.vector.tensor_tensor(cut, cut, top8[:, :, 7], ALU.max))
                then(nc.vector.tensor_tensor(sum8, top8, cut.unsqueeze(2).broadcast_to(wide), ALU.is_gt))
                then(nc.vector.tensor_tensor(sum8, sum8, top8, ALU.mult))
                then(nc.vector.reduce_sum(good, sum8, AX_X))
                then(nc.vector.tensor_tensor(quota, goal, above, ALU.subtract))
                then(nc.vector.tensor_tensor(quota, quota, good, ALU.subtract))
                then(nc.vector.tensor_tensor(quota, quota, cut, ALU.add))

            def search(s):
                dve.wait_ge(s_exp, T * (s + 1))
                link(nc.vector.tensor_scalar(goal, total, P_NUC, None, ALU.mult))
                link(nc.vector.tensor_scalar(low, total, FLOOR, None, ALU.mult))
                nc.vector.reciprocal(span0, low).then_inc(s_span, 1)
                link(nc.vector.tensor_copy(target, goal))
                if MINE[s] < T:
                    hers = slice(MINE[s], T)
                    link(nc.vector.tensor_tensor(target[:, hers], goal[:, hers], total[:, hers], ALU.subtract))
                dve.wait_ge(s_ratio, sum(FAST[:s + 1]))
                halve(FAST[s], None, MINE[s], s_halve[s])
                threshold(lambda then: then(nc.vector.scalar_tensor_tensor(
                    out=cand, in0=low, scalar=1 + 2e-5, in1=ratios[:, (FAST[s] - 1) * T:FAST[s] * T],
                    op0=ALU.mult, op1=ALU.mult)), s_cut[s])
                for t in range(T):
                    r = ROWS[t]
                    last = nc.vector.scalar_tensor_tensor(
                        out=(junk, junk_a)[t % 2][0:r, :], in0=rows_b[0:r, t, :], scalar=cut[0:r, t:t + 1],
                        in1=rows_b[0:r, t, :], op0=ALU.is_ge, op1=ALU.mult, accum_out=down_to[0:r, t:t + 1])
                    link(last)
                link(nc.vector.tensor_scalar(good, goal, 1 - 1e-6, None, ALU.mult))
                link(nc.vector.tensor_tensor(good, down_to, good, ALU.is_lt))
                link(nc.vector.reduce_max(flags[:, 0:1], good, AX_X))
                link(nc.vector.tensor_tensor(good, goal, cut, ALU.add))
                link(nc.vector.tensor_tensor(good, down_to, good, ALU.is_ge))
                nc.vector.reduce_max(flags[:, 1:2], good, AX_X).then_inc(s_flags, 1)
                dve.wait_ge(s_flags_all, s + 1)
                link(nc.vector.tensor_copy(flags_int, flags_all))
                lower = dve.value_load(flags_int[0:1, 0:1], min_val=0, max_val=1)
                tied = dve.value_load(flags_int[0:1, 1:2], min_val=0, max_val=1)
                with dve.If(lower > 0):
                    nc.vector.tensor_copy(target, goal).then_inc(s_target[s], 1)
                    dve.wait_ge(s_target[s], 1)
                    halve(SEARCH - FAST[s], FAST[s], T, s_halve_on[s])
                    threshold(lambda then: then(nc.vector.tensor_scalar(
                        cand, low, float(np.exp(SPAN / 2.0 ** SEARCH) * (1 + 2e-6)), None, ALU.mult)), s_cut_on[s])
                return lower + tied

            tie_steps = [0]

            def drop_ties(s, t):
                r = ROWS[t]
                row = rows_b[0:r, t, :]

                def then(ins):
                    tie_steps[0] += 1
                    ins.then_inc(s_tied[s], 1)
                    dve.wait_ge(s_tied[s], tie_steps[0])

                then(nc.vector.tensor_scalar(equal[0:r, :], row, cut[0:r, t:t + 1], cut[0:r, t:t + 1],
                                             ALU.is_equal, ALU.mult))
                then(nc.vector.tensor_tensor_scan(equal_sums[0:r, :], ones_row[0:r, :].broadcast_to([r, N]),
                                                  equal[0:r, :], 0.0, ALU.mult, ALU.add))
                then(nc.vector.scalar_tensor_tensor(
                    out=equal[0:r, :], in0=equal_sums[0:r, :], scalar=quota[0:r, t:t + 1], in1=equal[0:r, :],
                    op0=ALU.is_ge, op1=ALU.mult))
                then(nc.vector.tensor_tensor(row, row, equal[0:r, :], ALU.subtract))

            def attention(s, ties):
                tie_steps[0] = 0

                def keep(t):
                    r = ROWS[t]
                    with dve.If(ties > 0):
                        drop_ties(s, t)
                    nc.vector.scalar_tensor_tensor(
                        out=rows_b[0:r, t, :], in0=rows_b[0:r, t, :], scalar=cut[0:r, t:t + 1], in1=rows_b[0:r, t, :],
                        op0=ALU.is_ge, op1=ALU.mult, accum_out=kept[0:r, t:t + 1]).then_inc(s_a_rows, 1)
                    dve.wait_ge(s_a_rows, T * s + t + 1)
                    nc.vector.reciprocal(kept_inv[0:r, t:t + 1], kept[0:r, t:t + 1]).then_inc(s_kept_inv, 1)

                def finish(b, stage):
                    quad = QUADS[b]
                    tiles = QUAD_TILES[b]
                    if stage == NORM_Y:
                        norm_var(s_y_add, 5 * T + quad[-1] + 1, tiles)
                        return
                    if stage == NORM_H:
                        norm_coef(X_NORM[b], tiles)
                        return
                    norm_coef(Y_NORM[b], tiles)
                    dve.wait_ge(s_ln_coef, Y_NORM[b] + 1)
                    for t in quad:
                        last = nc.vector.tensor_scalar(x[:, t, :], x[:, t, :], rstd[:, t:t + 1], nmean[:, t:t + 1],
                                                       ALU.mult, ALU.add)
                    link(last)
                    dve.wait_ge(s_gb_in, 32)
                    for t in quad:
                        r = ROWS[t]
                        last = nc.vector.tensor_tensor(x[0:r, t, :], x[0:r, t, :], gamma_b[0:r, :], ALU.mult)
                    link(last)
                    dve.wait_ge(s_beta, T)
                    for t in quad:
                        r = ROWS[t]
                        nc.vector.tensor_tensor(x[0:r, t, :], x[0:r, t, :], h[0:r, t, :], ALU.add).then_inc(s_x_final, 1)
                    norm_var(s_x_final, quad[-1] + 1, tiles)

                def between(t):
                    for b, stage in NORM_AT.get(t, ()) if s else ():
                        if (b, stage) == (2, NORM_Y):
                            split_low(SPLIT_AFTER[T - 1])
                        finish(b, stage)

                keep(0)
                for t in range(T):
                    if t + 1 < T:
                        keep(t + 1)
                    r = ROWS[t]
                    i = T * s + t
                    b0 = 3 * (t % 2)
                    if s == 0:
                        dve.wait_ge(s_a_tr, 3 * i + 2)
                        nc.vector.tensor_copy(pT[:, t % 2, 4:8, 0:r],
                                              bank(b0 + 1).rearrange("p (k n) -> p k n", n=P)[:, :, 0:r]
                                              ).then_inc(s_pt_dve, 1)
                    between(t)
                between(T)

            tops(0)
            attention(0, search(0))
            take_hT(2)
            tops(1)
            attention(1, search(1))
            nc.vector.tensor_copy(ident16, ident[:, :]).then_inc(s_ident16, 1)

            for b, (c0, cw) in enumerate(CHUNKS):
                for kd in range(KD):
                    dve.wait_ge(s_hT_act, 9 + 2 * b + kd + 1)
                    nc.vector.tensor_tensor(hT2[:, LO, kd, c0:c0 + cw], bank(2 * b + kd, cw),
                                            hT2[:, HI, kd, c0:c0 + cw], ALU.subtract).then_inc(s_hT_dve, 1)
            split_low(5)
            def head(a, b):
                dve.wait_ge(s_wout_hi, a + 1)
                nc.vector.scalar_tensor_tensor(out=wout[:, LO, :, :], in0=wout_in, scalar=W_SCALE,
                                               in1=wout[:, HI, :, :], op0=ALU.mult,
                                               op1=ALU.subtract).then_inc(s_wout_lo, 1)
                for which, dst in enumerate((kT, qT, vT)):
                    for half in range(KD):
                        for g, group in enumerate(CGROUPS):
                            dve.wait_ge(s_hproj_act, a * 18 + (6 * which + 3 * half + g + 1))
                            nc.vector.scalar_tensor_tensor(
                                out=head_cols(dst, LO, half, b, group), in0=head_bank(half, g, group),
                                scalar=UNSCALE[which], in1=head_cols(dst, HI, half, b, group),
                                op0=ALU.mult, op1=ALU.subtract).then_inc(s_hproj_dve, 1)

                def take_vw(tiles):
                    for i in tiles:
                        dve.wait_ge(s_vw_act, a * T + (i + 1))
                        nc.vector.scalar_tensor_tensor(
                            out=vw[0:ROWS[i], LO, i, :], in0=bank(3 + i % 5, D, ROWS[i]), scalar=1 / W_SCALE,
                            in1=vw[0:ROWS[i], HI, i, :], op0=ALU.mult, op1=ALU.subtract).then_inc(s_vw_dve, 1)

                for t in range(T + 2):
                    if t < T:
                        r = ROWS[t]
                        own_wait(dve, s_qk, a * T + (t + 1), s_dve_passed)
                        nc.vector.tensor_tensor_reduce(out=att[0:r, t % 2, :], in0=psum[0:r, 0:N], in1=bias[0:r, t, :],
                                                       scale=1.0, scalar=-3.0e38, op0=ALU.add, op1=ALU.max,
                                                       accum_out=top[0:r, t:t + 1]).then_inc(s_biased, 1)
                        dve.wait_ge(s_biased, a * T + (t + 1))
                        nc.vector.tensor_scalar(neg_top[0:r, t:t + 1], top[0:r, t:t + 1], -1.0, LOG_P_SCALE,
                                                ALU.mult, ALU.add).then_inc(s_neg, 1)
                    if t == 0:
                        take_vw(range(0, T // 3))
                    if t >= 2:
                        i = t - 2
                        ri = ROWS[i]
                        dve.wait_ge(s_pv, a * T + (i + 1))
                        dve.wait_ge(s_hinv, a * T + (i + 1))
                        dve.wait_ge(s_x_add, a * T + (i + 1))
                        nc.vector.scalar_tensor_tensor(out=x[0:ri, i, :], in0=bank(6 + i % 2, D, ri),
                                                       scalar=kept_inv[0:ri, i:i + 1], in1=x[0:ri, i, :],
                                                       op0=ALU.mult, op1=ALU.add).then_inc(s_x_add, 1)
                    if t < T:
                        dve.wait_ge(s_hexp, a * T + (t + 1))
                        nc.vector.scalar_tensor_tensor(out=att[0:r, t % 2, :], in0=bias[0:r, t, :], scalar=MASKED / 2,
                                                       in1=att[0:r, t % 2, :], op0=ALU.is_gt,
                                                       op1=ALU.mult).then_inc(s_masked, 1)
                        nc.vector.reciprocal(kept_inv[0:r, t:t + 1], total[0:r, t:t + 1]).then_inc(s_hinv, 1)
                    if t == 0:
                        take_vw(range(T // 3, T))
                    if 1 <= t <= T:
                        i = t - 1
                        ri = ROWS[i]
                        dve.wait_ge(s_htr, a * (3 * T) + (3 * i + 2))
                        nc.vector.tensor_copy(pT2[i % 2][:, LO, 0:PT8, 0:ri],
                                              pt_bank(5)[:, :, 0:ri]).then_inc(s_hpt_dve, 1)

            dve.sem_inc(s_x_add, 1)
            dve.sem_inc(s_wout_lo, 1)
            with dve.Fori(0, 2) as g:
                with dve.Fori(0, 4) as b:
                    head(g * 4 + b, b)

            norm_var(s_x_add, 1 + HEADS * T)
            norm_coef(LAST_NORM)
            take_hT(4)
            dve.wait_ge(s_l3_in, L3_LOADS)
            for kd in range(KD):
                for a_row, dst in ((a_left, w_left[:, kd:kd + 1]), (a_right, w_s[:, kd, D:D + 1])):
                    link(nc.vector.scalar_tensor_tensor(out=dot_junk, in0=w_s[:, kd, 0:D], scalar=1.0, in1=a_row,
                                                        op0=ALU.mult, op1=ALU.mult, accum_out=dst))
            for kd in range(KD):
                last = nc.vector.tensor_scalar(w_rep[:, kd, :], ident[:, :], 0.0, w_left[:, kd:kd + 1],
                                               ALU.mult, ALU.add)
            last.then_inc(s_l3w, 1)
            nc.vector.memset(gate_a, 0.0)
            nc.vector.memset(gate_b, 0.0)
            dve.wait_ge(s_tr, 30)
            link(nc.vector.memset(hs[:, :, D], 1.0))
            for t in range(T):
                dve.wait_ge(s_l3proj, t + 1)
                r = ROWS[t]
                b0 = (4, 6)[t % 2]
                nc.vector.tensor_copy(right[0:r, t:t + 1], psum[0:r, b0 * BANK + D:b0 * BANK + D + 1])
                nc.vector.tensor_copy(hs[0:r, t, 0:D], bank(b0, D, r)).then_inc(s_l3proj_taken, 1)
                nc.vector.scalar_tensor_tensor(out=bias[0:r, t, :], in0=bias[0:r, t, :], scalar=MASKED / 2,
                                               in1=bias[0:r, t, :], op0=ALU.is_gt, op1=ALU.mult).then_inc(s_unbias, 1)
            u = 0
            for b, (c0, cw) in enumerate(CHUNKS):
                for k in range(T):
                    if u % 2:
                        dve.wait_ge(s_adj_tr, 33 + u + 1)
                        nc.vector.tensor_copy(adjT3[0:ROWS[k], k, c0:c0 + cw],
                                              bank(u % 6, cw, ROWS[k])).then_inc(s_adjT_dve, 1)
                    u += 1
            dve.wait_ge(s_left_taken, 3)
            dve.wait_ge(s_l3proj_taken, T)

            def mask_edge(k):
                r = ROWS[k]
                dve.wait_ge(s_e, k + 1)
                nc.vector.scalar_tensor_tensor(out=edge[0:r, k, :], in0=adjT3[0:r, k, :], scalar=0.0,
                                               in1=edge[0:r, k, :], op0=ALU.not_equal, op1=ALU.mult).then_inc(s_edge, 1)

            for k in range(T):
                r = ROWS[k]
                if k >= 2:
                    dve.wait_ge(s_e, k - 1)
                link(nc.vector.tensor_scalar(z[0:r, k % 2, :], left[0:r, :], right[0:r, k:k + 1], 0.01,
                                             ALU.add, ALU.mult))
                nc.vector.scalar_tensor_tensor(out=z[0:r, k % 2, :], in0=left[0:r, :], scalar=right[0:r, k:k + 1],
                                               in1=z[0:r, k % 2, :], op0=ALU.add, op1=ALU.max).then_inc(s_z, 1)
                if k:
                    mask_edge(k - 1)
                dve.wait_ge(s_conv, k + 1)
                b0 = (k % 2) * BANK
                nc.vector.scalar_tensor_tensor(out=conv[0:r, k, :], in0=bank(k % 2, D, r), scalar=0.5,
                                               in1=bg_b[0:r, :], op0=ALU.mult, op1=ALU.add)
                for j, gate in enumerate((gate_a, gate_b)):
                    last = nc.vector.scalar_tensor_tensor(
                        out=gate[0:r, k:k + 1], in0=psum[0:r, b0 + D + j:b0 + D + j + 1], scalar=0.5,
                        in1=hg[0:r, k, D + 2 + j:D + 3 + j], op0=ALU.mult, op1=ALU.add)
                last.then_inc(s_conv_taken, 1)
            mask_edge(T - 1)
            dve.wait_ge(s_gate, 1)
            for t in range(T):
                r = ROWS[t]
                last = nc.vector.tensor_scalar(conv[0:r, t, :], conv[0:r, t, :], gate_b[0:r, t:t + 1], None, ALU.mult)
            link(last)
            for t in range(T):
                r = ROWS[t]
                dve.wait_ge(s_gat, t + 1)
                s1 = (2 + t % 2) * BANK + D
                link(nc.vector.tensor_scalar(den[0:r, t:t + 1], psum[0:r, s1:s1 + 1], 1e-5, None, ALU.add))
                link(nc.vector.reciprocal(den[0:r, t:t + 1], den[0:r, t:t + 1]))
                link(nc.vector.tensor_tensor(den[0:r, t:t + 1], den[0:r, t:t + 1], gate_a[0:r, t:t + 1], ALU.mult))
                nc.vector.scalar_tensor_tensor(out=conv[0:r, t, :], in0=bank(2 + t % 2, D, r),
                                               scalar=den[0:r, t:t + 1], in1=conv[0:r, t, :],
                                               op0=ALU.mult, op1=ALU.add).then_inc(s_mixed, 1)


_INS = ['x', 'adj', 'L0_gnn_t', 'L0_gnn_weight', 'L1_gnn_W1', 'L1_gnn_W2', 'L1_gnn_W3', 'L1_gnn_U1', 'L1_gnn_U2',
        'L1_gnn_U3', 'L1_gnn_gamma', 'L1_gnn_beta', 'L2_gnn_Wq', 'L2_gnn_Wk', 'L2_gnn_Wv', 'L2_gnn_Wout',
        'L3_gnn_W_sa', 'L3_gnn_a_sa', 'L3_gnn_W_gcnb', 'L3_gnn_b_gcnb', 'L3_gnn_Wa', 'L3_gnn_ba', 'L3_gnn_Wb',
        'L3_gnn_bb']


def kernel(**inputs):
    import numpy as _np
    import concourse.bacc as _bacc
    from concourse import mybir as _mybir
    from concourse.bass_utils import run_bass_kernel_spmd as _run

    nc = _bacc.Bacc("TRN2", target_bir_lowering=False, num_devices=1)
    arrays, args = {}, []
    for name in _INS:
        a = _np.ascontiguousarray(inputs[name])
        arrays[f"in_{name}"] = a
        args.append(nc.dram_tensor(f"in_{name}", a.shape, _mybir.dt.from_np(a.dtype), kind="ExternalInput").ap())
    args.append(nc.dram_tensor("out_x", (N, D), _mybir.dt.float32, kind="ExternalOutput").ap())
    graph_layers(nc, *args)
    r = _run(nc, [arrays], core_ids=[0])
    return r.results[0]["out_x"]
```
